# Optimizing a Trainium2 kernel written in Bass

```python
import numpy as np
import jax
import jax.numpy as jnp

def _softmax(x, axis=-1):
    return jax.nn.softmax(x, axis=axis)

def _gelu(x):
    return jax.nn.gelu(x, approximate=True)

def _silu(x):
    return jax.nn.silu(x)

def _sigmoid(x):
    return jax.nn.sigmoid(x)

def _layernorm(x, axis=-1, eps=1e-05):
    m = jnp.mean(x, axis=axis, keepdims=True)
    v = jnp.var(x, axis=axis, keepdims=True)
    return (x - m) / jnp.sqrt(v + eps)

def _scatter_add(tgt, idx, src, axis=0):
    return tgt.at[idx].add(src)

def _segment_sum(src, seg, n):
    return jax.ops.segment_sum(src, seg, n)
kernel_name = 'mk_gps_d1_gnn_r16_cd2c35'

def setup_inputs(seed: int=0):
    np.random.seed(seed)
    _w = jnp.asarray

    def _rec_inputs():
        import jax
        import jax.numpy as jnp
        _gk = jax.random.key(seed)
        x = -0.0002117 + 1 * jax.random.normal(jax.random.fold_in(_gk, 1), (625, 1024), jnp.float32)
        src = jax.random.randint(jax.random.fold_in(_gk, 2), (20000,), 0, 625, jnp.int32)
        dst = jnp.minimum((625 * jax.random.uniform(jax.random.fold_in(_gk, 3), (20000,)) ** 2.0).astype(jnp.int32), 9999)
        _o = jnp.argsort(dst, stable=True)
        src = src[_o]
        dst = dst[_o]
        return (x, src, dst)
    x, src, dst = _rec_inputs()

    def _L0_gnn_setup():
        import jax, jax.numpy as jnp
        import numpy as np
        N_NODES = 25000
        N_EDGES = 25000
        D = 1024

        def _sage_layer(h, edge_src, edge_dst, deg_inv, W_self, W_neigh, b):
            msg = h[edge_src]
            agg = jax.ops.segment_sum(msg, edge_dst, num_segments=h.shape[0])
            mean = agg * deg_inv[:, None]
            return h @ W_self + mean @ W_neigh + b
        key = jax.random.key(seed)
        ks = jax.random.split(key, 8)
        s = 1.0 / np.sqrt(D)
        return {'x': jax.random.normal(ks[0], (N_NODES, D), dtype=jnp.float32), 'edge_src': jax.random.randint(ks[1], (N_EDGES,), 0, N_NODES, dtype=jnp.int32), 'edge_dst': jax.random.randint(ks[2], (N_EDGES,), 0, N_NODES, dtype=jnp.int32), 'W_self0': jax.random.normal(ks[3], (D, D), dtype=jnp.float32) * s, 'W_neigh0': jax.random.normal(ks[4], (D, D), dtype=jnp.float32) * s, 'b0': jnp.zeros((D,), dtype=jnp.float32), 'W_self1': jax.random.normal(ks[5], (D, D), dtype=jnp.float32) * s, 'W_neigh1': jax.random.normal(ks[6], (D, D), dtype=jnp.float32) * s, 'b1': jnp.zeros((D,), dtype=jnp.float32)}
    _L0_gnn_all = _L0_gnn_setup()
    _L0_gnn_in = {k: v for k, v in _L0_gnn_all.items() if k in ('W_self0', 'W_neigh0', 'b0', 'W_self1', 'W_neigh1', 'b1')}
    del _L0_gnn_all

    def _L0_mix_setup():
        import jax, jax.numpy as jnp
        import numpy as np
        B, T, DIM, H, DH = (4, 256, 1024, 16, 64)
        key = jax.random.key(seed)
        ks = jax.random.split(key, 6)
        s = lambda fan_in: 1.0 / np.sqrt(fan_in)
        x = jax.random.normal(ks[0], (B, T, DIM), dtype=jnp.float32)
        Wq = jax.random.uniform(ks[1], (DIM, H * DH), jnp.float32, -s(DIM), s(DIM))
        Wk = jax.random.uniform(ks[2], (DIM, H * DH), jnp.float32, -s(DIM), s(DIM))
        Wv = jax.random.uniform(ks[3], (DIM, H * DH), jnp.float32, -s(DIM), s(DIM))
        Wo = jax.random.uniform(ks[4], (H * DH, DIM), jnp.float32, -s(H * DH), s(H * DH))
        bo = jax.random.uniform(ks[5], (DIM,), jnp.float32, -s(H * DH), s(H * DH))
        return {'x': x, 'Wq': Wq, 'Wk': Wk, 'Wv': Wv, 'Wo': Wo, 'bo': bo}
    _L0_mix_all = _L0_mix_setup()
    _L0_mix_in = {k: v for k, v in _L0_mix_all.items() if k in ('Wq', 'Wk', 'Wv', 'Wo', 'bo')}
    del _L0_mix_all

    def _L0_ffn_setup():
        import jax, jax.numpy as jnp
        import numpy as np
        D = 1024
        F = 1024
        E = 8
        K = 2
        B, T = (2, 128)

        def _moe_forward(x, router_w, w1, w2, shared_gate_up, shared_down, shared_gate_w):
            b, t, d = x.shape
            xf = x.reshape(-1, d)
            n = xf.shape[0]
            logits = xf @ router_w
            probs = jax.nn.softmax(logits, axis=-1)
            topw, topi = jax.lax.top_k(probs, K)
            combine = jnp.zeros((n, E), dtype=probs.dtype).at[jnp.arange(n)[:, None], topi].add(topw)
            h = jax.nn.silu(jnp.einsum('nd,edf->nef', xf, w1))
            ye = jnp.einsum('nef,efd->ned', h, w2)
            routed = jnp.einsum('ne,ned->nd', combine, ye)
            gu = xf @ shared_gate_up
            gate, up = (gu[:, :F], gu[:, F:])
            shared = jax.nn.silu(gate) * up @ shared_down
            shared = jax.nn.sigmoid(xf @ shared_gate_w) * shared
            return (routed + shared).reshape(b, t, d)
        key = jax.random.key(seed)
        ks = jax.random.split(key, 7)
        std = 0.02
        x = jax.random.normal(ks[0], (B, T, D), dtype=jnp.float32)
        router_w = jax.random.normal(ks[1], (D, E), dtype=jnp.float32) * std
        w1 = jax.random.normal(ks[2], (E, D, F), dtype=jnp.float32) * std
        w2 = jax.random.normal(ks[3], (E, F, D), dtype=jnp.float32) * std
        shared_gate_up = jax.random.normal(ks[4], (D, 2 * F), dtype=jnp.float32) * std
        shared_down = jax.random.normal(ks[5], (F, D), dtype=jnp.float32) * std
        shared_gate_w = jax.random.normal(ks[6], (D, 1), dtype=jnp.float32) * std
        return {'x': x, 'router_w': router_w, 'w1': w1, 'w2': w2, 'shared_gate_up': shared_gate_up, 'shared_down': shared_down, 'shared_gate_w': shared_gate_w}
    _L0_ffn_all = _L0_ffn_setup()
    _L0_ffn_in = {k: v for k, v in _L0_ffn_all.items() if k in ('router_w', 'w1', 'w2', 'shared_gate_up', 'shared_down', 'shared_gate_w')}
    del _L0_ffn_all
    return {'x': x, 'src': src, 'dst': dst, 'L0_gnn_W_self0': _L0_gnn_in['W_self0'], 'L0_gnn_W_neigh0': _L0_gnn_in['W_neigh0'], 'L0_gnn_b0': _L0_gnn_in['b0'], 'L0_gnn_W_self1': _L0_gnn_in['W_self1'], 'L0_gnn_W_neigh1': _L0_gnn_in['W_neigh1'], 'L0_gnn_b1': _L0_gnn_in['b1'], 'L0_mix_Wq': _L0_mix_in['Wq'], 'L0_mix_Wk': _L0_mix_in['Wk'], 'L0_mix_Wv': _L0_mix_in['Wv'], 'L0_mix_Wo': _L0_mix_in['Wo'], 'L0_mix_bo': _L0_mix_in['bo'], 'L0_ffn_router_w': _L0_ffn_in['router_w'], 'L0_ffn_w1': _L0_ffn_in['w1'], 'L0_ffn_w2': _L0_ffn_in['w2'], 'L0_ffn_shared_gate_up': _L0_ffn_in['shared_gate_up'], 'L0_ffn_shared_down': _L0_ffn_in['shared_down'], 'L0_ffn_shared_gate_w': _L0_ffn_in['shared_gate_w']}

def reference(x, src, dst, L0_gnn_W_self0, L0_gnn_W_neigh0, L0_gnn_b0, L0_gnn_W_self1, L0_gnn_W_neigh1, L0_gnn_b1, L0_mix_Wq, L0_mix_Wk, L0_mix_Wv, L0_mix_Wo, L0_mix_bo, L0_ffn_router_w, L0_ffn_w1, L0_ffn_w2, L0_ffn_shared_gate_up, L0_ffn_shared_down, L0_ffn_shared_gate_w):
    import jax
    import jax.numpy as jnp

    def _L0_gnn_ref(x, edge_src, edge_dst, W_self0, W_neigh0, b0, W_self1, W_neigh1, b1):
        import jax, jax.numpy as jnp
        import numpy as np
        N_NODES = 25000
        N_EDGES = 25000
        D = 1024

        def _sage_layer(h, edge_src, edge_dst, deg_inv, W_self, W_neigh, b):
            msg = h[edge_src]
            agg = jax.ops.segment_sum(msg, edge_dst, num_segments=h.shape[0])
            mean = agg * deg_inv[:, None]
            return h @ W_self + mean @ W_neigh + b
        N = x.shape[0]
        deg = jax.ops.segment_sum(jnp.ones_like(edge_dst, dtype=x.dtype), edge_dst, num_segments=N)
        deg_inv = 1.0 / jnp.maximum(deg, 1.0)
        h = jax.nn.relu(_sage_layer(x, edge_src, edge_dst, deg_inv, W_self0, W_neigh0, b0))
        out = _sage_layer(h, edge_src, edge_dst, deg_inv, W_self1, W_neigh1, b1)
        return out

    def _L0_mix_ref(x, Wq, Wk, Wv, Wo, bo):
        import jax, jax.numpy as jnp
        import numpy as np
        B, T, DIM, H, DH = (4, 256, 1024, 16, 64)
        b, t, _ = x.shape
        to_heads = lambda y: y.reshape(b, t, H, DH).transpose(0, 2, 1, 3)
        q = to_heads(x @ Wq)
        k = to_heads(x @ Wk)
        v = to_heads(x @ Wv)
        q = jax.nn.softmax(q, axis=-1) * DH ** (-0.5)
        k = jax.nn.softmax(k, axis=-2)
        context = jnp.einsum('bhnd,bhne->bhde', k, v)
        attn = jnp.einsum('bhnd,bhde->bhne', q, context)
        attn = attn.transpose(0, 2, 1, 3).reshape(b, t, H * DH)
        return attn @ Wo + bo

    def _L0_ffn_ref(x, router_w, w1, w2, shared_gate_up, shared_down, shared_gate_w):
        import jax, jax.numpy as jnp
        import numpy as np
        D = 1024
        F = 1024
        E = 8
        K = 2
        B, T = (2, 128)

        def _moe_forward(x, router_w, w1, w2, shared_gate_up, shared_down, shared_gate_w):
            b, t, d = x.shape
            xf = x.reshape(-1, d)
            n = xf.shape[0]
            logits = xf @ router_w
            probs = jax.nn.softmax(logits, axis=-1)
            topw, topi = jax.lax.top_k(probs, K)
            combine = jnp.zeros((n, E), dtype=probs.dtype).at[jnp.arange(n)[:, None], topi].add(topw)
            h = jax.nn.silu(jnp.einsum('nd,edf->nef', xf, w1))
            ye = jnp.einsum('nef,efd->ned', h, w2)
            routed = jnp.einsum('ne,ned->nd', combine, ye)
            gu = xf @ shared_gate_up
            gate, up = (gu[:, :F], gu[:, F:])
            shared = jax.nn.silu(gate) * up @ shared_down
            shared = jax.nn.sigmoid(xf @ shared_gate_w) * shared
            return (routed + shared).reshape(b, t, d)
        return _moe_forward(x, router_w, w1, w2, shared_gate_up, shared_down, shared_gate_w)
    xn = _layernorm(x, axis=-1)
    x = x + _L0_gnn_ref(xn, src, dst, L0_gnn_W_self0, L0_gnn_W_neigh0, L0_gnn_b0, L0_gnn_W_self1, L0_gnn_W_neigh1, L0_gnn_b1) + _L0_mix_ref(xn[None], L0_mix_Wq, L0_mix_Wk, L0_mix_Wv, L0_mix_Wo, L0_mix_bo)[0]
    x = x + _L0_ffn_ref(_layernorm(x, axis=-1)[None], L0_ffn_router_w, L0_ffn_w1, L0_ffn_w2, L0_ffn_shared_gate_up, L0_ffn_shared_down, L0_ffn_shared_gate_w)[0]
    return x

_drawn_inputs = setup_inputs


def setup_inputs(seed=0):
    import zlib

    import numpy as np

    out = dict(_drawn_inputs(seed))
    spreads = {'L0_gnn_b0': (0.0, 0.1), 'L0_gnn_b1': (0.0, 0.1)}
    factors = {'L0_mix_Wq': 8.0,
     'L0_mix_Wk': 8.0,
     'L0_mix_Wv': 8.0,
     'L0_mix_Wo': 8.0,
     'L0_mix_bo': 3.876,
     'L0_ffn_shared_gate_w': 3.059}
    for name, (base, spread) in spreads.items():
        noise = np.random.default_rng([zlib.crc32(name.encode()), seed]).standard_normal(out[name].shape)
        drawn = base * np.exp(spread * noise) if base else spread * noise
        out[name] = jnp.asarray(drawn.astype(out[name].dtype))
    for name, factor in factors.items():
        out[name] = (out[name] * factor).astype(out[name].dtype)
    return out
```

```python
import concourse.bass as bass
from concourse import mybir
from contextlib import ExitStack


def gps_layer(nc, x, src, dst, w_self0, w_neigh0, b0, w_self1, w_neigh1, b1,
              wq, wk, wv, wo, bo, router_w, w1, w2, gate_up, down, gate_w, out):
    f32, f32r, f16 = mybir.dt.float32, mybir.dt.float32r, mybir.dt.float16
    i32, u32 = mybir.dt.int32, mybir.dt.uint32
    ALU, ACT, AX = mybir.AluOpType, mybir.ActivationFunctionType, mybir.AxisListType

    N, D = x.shape
    E = src.shape[0]
    T = 125
    NT = N // T
    KF = D // 128
    HW = D // 2
    HK = KF // 2
    TP = 628
    TH = TP // 2
    LASTH = N - TH
    DH = 64
    HH = HW // DH
    X = router_w.shape[1]
    XP = X + 2
    B = 256
    BC = B // 128
    MAXB = X + (2 * N - X) // B + 1
    SLOTC = MAXB * BC
    CP = 125
    NC = E // CP
    NG = 5
    CG = NC // NG
    OHB = 4
    DIGIT = 4096.0
    EPS = 1e-5
    assert CG * CP < DIGIT and CG % OHB == 0 and NT * T == N and NC * CP == E

    halves = lambda m: [m[:, h * HW:(h + 1) * HW].rearrange("(k p) n -> p k n", p=128) for h in range(2)]
    gate, up = gate_up[:, 0:D], gate_up[:, D:2 * D]
    V, K, Q, O = halves(wv), halves(wk), halves(wq), halves(wo)
    N0, S0, N1, S1 = halves(w_neigh0), halves(w_self0), halves(w_neigh1), halves(w_self1)
    G, U, Dn = halves(gate), halves(up), halves(down)
    STREAM = [V[0], V[1], K[0], K[1], Q[0], Q[1], O[0], O[1], N0[0], S0[0], N0[1], S0[1],
              N1[0], S1[0], N1[1], S1[1], G[0], U[0], G[1], U[1], Dn[0], Dn[1]]
    (J_V, J_K, J_Q, J_O, J_L0, J_L1, J_GU, J_D, J_X) = (0, 2, 4, 6, 8, 12, 16, 20, 22)
    w1v = w1.rearrange("e (k p) n -> p e k n", p=128)
    w2v = w2.rearrange("e (k p) n -> p e k n", p=128)

    RING = 4
    units = [("deg",)] + [("xt", i, f) for i in range(NT) for f in range(2)]
    units += [("v", h, i) for h in range(2) for i in range(NT)]
    for m in range(KF):
        units += [("k", m)] + ([("kt", m - 1)] if m else [])
    units += [("kt", KF - 1), ("ctx", 0), ("ctx", 1)]
    QLAG = 2
    for m in range(2 * NT + QLAG):
        if m - QLAG == NT:
            units += [("at", n) for n in range(HK)]
        if m < 2 * NT:
            units += [("q", m)]
        if m >= QLAG:
            units += [("qt", m - QLAG)]
    units += [("at", n) for n in range(HK, KF)]
    units += [("o", h, i) for h in range(2) for i in range(NT)]
    for h in range(2):
        units += [("g0", h, i) for i in range(NT)] + [("h", h * HK + n) for n in range(HK)]
    for h in range(2):
        units += [("g1", h, i) for i in range(NT)] + [("x1", h, i) for i in range(NT)]
    units += [("x2t", i, f) for i in range(NT) for f in range(2)] + [("lg",), ("lt",)]
    for h in range(2):
        units += [("gt", h * HK + n) for n in range(HK)] + ([("pos",)] if h == 0 else [])
        units += [("up", h * HK + n) for n in range(HK)]
    units += [("xe", s, f) for s in range(BC) for f in range(2)]
    units += [("sd", h, i) for h in range(2) for i in range(NT)]
    U0 = len(units)
    place = {key: n for n, key in enumerate(units)}
    block_units = ([("he", n) for n in range(KF // 2)] + [("xe+", s, f) for s in range(BC) for f in range(2)]
                   + [("y", h, s) for h in range(2) for s in range(BC)])
    BU = len(block_units) // RING
    assert BU * RING == len(block_units)
    place.update({key: U0 + n for n, key in enumerate(block_units)})
    slot = lambda key: place[key] % RING
    use = lambda key: place[key] // RING

    attn_d = nc.dram_tensor("attn_out", (N, D), f32, kind="Internal").ap()
    xn2_d = nc.dram_tensor("xn2_rows", (N, D), f32, kind="Internal").ap()
    slot_d = nc.dram_tensor("token_of_slot", (SLOTC * 128, 1), u32, kind="Internal").ap()
    y_d = nc.dram_tensor("expert_rows", (SLOTC * 128, D), f32, kind="Internal").ap()
    y_c = y_d.rearrange("(c p) f -> p c f", p=128)
    y_block = lambda c, f0, f1: y_c[:, bass.ds(c, 1), f0:f1].rearrange("p c f -> p (c f)")
    tok = lambda a: a.rearrange("(i p) f -> p i f", p=T)

    ctx = ExitStack()
    with ctx:
        sem = lambda name: ctx.enter_context(nc.semaphore(name))
        BASE = (nc.sbuf_base + 31) // 32 * 32

        def at(name, offset, shape, dt):
            return nc.alloc_sbuf_tensor_at(name, shape, dt, offset=BASE + offset)

        HALF = KF * HW * 4
        o_w = 0
        o_raw = o_w + 4 * HALF
        R1 = o_raw + HALF
        R1S = 2 * NT * D * 4
        R2 = R1 + R1S
        PAIR = 2 * KF * TP * 4
        RC = R2 + PAIR
        CS = (NT * TP * 4 + 31) // 32 * 32
        VS = (NT * TH * 4 + 31) // 32 * 32
        RCS = 2 * CS
        RG = RC + RCS
        RGS = NT * D * 4
        o_misc = RG + RGS

        w_hi = [at(f"w_hi{b}", o_w + 2 * b * HALF, [128, KF, HW], f32r) for b in range(2)]
        w_lo = [at(f"w_lo{b}", o_w + (2 * b + 1) * HALF, [128, KF, HW], f32r) for b in range(2)]
        w_raw = [at(f"w_raw{b}", o_raw + b * HALF // 2, [128, HK, HW], f32) for b in range(2)]
        xt_hi = at("xt_hi", R1, [128, KF, TP], f32r)
        xt_lo = at("xt_lo", R1 + PAIR // 2, [128, KF, TP], f32r)
        x1 = at("x1", R1, [T, NT, D], f32)
        part = at("part", R1 + R1S // 2, [T, NT, D], f32)
        gate_s = at("gate_s", R1 + R1S // 2, [128, HK, TP], f32)
        zrow = at("zrow", R1 + R1S // 2, [128, D], f32)
        xg = at("xg", R1 + R1S // 2 + HK * TP * 4, [128, BC, D], f32)
        TAIL = R2 + RGS
        k_tok = at("k_tok", R2, [T, NT, D], f32)
        at_lo = at("at_lo", R2, [128, KF, TP], f32r)
        k_exp = at("k_exp", TAIL, [128, 2, TP], f32)
        q_s = at("q_s", TAIL, [T, 2, HW], f32)
        o_s = at("o_s", TAIL, [T, 2, HW], f32)
        ctx_s = at("ctx_s", TAIL + 2 * TP * 4, [128, KF, 128], f32)
        q_t = at("q_t", TAIL + 2 * TP * 4 + KF * 512, [128, HK, TP], f32)
        bias_o = at("bias_o", TAIL + 2 * TP * 4 + KF * 512, [1, 2, D], f32)
        t2_hi = at("t2_hi", R2, [128, KF, TP], f32r)
        t2_lo = at("t2_lo", R2 + PAIR // 2, [128, KF, TP], f32r)
        XE = KF * B * 4
        xe_hi = at("xe_hi", R2, [128, KF, B], f32r)
        xe_lo = at("xe_lo", R2 + XE, [128, KF, B], f32r)
        he_hi = at("he_hi", R2 + 2 * XE, [128, KF, B], f32r)
        he_lo = at("he_lo", R2 + 3 * XE, [128, KF, B], f32r)
        y_s = at("y_s", R2 + 4 * XE, [128, 2, HW], f32)
        c_hi = at("c_hi", RC, [T, NT, TP], f32r)
        c_lo = at("c_lo", RC + RCS // 2, [T, NT, TP], f32r)
        v_tok = at("v_tok", RG, [T, NT, D], f32)
        at_hi = at("at_hi", RG, [128, KF, TP], f32r)
        g_hi = at("g_hi", RG, [T, NT, HW], f32r)
        g_lo = at("g_lo", RG + RGS // 2, [T, NT, HW], f32r)
        s_hi = at("s_hi", RC, [128, KF, TP], f32r)
        s_lo = at("s_lo", RC + PAIR // 2, [128, KF, TP], f32r)
        y_g = at("y_g", RC, [T, 2 * NT, D], f32)
        o_route = RC + PAIR
        x_s = at("x_s", o_w + 2 * HALF, [T, NT, D], f32)
        c_f = at("c_f", R2, [T, NT, 2, TH], f32)
        cv = at("cv", R2 + CS, [T, NT, TH], f32)
        ch = at("ch", R2 + CS + VS, [T, NT, TH], i32)
        deg_s = at("deg_s", R2 + CS + 2 * VS, [T, 2, TH], f32)
        off = [RG]

        def early(name, shape, dt, size):
            t = at(name, off[0], shape, dt)
            off[0] += (shape[1] * (shape[2] if len(shape) > 2 else 1) * size + 31) // 32 * 32
            return t

        src_oh = early("src_oh", [CP, OHB, N + 1], f16, 2)
        dst_oh = early("dst_oh", [CP, OHB, TH], f16, 2)
        iota_n = early("iota_n", [CP, N + 1], f16, 2)
        zero16 = early("zero16", [CP, TH], f16, 2)
        src_i = early("src_i", [CP, NC], i32, 4)
        dst_i = early("dst_i", [CP, NC], i32, 4)
        src_f = early("src_f", [CP, NC], f32, 4)
        dst_f = early("dst_f", [CP, NC], f32, 4)
        dst_w = early("dst_w", [CP, NC], f32, 4)
        dst_b = early("dst_b", [CP, NC], f32, 4)
        assert off[0] <= RG + RGS
        off = [o_misc]
        ident = early("ident", [128, 128], f32, 4)
        ones = early("ones", [128, 128], f32, 4)
        b0_s = early("b0_s", [128, KF], f32, 4)
        st = early("st", [T, 2, 6], f32, 4)
        mv = early("mv", [T, 2], f32, 4)
        ve = early("ve", [T, 1], f32, 4)
        sq = early("sq", [T, 1], f32, 4)
        rs = early("rs", [T, 1], f32, 4)
        rt = early("rt", [T, 1], f32, 4)
        k_m2 = early("k_m2", [128, 2, 2], f32, 4)
        k_nm = early("k_nm", [128, 2], f32, 4)
        k_sum = early("k_sum", [128, KF, 2], f32, 4)
        k_rs = early("k_rs", [128, KF], f32, 4)
        q_m = early("q_m", [T, HH], f32, 4)
        q_sum = early("q_sum", [T, HH], f32, 4)
        rw_raw = early("rw_raw", [128, KF, XP], f32, 4)
        rw_hi = early("rw_hi", [128, KF, XP], f32r, 4)
        rw_lo = early("rw_lo", [128, KF, XP], f32r, 4)
        tri = early("tri", [T, 128], f32, 4)
        tok_id = early("tok_id", [T, NT], u32, 4)
        slots = early("slots", [T, 2, NT], u32, 4)
        wts = early("wts", [T, 3, NT], f32, 4)
        cols = early("cols", [128, SLOTC], u32, 4)
        idx2 = early("idx2", [128, BC], u32, 4)
        table = early("table", [1, 2, MAXB], i32, 4)
        assert BASE + off[0] <= nc.sbuf_usable_end, (BASE + off[0], nc.sbuf_usable_end)
        off = [o_route]
        lgT = early("lgT", [XP, TP], f32, 4)
        lg = early("lg", [T, NT, XP], f32, 4)
        pr = early("pr", [T, NT, X], f32, 4)
        eq = early("eq", [T, NT, X], f32, 4)
        m1 = early("m1", [T, NT, X], f32, 4)
        m2 = early("m2", [T, NT, X], f32, 4)
        mm = early("mm", [T, NT, X], f32, 4)
        r1 = early("r1", [T, NT], f32, 4)
        iota_m8 = early("iota_m8", [T, X], f32, 4)
        start = early("start", [T, X], f32, 4)
        iota_j = early("iota_j", [T, MAXB], f32, 4)
        nb = early("nb", [T, X], f32, 4)
        cum = early("cum", [T, 2, X], f32, 4)
        ind = early("ind", [T, MAXB, X], f32, 4)
        je = early("je", [T, MAXB], f32, 4)
        zslot = early("zslot", [128, SLOTC], u32, 4)
        assert off[0] <= RG + RGS, (off[0], RG + RGS)

        ps = [ctx.enter_context(nc.psum_tensor(f"ps{n}", [128, 2, 512], f32)) for n in range(RING)]
        PS = lambda key: ps[slot(key)]
        as32 = lambda ap: ap.bitcast(f32)
        moving = lambda key: PS(key)[:, :, 0:TH]

        def halved(t, k, p=128):
            return t[0:p, k, :].rearrange("p (c n) -> p c n", c=2)

        ready = [sem(f"psum_ready{n}") for n in range(RING)]
        free = [sem(f"psum_free{n}") for n in range(RING)]
        w_loaded = [sem(f"w_loaded{n}") for n in range(2)]
        hi_done = sem("hi_done")
        lo_done = sem("lo_done")
        w_used = sem("w_used")
        x_loaded, idx_loaded, b0_loaded = sem("x_loaded"), sem("idx_loaded"), sem("b0_loaded")
        iotas_set, consts_set = sem("iotas_set"), sem("consts_set")
        oh_ready, oh_free = sem("oh_ready"), sem("oh_free")
        cnt_ready, cnt_free, cv_ready, cv_free = sem("cnt_ready"), sem("cnt_free"), sem("cv_ready"), sem("cv_free")
        ln_var, ln_sqrt, ln_done = sem("ln_var"), sem("ln_sqrt"), sem("ln_done")
        c_ready = sem("c_ready")
        ch_done = sem("ch_done")
        cl_done = sem("cl_done")
        hi_out = sem("hi_out")
        lo_out = sem("lo_out")
        pads_set = sem("pads_set")
        v_done, k_max, k_expd, kt_done, ctx_done = sem("v_done"), sem("k_max"), sem("k_expd"), sem("kt_done"), sem("ctx_done")
        q_sub, q_expd, q_done, qt_done = sem("q_sub"), sem("q_expd"), sem("q_done"), sem("qt_done")
        bias_loaded = sem("bias_loaded")
        o_copied = sem("o_copied")
        o_stored = [sem(f"o_stored{n}") for n in range(2)]
        h_relu = sem("h_relu")
        x1_loaded, x1_done = sem("x1_loaded"), sem("x1_done")
        rw_loaded, rwh_done, rwl_done = sem("rw_loaded"), sem("rwh_done"), sem("rwl_done")
        lgT_done, lg_sub, lg_expd, m_ready = sem("lgT_done"), sem("lg_sub"), sem("lg_expd"), sem("m_ready")
        route_set, slots_ready, table_ready = sem("route_set"), sem("slots_ready"), sem("table_ready")
        zero_stored, ids_stored, cols_loaded, xn2_stored = sem("zero_stored"), sem("ids_stored"), sem("cols_loaded"), sem("xn2_stored")
        idx_ready, xg_loaded, xg_free = sem("idx_ready"), sem("xg_loaded"), sem("xg_free")
        gate_done, prod_done = sem("gate_done"), sem("prod_done")
        silu_done = sem("silu_done")
        y_copied = sem("y_copied")
        y_stored = [sem(f"y_stored{n}") for n in range(2)]
        zrow_set = sem("zrow_set")
        y_rows = sem("y_rows")
        yg_loaded, out_ready, out_stored = sem("yg_loaded"), sem("out_ready"), sem("out_stored")

        results = ([("xt", i, f) for i in range(NT) for f in range(2)] + [("at", n) for n in range(KF)])
        for h in range(2):
            results += [("g0", h, i) for i in range(NT)] + [("h", h * HK + n) for n in range(HK)]
        for h in range(2):
            results += [("g1", h, i) for i in range(NT)]
        results += [("x2t", i, f) for i in range(NT) for f in range(2)]
        results += [("up", n) for n in range(KF)] + [("xe", s, f) for s in range(BC) for f in range(2)]
        nth = {key: n + 1 for n, key in enumerate(results)}
        R0 = len(results)
        block_results = [("he", n) for n in range(KF // 2)] + [("xe+", s, f) for s in range(BC) for f in range(2)]
        nth.update({key: R0 + n + 1 for n, key in enumerate(block_results)})
        BR = len(block_results)

        block = ctx.enter_context(nc.Block())

        @block.sync
        def _(sp):
            sp.dma_start(src_i[:, :], src.rearrange("(p c) -> p c", c=NC)).then_inc(idx_loaded, 16)
            sp.dma_start(dst_i[:, :], dst.rearrange("(p c) -> p c", c=NC)).then_inc(idx_loaded, 16)
            sp.dma_start(x_s[:, :, :], tok(x)).then_inc(x_loaded, 16)
            sp.dma_start(b0_s[:, :], b0.rearrange("(k p) -> p k", p=128),
                         allow_slow_non_contiguous=True).then_inc(b0_loaded, 16)

            def load(job, view):
                for s in range(2):
                    if job > 0:
                        sp.wait_ge(lo_done, 2 * (job - 1) + s + 1)
                    sp.dma_start(w_raw[s][:, :, :], view[:, s * HK:(s + 1) * HK, :]).then_inc(w_loaded[s], 16)

            for job in range(J_X):
                if job == J_O + 1:
                    sp.wait_ge(ready[slot(("at", KF - 1))], use(("at", KF - 1)) + 1)
                    sp.dma_start(bias_o[:, 0, :], bo.rearrange("(a n) -> a n", a=1)).then_inc(bias_loaded, 16)
                    sp.dma_start(bias_o[:, 1, :], b1.rearrange("(a n) -> a n", a=1)).then_inc(bias_loaded, 16)
                if job == J_L1 + 2:
                    sp.wait_ge(w_used, J_L1)
                    sp.wait_ge(o_stored[0], 16 * NT)
                    sp.wait_ge(o_stored[1], 16 * NT)
                    sp.dma_start(x1[:, :, :], tok(x)).then_inc(x1_loaded, 16)
                    sp.dma_start(part[:, :, :], tok(attn_d)).then_inc(x1_loaded, 16)
                    sp.dma_start(rw_raw[:, :, 0:X], router_w.rearrange("(k p) e -> p k e", p=128)).then_inc(rw_loaded, 16)
                    sp.dma_start(rw_raw[:, :, X:X + 1], gate_w.rearrange("(k p) e -> p k e", p=128),
                                 allow_slow_non_contiguous=True).then_inc(rw_loaded, 16)
                if job == J_GU + 1:
                    sp.wait_ge(ln_done, 2 * NT)
                    sp.dma_start(tok(xn2_d), part[:, :, :]).then_inc(xn2_stored, 16)
                load(job, STREAM[job])

            sp.wait_ge(table_ready, 1)
            blocks = sp.value_load(table[0:1, 1, 0:1], min_val=1, max_val=MAXB - 1)
            with sp.Fori(0, blocks) as j:
                expert = sp.value_load(table[0:1, 0, bass.ds(j, 1)], min_val=0, max_val=X - 1)
                for i in range(4):
                    for s in range(2):
                        sp.wait_ge(lo_done, j * 8 + (2 * (J_X + i - 1) + s + 1))
                        view = (w1v if i < 2 else w2v)[:, bass.ds(expert, 1), s * HK:(s + 1) * HK,
                                                       (i % 2) * HW:(i % 2 + 1) * HW]
                        sp.dma_start(w_raw[s][:, :, :], view.rearrange("p e k n -> p (e k) n")).then_inc(w_loaded[s], 16)
            for s in range(2):
                sp.wait_ge(lo_done, blocks * 8 + (2 * (J_X - 1) + s + 1))
                sp.dma_start(w_raw[s][:, :, :], w1v[:, 0, s * HK:(s + 1) * HK, 0:HW]).then_inc(w_loaded[s], 16)
            for s in range(2):
                sp.wait_ge(w_loaded[s], blocks * 64 + 16 * (J_X + 1))
            for i in range(NT):
                sp.wait_ge(out_ready, i + 1)
                sp.dma_start(out[i * T:(i + 1) * T, :], x1[:, i, :]).then_inc(out_stored, 16)
            sp.wait_ge(out_stored, 16 * NT)

        @block.gpsimd
        def _(pool):
            nc.gpsimd.iota(iota_n[:, :], [[1, N + 1]], base=0, channel_multiplier=0,
                           allow_small_or_imprecise_dtypes=True)
            nc.gpsimd.memset(zero16[:, :], 0.0)
            nc.gpsimd.memset(cv[:, :, :], 0.0)
            nc.gpsimd.memset(ch[:, :, :], 0)
            nc.gpsimd.memset(c_f[:, :, :, :], 0.0)
            nc.gpsimd.drain().then_inc(iotas_set, 1)
            nc.gpsimd.drain().then_inc(oh_free, OHB)
            nc.gpsimd.drain().then_inc(cnt_free, NT)
            nc.gpsimd.drain().then_inc(cv_ready, 1)
            nc.gpsimd.memset(ones[:, :], 1.0)
            nc.gpsimd.memset(ident[:, :], 0.0)
            nc.gpsimd.memset(tri[:, :], 1.0)
            nc.gpsimd.memset(rw_raw[:, :, :], 0.0)
            nc.gpsimd.drain()
            nc.gpsimd.affine_select(out=ident[:, :], in_=ident[:, :], compare_op=ALU.not_equal, fill=1.0, base=0,
                                    pattern=[[-1, 128]], channel_multiplier=1)
            nc.gpsimd.affine_select(out=tri[:, :], in_=tri[:, :], compare_op=ALU.is_gt, fill=0.0, base=0,
                                    pattern=[[1, 128]], channel_multiplier=-1)
            nc.gpsimd.iota(tok_id[:, :], [[T, NT]], base=0, channel_multiplier=1)
            nc.gpsimd.memset(as32(xt_hi[:, :, N:TP]), 0.0)
            nc.gpsimd.memset(as32(xt_lo[:, :, N:TP]), 0.0)
            nc.gpsimd.drain().then_inc(consts_set, 1)
            pool.wait_ge(cl_done, NT)
            nc.gpsimd.memset(q_t[:, :, N:TP], 0.0)
            nc.gpsimd.memset(ctx_s[:, :, :], 0.0)
            nc.gpsimd.drain().then_inc(pads_set, 1)
            pool.wait_ge(w_used, J_GU)
            nc.gpsimd.memset(as32(t2_hi[:, :, N:TP]), 0.0)
            nc.gpsimd.memset(as32(t2_lo[:, :, N:TP]), 0.0)
            nc.gpsimd.iota(iota_m8[:, :], [[1, X]], base=-X, channel_multiplier=0, allow_small_or_imprecise_dtypes=True)
            nc.gpsimd.iota(iota_j[:, :], [[1, MAXB]], base=0, channel_multiplier=0, allow_small_or_imprecise_dtypes=True)
            nc.gpsimd.memset(zslot[:, :], 0)
            nc.gpsimd.drain().then_inc(route_set, 1)
            pool.wait_ge(route_set, 1)
            pool.dma_start(slot_d.rearrange("(p c) o -> p (c o)", p=128), zslot[:, :]).then_inc(zero_stored, 16)
            pool.wait_ge(zero_stored, 16)
            pool.wait_ge(slots_ready, 1)
            for c in range(2):
                for i in range(NT):
                    nc.gpsimd.indirect_dma_start(
                        out=slot_d, out_offset=bass.IndirectOffsetOnAxis(ap=slots[:, c, i:i + 1], axis=0),
                        in_=tok_id[:, i:i + 1], in_offset=None).then_inc(ids_stored, 16)
            pool.wait_ge(ids_stored, 16 * 2 * NT)
            pool.dma_start(cols[:, :], slot_d.rearrange("(c p) o -> p (c o)", p=128),
                           allow_slow_non_contiguous=True).then_inc(cols_loaded, 16)
            pool.wait_ge(cols_loaded, 16)
            pool.wait_ge(xn2_stored, 16)
            pool.wait_ge(table_ready, 1)
            blocks = pool.value_load(table[0:1, 1, 0:1], min_val=1, max_val=MAXB - 1)
            nc.gpsimd.tensor_copy(idx2[:, :], cols[:, 0:BC]).then_inc(idx_ready, 1)
            pool.wait_ge(idx_ready, 1)
            for s in range(BC):
                nc.gpsimd.indirect_dma_start(
                    out=xg[:, s, :], out_offset=None, in_=xn2_d,
                    in_offset=bass.IndirectOffsetOnAxis(ap=idx2[:, s:s + 1], axis=0)).then_inc(xg_loaded, 16)
            pool.wait_ge(w_used, J_D)
            pool.wait_ge(prod_done, KF)
            nc.gpsimd.memset(zrow[:, :], 0.0)
            nc.gpsimd.drain().then_inc(zrow_set, 1)
            with pool.Fori(0, blocks) as j:
                pool.wait_ge(xg_free, j + 1)
                nc.gpsimd.tensor_copy(idx2[:, :], cols[:, bass.ds(j * BC + BC, BC)])
                nc.gpsimd.drain()
                for s in range(BC):
                    nc.gpsimd.indirect_dma_start(
                        out=xg[:, s, :], out_offset=None, in_=xn2_d,
                        in_offset=bass.IndirectOffsetOnAxis(ap=idx2[:, s:s + 1], axis=0)).then_inc(xg_loaded, 16)
            pool.wait_ge(y_rows, 16 * BC * MAXB)
            pool.wait_ge(w_used, J_X)
            for i in range(NT):
                for c in range(2):
                    nc.gpsimd.indirect_dma_start(
                        out=y_g[:, 2 * i + c, :], out_offset=None, in_=y_d,
                        in_offset=bass.IndirectOffsetOnAxis(ap=slots[:, c, i:i + 1], axis=0)).then_inc(yg_loaded, 16)
            pool.wait_ge(yg_loaded, 16 * 2 * NT)
            pool.wait_ge(xg_loaded, blocks * (16 * BC) + 16 * BC)

        @block.scalar
        def _(act):
            copy = nc.scalar.copy

            def split_hi(job, base=None):
                b = job % 2
                shift = (lambda v, per: v) if base is None else (lambda v, per: base * per + v)
                if job >= 2:
                    act.wait_ge(w_used, shift(job - 1, 4))
                for s in range(2):
                    act.wait_ge(w_loaded[s], shift(16 * (job + 1), 64))
                    copy(w_hi[b][:, s * HK:(s + 1) * HK, :], w_raw[s][:, :, :]).then_inc(hi_done, 1)

            def wait_unit(key, base=None):
                act.wait_ge(ready[slot(key)], use(key) + 1 if base is None else base * BU + (use(key) + 1))

            act.wait_ge(iotas_set, 1)
            with act.Fori(0, NG) as g:
                act.wait_ge(ln_var, g + 1)
                nc.scalar.activation(sq[:, :], ve[:, :], ACT.Sqrt).then_inc(ln_sqrt, 1)
                act.wait_ge(cnt_ready, g + 1)
                act.wait_ge(cv_free, g + 1)
                for n in range(NT):
                    src_ps = ps[n // 2][0:T, n % 2, 0:TH]
                    copy(cv[:, n, :], src_ps)
                    nc.scalar.activation(ch[:, n, :], src_ps, ACT.Copy, bias=-(DIGIT / 2 - 1) / DIGIT,
                                         scale=1.0 / DIGIT).then_inc(cnt_free, 1)
                nc.scalar.drain().then_inc(cv_ready, 1)
            split_hi(0)
            act.wait_ge(c_ready, 2)
            for n in range(NT):
                copy(c_hi[:, n, :], c_f[:, n, :, :].rearrange("p a b -> p (a b)")).then_inc(ch_done, 1)

            def hi_of(key, out_ap, in_ap, base=None):
                wait_unit(key, base)
                copy(out_ap, in_ap).then_inc(hi_out, 1)

            act.wait_ge(consts_set, 1)
            for i in range(NT):
                for f in range(2):
                    hi_of(("xt", i, f), xt_hi[:, f * HK:(f + 1) * HK, i * T:(i + 1) * T],
                          PS(("xt", i, f))[:, 0, 0:HK * T].rearrange("p (k t) -> p k t", t=T))
            for h in range(2):
                split_hi(J_V + h + 1)
                for i in range(NT):
                    wait_unit(("v", h, i))
                    copy(v_tok[:, i, h * HW:(h + 1) * HW], PS(("v", h, i))[0:T, 0, :]).then_inc(free[slot(("v", h, i))], 1)

            def keys_back(m):
                key = ("kt", m)
                wait_unit(key)
                copy(k_tok[:, 0:4, m * 128:(m + 1) * 128],
                     PS(key)[0:T, 0, :].rearrange("p (i n) -> p i n", i=4)).then_inc(kt_done, 1)
                copy(k_tok[:, 4, m * 128:(m + 1) * 128], PS(key)[0:T, 1, 0:128]).then_inc(kt_done, 1)
                act.wait_ge(kt_done, 2 * (m + 1))
                nc.scalar.drain().then_inc(free[slot(key)], 1)

            act.wait_ge(pads_set, 1)
            for m in range(KF):
                if m % HK == 0:
                    split_hi(J_K + m // HK + 1)
                wait_unit(("k", m))
                act.wait_ge(k_max, m + 1)
                if m >= 2:
                    act.wait_ge(ready[slot(("kt", m - 2))], use(("kt", m - 2)) + 1)
                nc.scalar.activation(k_exp[:, m % 2, 0:TH], PS(("k", m))[:, 0, 0:TH], ACT.Exp,
                                     bias=k_nm[:, m % 2:m % 2 + 1], accum_out=k_sum[:, m, 0:1])
                nc.scalar.activation(k_exp[:, m % 2, TH:N], PS(("k", m))[:, 1, 0:LASTH], ACT.Exp,
                                     bias=k_nm[:, m % 2:m % 2 + 1], accum_out=k_sum[:, m, 1:2])
                nc.scalar.drain().then_inc(k_expd, 1)
                nc.scalar.drain().then_inc(free[slot(("k", m))], 1)
                if m:
                    keys_back(m - 1)
            keys_back(KF - 1)

            def attention_hi(n):
                hi_of(("at", n), halved(at_hi, n), moving(("at", n)))

            for m in range(2 * NT + QLAG):
                if m - QLAG == NT:
                    for n in range(HK):
                        attention_hi(n)
                if m < 2 * NT:
                    if m % NT == 0:
                        split_hi(J_Q + m // NT + 1)
                    act.wait_ge(q_sub, m + 1)
                    nc.scalar.activation(q_s[:, m % 2, :], q_s[:, m % 2, :], ACT.Exp).then_inc(q_expd, 1)
                if m >= QLAG:
                    n = m - QLAG
                    wait_unit(("qt", n))
                    if n == NT:
                        act.wait_ge(ready[slot(("at", HK - 1))], use(("at", HK - 1)) + 1)
                    copy(q_t[:, :, n % NT * T:(n % NT + 1) * T],
                         PS(("qt", n))[:, 0, 0:HK * T].rearrange("p (k t) -> p k t", t=T)).then_inc(qt_done, 1)
                    act.wait_ge(qt_done, n + 1)
                    nc.scalar.drain().then_inc(free[slot(("qt", n))], 1)
            for n in range(HK, KF):
                attention_hi(n)
            for h in range(2):
                split_hi(J_O + h + 1)
                for i in range(NT):
                    n = h * NT + i
                    wait_unit(("o", h, i))
                    if n >= 2:
                        act.wait_ge(o_stored[n % 2], 16 * (n // 2))
                    copy(o_s[:, n % 2, :], PS(("o", h, i))[0:T, 0, :]).then_inc(free[slot(("o", h, i))], 1)
                    act.wait_ge(free[slot(("o", h, i))], use(("o", h, i)) + 1)
                    act.dma_start(attn_d[i * T:(i + 1) * T, h * HW:(h + 1) * HW],
                                  o_s[:, n % 2, :]).then_inc(o_stored[n % 2], 16)
            for h in range(2):
                split_hi(J_L0 + 2 * h + 1)
                for i in range(NT):
                    hi_of(("g0", h, i), g_hi[:, i, :], PS(("g0", h, i))[0:T, 0, :])
                split_hi(J_L0 + 2 * h + 2)
                for n in range(HK):
                    if h == 0 and n == 0:
                        act.wait_ge(o_stored[0], 16 * NT)
                        act.wait_ge(o_stored[1], 16 * NT)
                    act.wait_ge(h_relu, h * HK + n + 1)
                    hi_of(("h", h * HK + n), halved(t2_hi, h * HK + n), moving(("h", h * HK + n)))
            for h in range(2):
                split_hi(J_L1 + 2 * h + 1)
                for i in range(NT):
                    hi_of(("g1", h, i), g_hi[:, i, :], PS(("g1", h, i))[0:T, 0, :])
                split_hi(J_L1 + 2 * h + 2)
            act.wait_ge(rw_loaded, 32)
            copy(rw_hi[:, :, :], rw_raw[:, :, :]).then_inc(rwh_done, 1)
            for i in range(NT):
                act.wait_ge(ln_var, NT + i + 1)
                nc.scalar.activation(sq[:, :], ve[:, :], ACT.Sqrt).then_inc(ln_sqrt, 1)
            act.wait_ge(route_set, 1)
            for i in range(NT):
                for f in range(2):
                    hi_of(("x2t", i, f), t2_hi[:, f * HK:(f + 1) * HK, i * T:(i + 1) * T],
                          PS(("x2t", i, f))[:, 0, 0:HK * T].rearrange("p (k t) -> p k t", t=T))
            wait_unit(("lg",))
            copy(lgT[:, :].rearrange("p (c n) -> p c n", c=2), PS(("lg",))[0:XP, :, 0:TH]).then_inc(lgT_done, 1)
            act.wait_ge(lgT_done, 1)
            nc.scalar.drain().then_inc(free[slot(("lg",))], 1)
            act.wait_ge(lg_sub, 1)
            nc.scalar.activation(pr[:, :, :], pr[:, :, :], ACT.Exp).then_inc(lg_expd, 1)
            nc.scalar.activation(wts[:, 2, :], lg[:, :, X], ACT.Exp, scale=-1.0).then_inc(lg_expd, 1)
            for h in range(2):
                split_hi(J_GU + 2 * h + 1)
                for n in range(HK):
                    key = ("gt", h * HK + n)
                    wait_unit(key)
                    if h == 0 and n == 0:
                        act.wait_ge(xn2_stored, 16)
                    if h == 1:
                        act.wait_ge(prod_done, n + 1)
                    nc.scalar.activation(gate_s[:, n, :].rearrange("p (c n) -> p c n", c=2), moving(key),
                                         ACT.Silu).then_inc(gate_done, 1)
                    act.wait_ge(gate_done, h * HK + n + 1)
                    nc.scalar.drain().then_inc(free[slot(key)], 1)
                split_hi(J_GU + 2 * h + 2)
                for n in range(HK):
                    act.wait_ge(prod_done, h * HK + n + 1)
                    hi_of(("up", h * HK + n), halved(s_hi, h * HK + n), moving(("up", h * HK + n)))
            for s in range(BC):
                for f in range(2):
                    hi_of(("xe", s, f), xe_hi[:, f * HK:(f + 1) * HK, s * 128:(s + 1) * 128],
                          PS(("xe", s, f))[:, 0, :].rearrange("p (k t) -> p k t", t=128))
            for h in range(2):
                split_hi(J_D + h + 1)
            act.wait_ge(table_ready, 1)
            blocks = act.value_load(table[0:1, 1, 0:1], min_val=1, max_val=MAXB - 1)
            act.wait_ge(zrow_set, 1)
            with act.Fori(blocks, MAXB) as j:
                for s in range(BC):
                    act.dma_start(y_block(j * BC + s, 0, D), zrow[:, :]).then_inc(y_rows, 16)
            with act.Fori(0, blocks) as j:
                for h in range(2):
                    split_hi(J_X + h + 1, j)
                    for n in range(h * HK // 2, (h + 1) * HK // 2):
                        key = ("he", n)
                        wait_unit(key, j)
                        nc.scalar.activation(PS(key)[:, 0, :], PS(key)[:, 0, :], ACT.Silu).then_inc(silu_done, 1)
                        act.wait_ge(silu_done, j * (KF // 2) + (n + 1))
                        copy(he_hi[:, 2 * n:2 * n + 2, :].rearrange("p k n -> p (k n)"), PS(key)[:, 0, :]).then_inc(hi_out, 1)
                for s in range(BC):
                    for f in range(2):
                        hi_of(("xe+", s, f), xe_hi[:, f * HK:(f + 1) * HK, s * 128:(s + 1) * 128],
                              PS(("xe+", s, f))[:, 0, :].rearrange("p (k t) -> p k t", t=128), j)
                for h in range(2):
                    split_hi(J_X + 2 + h + 1, j)
                    for s in range(BC):
                        key = ("y", h, s)
                        wait_unit(key, j)
                        if h:
                            act.wait_ge(y_stored[s], j * 32 + 16)
                        copy(y_s[:, s, :], PS(key)[:, 0, :]).then_inc(y_copied, 1)
                        act.wait_ge(y_copied, j * (2 * BC) + (h * BC + s + 1))
                        act.sem_inc(free[slot(key)], 1)
                        act.dma_start(y_block(j * BC + s, h * HW, (h + 1) * HW), y_s[:, s, :]).then_inc(y_stored[s], 16)
                for s in range(BC):
                    act.wait_ge(y_stored[s], j * 32 + 32)
                act.sem_inc(y_rows, 16 * BC)

        @block.vector
        def _(dve):
            V_ = nc.vector

            def split_lo(job, base=None):
                b = job % 2
                for s in range(2):
                    done = 2 * job + s + 1
                    dve.wait_ge(hi_done, done if base is None else base * 8 + done)
                    k = slice(s * HK, (s + 1) * HK)
                    V_.tensor_tensor(w_lo[b][:, k, :], w_raw[s][:, :, :], as32(w_hi[b][:, k, :]),
                                     ALU.subtract).then_inc(lo_done, 1)

            def lo_of(key, out_ap, in_ap, hi_ap, base=None):
                dve.wait_ge(hi_out, nth[key] if base is None else base * BR + nth[key])
                V_.tensor_tensor(out_ap, in_ap, as32(hi_ap), ALU.subtract).then_inc(lo_out, 1)
                dve.wait_ge(lo_out, nth[key] if base is None else base * BR + nth[key])
                dve.sem_inc(free[slot(key)], 1)

            def wait_unit(key, base=None):
                dve.wait_ge(ready[slot(key)], use(key) + 1 if base is None else base * BU + (use(key) + 1))

            def layer_norm(in_ap, out_ap, n):
                for c in range(2):
                    V_.bn_stats(st[:, c, :], in_ap[:, c * HW:(c + 1) * HW])
                V_.drain()
                V_.bn_aggr(mv[:, :], st[:, :, :])
                V_.drain()
                V_.tensor_scalar(ve[:, :], mv[:, 1:2], EPS, None, ALU.add).then_inc(ln_var, 1)
                dve.wait_ge(ln_sqrt, n)
                V_.reciprocal(rs[:, :], sq[:, :])
                V_.drain()
                V_.tensor_tensor(rt[:, :], rs[:, :], rs[:, :], ALU.mult)
                V_.drain()
                V_.tensor_tensor(rt[:, :], rt[:, :], ve[:, :], ALU.mult)
                V_.drain()
                V_.tensor_scalar(rt[:, :], rt[:, :], -0.5, 1.5, ALU.mult, ALU.add)
                V_.drain()
                V_.tensor_tensor(rs[:, :], rs[:, :], rt[:, :], ALU.mult)
                V_.drain()
                V_.tensor_scalar(out_ap, in_ap, mv[:, 0:1], rs[:, 0:1], ALU.subtract, ALU.mult).then_inc(ln_done, 1)

            dve.wait_ge(idx_loaded, 32)
            V_.tensor_copy(src_f[:, :], src_i[:, :])
            V_.tensor_copy(dst_f[:, :], dst_i[:, :])
            V_.drain()
            V_.tensor_scalar(dst_b[:, :], dst_f[:, :], float(TH), None, ALU.is_ge)
            V_.drain()
            V_.tensor_scalar(dst_w[:, :], dst_b[:, :], DIGIT - 1.0, 1.0, ALU.mult, ALU.add)
            V_.scalar_tensor_tensor(dst_f[:, :], dst_b[:, :], -float(TH), dst_f[:, :], ALU.mult, ALU.add)
            V_.drain()

            def one_hots(n, b):
                dve.wait_ge(oh_free, n + 1)
                V_.tensor_scalar(src_oh[:, b, :], iota_n[:, :], src_f[:, bass.ds(n, 1)], None, ALU.is_equal)
                V_.tensor_scalar(dst_oh[:, b, :], iota_n[:, 0:TH], dst_f[:, bass.ds(n, 1)],
                                 dst_w[:, bass.ds(n, 1)], ALU.is_equal, ALU.mult)
                V_.drain().then_inc(oh_ready, 1)

            def unpack():
                V_.scalar_tensor_tensor(cv[:, :, :], ch[:, :, :], -DIGIT, cv[:, :, :], ALU.mult, ALU.add)
                V_.tensor_tensor(c_f[:, :, 1, :], c_f[:, :, 1, :], ch[:, :, :], ALU.add)
                V_.drain()
                V_.tensor_tensor(c_f[:, :, 0, :], c_f[:, :, 0, :], cv[:, :, :], ALU.add)
                V_.drain().then_inc(cv_free, 1)

            dve.wait_ge(iotas_set, 1)
            dve.wait_ge(x_loaded, 16)
            with dve.Fori(0, NG) as g:
                with dve.Fori(0, CG // 2 // OHB) as c:
                    for b in range(OHB):
                        one_hots(g * CG + c * OHB + b, b)
                tile = x_s[:, bass.ds(g, 1), :].rearrange("p a f -> p (a f)")
                layer_norm(tile, tile, g + 1)
                with dve.Fori(CG // 2 // OHB, CG // OHB) as c:
                    for b in range(OHB):
                        one_hots(g * CG + c * OHB + b, b)
                dve.wait_ge(cv_ready, g + 1)
                unpack()
            dve.wait_ge(cv_ready, NG + 1)
            unpack()
            V_.drain().then_inc(c_ready, 1)
            split_lo(0)
            wait_unit(("deg",))
            V_.tensor_scalar(deg_s[:, :, :], PS(("deg",))[0:T, :, 0:TH], 1.0, None, ALU.max)
            V_.drain().then_inc(free[slot(("deg",))], 1)
            V_.reciprocal(deg_s[:, :, :], deg_s[:, :, :])
            V_.drain()
            for n in range(NT):
                V_.tensor_tensor(c_f[:, n, :, :], c_f[:, n, :, :], deg_s[:, :, :], ALU.mult)
            V_.drain().then_inc(c_ready, 1)
            for n in range(NT):
                dve.wait_ge(ch_done, n + 1)
                V_.tensor_tensor(c_lo[:, n, :], c_f[:, n, :, :].rearrange("p a b -> p (a b)"), as32(c_hi[:, n, :]),
                                 ALU.subtract).then_inc(cl_done, 1)

            def transposed_lo(key, lo, hi, i, f, w=T, base=None):
                at_ = (slice(None), slice(f * HK, (f + 1) * HK), slice(i * w, (i + 1) * w))
                lo_of(key, lo[at_], PS(key)[:, 0, 0:HK * w].rearrange("p (k t) -> p k t", t=w), hi[at_], base)

            for i in range(NT):
                for f in range(2):
                    transposed_lo(("xt", i, f), xt_lo, xt_hi, i, f)
            split_lo(J_V + 1)
            split_lo(J_V + 2)

            for m in range(KF):
                if m % HK == 0:
                    split_lo(J_K + m // HK + 1)
                key, b = ("k", m), m % 2
                wait_unit(key)
                V_.reduce_max(k_m2[:, b, 0:1], PS(key)[:, 0, 0:TH], axis=AX.X)
                V_.reduce_max(k_m2[:, b, 1:2], PS(key)[:, 1, 0:LASTH], axis=AX.X)
                V_.drain()
                if m >= 2:
                    dve.wait_ge(k_expd, m - 1)
                V_.tensor_scalar(k_nm[:, b:b + 1], k_m2[:, b, 0:1], k_m2[:, b, 1:2], -1.0,
                                 ALU.max, ALU.mult).then_inc(k_max, 1)
            dve.wait_ge(k_expd, KF)
            dve.wait_ge(pads_set, 1)
            V_.tensor_tensor(k_rs[:, :], k_sum[:, :, 0], k_sum[:, :, 1], ALU.add)
            V_.drain()
            V_.reciprocal(k_rs[:, :], k_rs[:, :])
            V_.drain()
            for c in range(2):
                wait_unit(("ctx", c))
                for p in range(HK):
                    m = c * HK + p
                    for a in range(0, 128, DH):
                        V_.tensor_scalar(ctx_s[a:a + DH, m, a:a + DH],
                                         PS(("ctx", c))[a:a + DH, 0, p * 128 + a:p * 128 + a + DH],
                                         k_rs[a:a + DH, m:m + 1], None, ALU.mult)
                V_.drain().then_inc(free[slot(("ctx", c))], 1)
                V_.drain().then_inc(ctx_done, 1)

            def attention_lo(n):
                lo_of(("at", n), halved(at_lo, n), moving(("at", n)), halved(at_hi, n))

            heads = lambda ap: ap.rearrange("p (h d) -> p h d", d=DH)
            wide = lambda ap: ap.unsqueeze(2).to_broadcast([T, HH, DH])
            for m in range(2 * NT + QLAG):
                if m - QLAG == NT:
                    for n in range(HK):
                        attention_lo(n)
                if m < 2 * NT:
                    if m % NT == 0:
                        split_lo(J_Q + m // NT + 1)
                    key, b = ("q", m), m % 2
                    wait_unit(key)
                    V_.reduce_max(q_m[:, :], heads(PS(key)[0:T, 0, :]), axis=AX.X)
                    V_.drain()
                    if m >= 2:
                        dve.wait_ge(ready[slot(("qt", m - 2))], use(("qt", m - 2)) + 1)
                    V_.tensor_tensor(heads(q_s[:, b, :]), heads(PS(key)[0:T, 0, :]), wide(q_m[:, :]),
                                     ALU.subtract).then_inc(q_sub, 1)
                    V_.drain().then_inc(free[slot(key)], 1)
                    dve.wait_ge(q_expd, m + 1)
                    V_.reduce_sum(q_sum[:, :], heads(q_s[:, b, :]), axis=AX.X)
                    V_.drain()
                    V_.reciprocal(q_sum[:, :], q_sum[:, :])
                    V_.drain()
                    V_.scalar_tensor_tensor(heads(q_s[:, b, :]), heads(q_s[:, b, :]), float(DH) ** -0.5,
                                            wide(q_sum[:, :]), ALU.mult, ALU.mult).then_inc(q_done, 1)
            for n in range(HK, KF):
                attention_lo(n)
            for h in range(2):
                split_lo(J_O + h + 1)
            dve.wait_ge(b0_loaded, 16)
            for h in range(2):
                split_lo(J_L0 + 2 * h + 1)
                for i in range(NT):
                    key = ("g0", h, i)
                    lo_of(key, g_lo[:, i, :], PS(key)[0:T, 0, :], g_hi[:, i, :])
                split_lo(J_L0 + 2 * h + 2)
                for n in range(h * HK, (h + 1) * HK):
                    key = ("h", n)
                    wait_unit(key)
                    V_.tensor_scalar(moving(key), moving(key), b0_s[:, n:n + 1], 0.0, ALU.add,
                                     ALU.max).then_inc(h_relu, 1)
                    lo_of(key, halved(t2_lo, n), moving(key), halved(t2_hi, n))
            for h in range(2):
                split_lo(J_L1 + 2 * h + 1)
                for i in range(NT):
                    key = ("g1", h, i)
                    lo_of(key, g_lo[:, i, :], PS(key)[0:T, 0, :], g_hi[:, i, :])
                split_lo(J_L1 + 2 * h + 2)
                dve.wait_ge(x1_loaded, 32)
                cols_h = slice(h * HW, (h + 1) * HW)
                for i in range(NT):
                    key = ("x1", h, i)
                    wait_unit(key)
                    V_.tensor_tensor(x1[:, i, cols_h], x1[:, i, cols_h], PS(key)[0:T, 0, :], ALU.add)
                    V_.drain().then_inc(free[slot(key)], 1)
                    V_.tensor_tensor(x1[:, i, cols_h], x1[:, i, cols_h], part[:, i, cols_h], ALU.add)
                    if h == 1:
                        if i == 0:
                            dve.wait_ge(rwh_done, 1)
                            V_.tensor_tensor(rw_lo[:, :, :], rw_raw[:, :, :], as32(rw_hi[:, :, :]),
                                             ALU.subtract).then_inc(rwl_done, 1)
                        V_.drain()
                        layer_norm(x1[:, i, :], part[:, i, :], NT + i + 1)
            for i in range(NT):
                for f in range(2):
                    transposed_lo(("x2t", i, f), t2_lo, t2_hi, i, f)

            ex = lambda ap: ap.unsqueeze(2).to_broadcast([T, NT, X])
            ti = lambda ap: ap.unsqueeze(1).to_broadcast([T, NT, X])
            dve.wait_ge(route_set, 1)
            wait_unit(("lt",))
            V_.tensor_copy(lg[:, :, :], PS(("lt",))[0:T, 0, 0:NT * XP].rearrange("p (i e) -> p i e", e=XP))
            V_.drain().then_inc(free[slot(("lt",))], 1)
            V_.reduce_max(r1[:, :], lg[:, :, 0:X], axis=AX.X)
            V_.drain()
            V_.tensor_tensor(pr[:, :, :], lg[:, :, 0:X], ex(r1[:, :]), ALU.subtract).then_inc(lg_sub, 1)
            dve.wait_ge(lg_expd, 2)
            V_.reduce_sum(r1[:, :], pr[:, :, :], axis=AX.X)
            V_.tensor_scalar(wts[:, 2, :], wts[:, 2, :], 1.0, None, ALU.add)
            V_.drain()
            V_.reciprocal(r1[:, :], r1[:, :])
            V_.reciprocal(wts[:, 2, :], wts[:, 2, :])
            V_.drain()
            V_.tensor_tensor(pr[:, :, :], pr[:, :, :], ex(r1[:, :]), ALU.mult)
            V_.drain()
            for c, mask in enumerate((m1, m2)):
                V_.reduce_max(wts[:, c, :], pr[:, :, :], axis=AX.X)
                V_.drain()
                V_.tensor_tensor(eq[:, :, :], pr[:, :, :], ex(wts[:, c, :]), ALU.is_equal)
                V_.drain()
                V_.tensor_tensor(eq[:, :, :], eq[:, :, :], ti(iota_m8[:, :]), ALU.mult)
                V_.drain()
                V_.tensor_reduce(r1[:, :], eq[:, :, :], axis=AX.X, op=ALU.min)
                V_.drain()
                V_.tensor_tensor(mask[:, :, :], ti(iota_m8[:, :]), ex(r1[:, :]), ALU.is_equal)
                V_.drain()
                if c == 0:
                    V_.scalar_tensor_tensor(pr[:, :, :], m1[:, :, :], -2.0, pr[:, :, :], ALU.mult, ALU.add)
                    V_.drain()
            V_.tensor_tensor(mm[:, :, :], m1[:, :, :], m2[:, :, :], ALU.add).then_inc(m_ready, 1)

            def shared_lo(h):
                for n in range(h * HK, (h + 1) * HK):
                    key = ("up", n)
                    wait_unit(key)
                    dve.wait_ge(gate_done, n + 1)
                    V_.tensor_tensor(moving(key), moving(key), gate_s[:, n % HK, :].rearrange("p (c n) -> p c n", c=2),
                                     ALU.mult).then_inc(prod_done, 1)
                    lo_of(key, halved(s_lo, n), moving(key), halved(s_hi, n))

            split_lo(J_GU + 1)
            wait_unit(("pos",))
            pos = PS(("pos",))[0:T, 0, 0:NT * X].rearrange("p (i e) -> p i e", e=X)
            cnt = PS(("pos",))[0:T, 1, 0:X]
            V_.tensor_scalar(nb[:, :], cnt, 0.0, None, ALU.is_gt)
            V_.drain()
            for c in range(B, N, B):
                V_.scalar_tensor_tensor(nb[:, :], cnt, float(c), nb[:, :], ALU.is_gt, ALU.add)
                V_.drain()
            V_.tensor_copy(cum[:, 0, :], nb[:, :])
            V_.drain()
            for c, step in enumerate((1, 2, 4)):
                V_.tensor_copy(cum[:, (c + 1) % 2, 0:step], cum[:, c % 2, 0:step])
                V_.tensor_tensor(cum[:, (c + 1) % 2, step:X], cum[:, c % 2, step:X], cum[:, c % 2, 0:X - step], ALU.add)
                V_.drain()
            V_.tensor_tensor(start[:, :], cum[:, 1, :], nb[:, :], ALU.subtract)
            V_.drain()
            V_.tensor_scalar(start[:, :], start[:, :], float(B), None, ALU.mult)
            V_.drain()
            V_.tensor_tensor(pr[:, :, :], pos, ti(start[:, :]), ALU.add)
            V_.drain().then_inc(free[slot(("pos",))], 1)
            for c, mask in enumerate((m1, m2)):
                V_.tensor_tensor(eq[:, :, :], pr[:, :, :], mask[:, :, :], ALU.mult)
                V_.drain()
                V_.reduce_sum(r1[:, :], eq[:, :, :], axis=AX.X)
                V_.drain()
                V_.tensor_copy(slots[:, c, :], r1[:, :])
                V_.drain()
            V_.drain().then_inc(slots_ready, 1)
            be = [T, MAXB, X]
            V_.tensor_tensor(ind[:, :, :], cum[:, 1, :].unsqueeze(1).to_broadcast(be),
                             iota_j[:, :].unsqueeze(2).to_broadcast(be), ALU.is_le)
            V_.drain()
            V_.reduce_sum(je[:, :], ind[:, :, :], axis=AX.X)
            V_.drain()
            V_.tensor_scalar(table[0:1, 0, :], je[0:1, :], float(X - 1), None, ALU.min)
            V_.tensor_copy(table[0:1, 1, 0:1], cum[0:1, 1, X - 1:X])
            V_.drain().then_inc(table_ready, 1)
            for h in range(2):
                if h:
                    split_lo(J_GU + 2 * h + 1)
                split_lo(J_GU + 2 * h + 2)
                shared_lo(h)
            for s in range(BC):
                for f in range(2):
                    transposed_lo(("xe", s, f), xe_lo, xe_hi, s, f, 128)
            for h in range(2):
                split_lo(J_D + h + 1)
                for i in range(NT):
                    key = ("sd", h, i)
                    wait_unit(key)
                    part_h = x1[:, i, h * HW:(h + 1) * HW]
                    V_.scalar_tensor_tensor(part_h, PS(key)[0:T, 0, :], wts[:, 2, i:i + 1], part_h, ALU.mult, ALU.add)
                    V_.drain().then_inc(free[slot(key)], 1)
            blocks = dve.value_load(table[0:1, 1, 0:1], min_val=1, max_val=MAXB - 1)
            with dve.Fori(0, blocks) as j:
                for h in range(2):
                    split_lo(J_X + h + 1, j)
                    for n in range(h * HK // 2, (h + 1) * HK // 2):
                        key = ("he", n)
                        two = lambda t: t[:, 2 * n:2 * n + 2, :].rearrange("p k n -> p (k n)")
                        lo_of(key, two(he_lo), PS(key)[:, 0, :], two(he_hi), j)
                for s in range(BC):
                    for f in range(2):
                        transposed_lo(("xe+", s, f), xe_lo, xe_hi, s, f, 128, j)
                for h in range(2):
                    split_lo(J_X + 2 + h + 1, j)
            dve.wait_ge(yg_loaded, 16 * 2 * NT)
            for i in range(NT):
                for c in range(2):
                    V_.scalar_tensor_tensor(x1[:, i, :], y_g[:, 2 * i + c, :], wts[:, c, i:i + 1], x1[:, i, :],
                                            ALU.mult, ALU.add)
                    V_.drain()
                V_.drain().then_inc(out_ready, 1)

        @block.tensor
        def _(pe):
            mat = nc.tensor.matmul

            def claim(key, base=None):
                if base is not None:
                    pe.wait_ge(free[slot(key)], base * BU + use(key))
                elif use(key) > 0:
                    pe.wait_ge(free[slot(key)], use(key))

            def passes(out_ap, left, right, start, stop):
                (lh, ll), (rh, rl) = left, right
                mat(out_ap, lh, rh, start=start, stop=False)
                mat(out_ap, lh, rl, start=False, stop=False)
                return mat(out_ap, ll, rh, start=False, stop=stop)

            def weights(job, base=None):
                pe.wait_ge(lo_done, 2 * (job + 1) if base is None else base * 8 + 2 * (job + 1))
                return w_hi[job % 2], w_lo[job % 2]

            def by_tokens(key, out_ap, operand, job, tokens, start=True, stop=True):
                wh, wl = w_hi[job % 2], w_lo[job % 2]
                for k in range(KF):
                    last = passes(out_ap, [t[:, k, tokens] for t in operand], (wh[:, k, :], wl[:, k, :]),
                                  start and k == 0, stop and k == KF - 1)
                return last

            def by_features(key, n, operand, job, stop=True):
                wh, wl = w_hi[job % 2], w_lo[job % 2]
                for c in range(2):
                    for k in range(KF):
                        w_cols = slice(n % HK * 128, (n % HK + 1) * 128)
                        last = passes(PS(key)[:, c, 0:TH], (wh[:, k, w_cols], wl[:, k, w_cols]),
                                      [t[:, k, c * TH:(c + 1) * TH] for t in operand], k == 0, stop and k == KF - 1)
                return last

            tile = lambda i: slice(i * T, (i + 1) * T)
            XT, T2, AT, SH, XEP, HE = (xt_hi, xt_lo), (t2_hi, t2_lo), (at_hi, at_lo), (s_hi, s_lo), (xe_hi, xe_lo), (he_hi, he_lo)

            pe.wait_ge(iotas_set, 1)
            acc = [ps[n // 2][0:T, n % 2, 0:TH] for n in range(NT)]
            with pe.Fori(0, NG) as g:
                pe.wait_ge(cnt_free, g * NT + NT)
                for n in range(NT):
                    mat(acc[n], zero16[:, 0:T], zero16[:, :], start=True, stop=False)
                with pe.Fori(0, CG // OHB) as c:
                    for b in range(OHB):
                        pe.wait_ge(oh_ready, g * CG + c * OHB + (b + 1))
                        for n in range(NT):
                            last = mat(acc[n], src_oh[:, b, n * T:(n + 1) * T], dst_oh[:, b, :], start=False, stop=False)
                        last.then_inc(oh_free, 1)
                for n in range(NT):
                    last = mat(acc[n], zero16[:, 0:T], zero16[:, :], start=False, stop=True)
                last.then_inc(cnt_ready, 1)
            pe.wait_ge(cnt_free, NG * NT + NT)
            pe.wait_ge(consts_set, 1)
            pe.wait_ge(c_ready, 1)
            for c in range(2):
                for n in range(NT):
                    last = mat(PS(("deg",))[0:T, c, 0:TH], ones[0:T, 0:T], c_f[:, n, c, :], start=n == 0, stop=n == NT - 1)
            last.then_inc(ready[slot(("deg",))], 1)

            def transposes(key, source, count, width, ins, base=None):
                claim(key, base)
                for a in range(count):
                    last = nc.tensor.transpose(PS(key)[:, 0, a * width:(a + 1) * width], source(a), ident[0:ins, 0:ins])
                last.then_inc(ready[slot(key)], 1)

            for i in range(NT):
                pe.wait_ge(ln_done, i + 1)
                for f in range(2):
                    transposes(("xt", i, f), lambda a: x_s[:, i, (f * HK + a) * 128:(f * HK + a + 1) * 128], HK, T, T)
            for h in range(2):
                weights(J_V + h)
                for i in range(NT):
                    key = ("v", h, i)
                    pe.wait_ge(lo_out, nth[("xt", NT - 1, 1)])
                    claim(key)
                    last = by_tokens(key, PS(key)[0:T, 0, :], XT, J_V + h, tile(i))
                    last.then_inc(ready[slot(key)], 1)
                nc.tensor.drain().then_inc(w_used, 1)

            def keys_back(m):
                key = ("kt", m)
                pe.wait_ge(k_expd, m + 1)
                claim(key)
                for i in range(NT):
                    last = nc.tensor.transpose(PS(key)[0:T, i // 4, i % 4 * 128:(i % 4 + 1) * 128],
                                               k_exp[:, m % 2, tile(i)], ident[:, :])
                last.then_inc(ready[slot(key)], 1)

            for m in range(KF):
                if m % HK == 0:
                    weights(J_K + m // HK)
                key = ("k", m)
                claim(key)
                by_features(key, m, XT, J_K + m // HK).then_inc(ready[slot(key)], 1)
                if m % HK == HK - 1:
                    nc.tensor.drain().then_inc(w_used, 1)
                if m:
                    keys_back(m - 1)
            keys_back(KF - 1)
            pe.wait_ge(kt_done, 2 * KF)
            for c in range(2):
                key = ("ctx", c)
                claim(key)
                for p in range(HK):
                    m = c * HK + p
                    for i in range(NT):
                        last = mat(PS(key)[:, 0, p * 128:(p + 1) * 128], k_tok[:, i, m * 128:(m + 1) * 128],
                                   v_tok[:, i, m * 128:(m + 1) * 128], start=i == 0, stop=i == NT - 1)
                last.then_inc(ready[slot(key)], 1)

            def attend(n):
                key = ("at", n)
                pe.wait_ge(ctx_done, 2)
                pe.wait_ge(qt_done, NT if n < HK else 2 * NT)
                claim(key)
                for c in range(2):
                    last = mat(PS(key)[:, c, 0:TH], ctx_s[:, n, :], q_t[:, n % HK, c * TH:(c + 1) * TH], start=True, stop=True)
                last.then_inc(ready[slot(key)], 1)

            for m in range(2 * NT + QLAG):
                if m - QLAG == NT:
                    for n in range(HK):
                        attend(n)
                if m < 2 * NT:
                    if m % NT == 0:
                        weights(J_Q + m // NT)
                    key = ("q", m)
                    claim(key)
                    by_tokens(key, PS(key)[0:T, 0, :], XT, J_Q + m // NT, tile(m % NT)).then_inc(ready[slot(key)], 1)
                    if m % NT == NT - 1:
                        nc.tensor.drain().then_inc(w_used, 1)
                if m >= QLAG:
                    n = m - QLAG
                    pe.wait_ge(q_done, n + 1)
                    transposes(("qt", n), lambda a: q_s[:, n % 2, a * 128:(a + 1) * 128], HK, T, T)
            for n in range(HK, KF):
                attend(n)
            pe.wait_ge(lo_out, nth[("at", KF - 1)])
            pe.wait_ge(bias_loaded, 32)
            for h in range(2):
                weights(J_O + h)
                for i in range(NT):
                    key = ("o", h, i)
                    claim(key)
                    by_tokens(key, PS(key)[0:T, 0, :], AT, J_O + h, tile(i), stop=False)
                    for a in range(2):
                        last = mat(PS(key)[0:T, 0, :], ones[0:1, 0:T], bias_o[:, a, h * HW:(h + 1) * HW],
                                   start=False, stop=a == 1)
                    last.then_inc(ready[slot(key)], 1)
                nc.tensor.drain().then_inc(w_used, 1)
            pe.wait_ge(cl_done, NT)
            for h in range(2):
                job = J_L0 + 2 * h
                weights(job)
                for i in range(NT):
                    key = ("g0", h, i)
                    claim(key)
                    by_tokens(key, PS(key)[0:T, 0, :], XT, job, tile(i)).then_inc(ready[slot(key)], 1)
                nc.tensor.drain().then_inc(w_used, 1)
                weights(job + 1)
                for n in range(h * HK, (h + 1) * HK):
                    key = ("h", n)
                    claim(key)
                    by_features(key, n, XT, job + 1, stop=False)
                    pe.wait_ge(lo_out, nth[("g0", h, NT - 1)])
                    g_cols = slice(n % HK * 128, (n % HK + 1) * 128)
                    for c in range(2):
                        for i in range(NT):
                            last = passes(PS(key)[:, c, 0:TH], (g_hi[:, i, g_cols], g_lo[:, i, g_cols]),
                                          [t[:, i, c * TH:(c + 1) * TH] for t in (c_hi, c_lo)], False, i == NT - 1)
                    last.then_inc(ready[slot(key)], 1)
                nc.tensor.drain().then_inc(w_used, 1)
            for h in range(2):
                job = J_L1 + 2 * h
                weights(job)
                for i in range(NT):
                    key = ("g1", h, i)
                    pe.wait_ge(lo_out, nth[("h", KF - 1)])
                    claim(key)
                    by_tokens(key, PS(key)[0:T, 0, :], T2, job, tile(i)).then_inc(ready[slot(key)], 1)
                nc.tensor.drain().then_inc(w_used, 1)
                weights(job + 1)
                for i in range(NT):
                    key = ("x1", h, i)
                    claim(key)
                    by_tokens(key, PS(key)[0:T, 0, :], T2, job + 1, tile(i), stop=False)
                    pe.wait_ge(lo_out, nth[("g1", h, NT - 1)])
                    for s in range(NT):
                        last = passes(PS(key)[0:T, 0, :], [t[:, s, tile(i)] for t in (c_hi, c_lo)],
                                      (g_hi[:, s, :], g_lo[:, s, :]), False, s == NT - 1)
                    last.then_inc(ready[slot(key)], 1)
                nc.tensor.drain().then_inc(w_used, 1)
            for i in range(NT):
                pe.wait_ge(ln_done, NT + i + 1)
                for f in range(2):
                    transposes(("x2t", i, f), lambda a: part[:, i, (f * HK + a) * 128:(f * HK + a + 1) * 128], HK, T, T)
            pe.wait_ge(lo_out, nth[("x2t", NT - 1, 1)])
            pe.wait_ge(rwl_done, 1)
            pe.wait_ge(route_set, 1)
            key = ("lg",)
            claim(key)
            for c in range(2):
                for k in range(KF):
                    last = passes(PS(key)[0:XP, c, 0:TH], (rw_hi[:, k, :], rw_lo[:, k, :]),
                                  [t[:, k, c * TH:(c + 1) * TH] for t in T2], k == 0, k == KF - 1)
            last.then_inc(ready[slot(key)], 1)
            key = ("lt",)
            pe.wait_ge(lgT_done, 1)
            claim(key)
            for i in range(NT):
                last = nc.tensor.transpose(PS(key)[0:T, 0, i * XP:(i + 1) * XP], lgT[:, tile(i)], ident[0:XP, 0:XP])
            last.then_inc(ready[slot(key)], 1)
            for h in range(2):
                for a, name in enumerate(("gt", "up")):
                    job = J_GU + 2 * h + a
                    weights(job)
                    for n in range(h * HK, (h + 1) * HK):
                        key = (name, n)
                        claim(key)
                        by_features(key, n, T2, job).then_inc(ready[slot(key)], 1)
                    nc.tensor.drain().then_inc(w_used, 1)
                    if h == 0 and a == 0:
                        key = ("pos",)
                        pe.wait_ge(m_ready, 1)
                        claim(key)
                        for i in range(NT):
                            out_ap = PS(key)[0:T, 0, i * X:(i + 1) * X]
                            for b in range(i):
                                mat(out_ap, ones[0:T, 0:T], mm[:, b, :], start=b == 0, stop=False)
                            mat(out_ap, tri[:, 0:T], mm[:, i, :], start=i == 0, stop=True)
                        for i in range(NT):
                            last = mat(PS(key)[0:T, 1, 0:X], ones[0:T, 0:T], mm[:, i, :], start=i == 0, stop=i == NT - 1)
                        last.then_inc(ready[slot(key)], 1)
            pe.wait_ge(xg_loaded, 16 * BC)
            for s in range(BC):
                for f in range(2):
                    transposes(("xe", s, f), lambda a: xg[:, s, (f * HK + a) * 128:(f * HK + a + 1) * 128], HK, 128, 128)
            nc.tensor.drain().then_inc(xg_free, 1)
            for h in range(2):
                weights(J_D + h)
                for i in range(NT):
                    key = ("sd", h, i)
                    pe.wait_ge(lo_out, nth[("up", KF - 1)])
                    claim(key)
                    by_tokens(key, PS(key)[0:T, 0, :], SH, J_D + h, tile(i)).then_inc(ready[slot(key)], 1)
                nc.tensor.drain().then_inc(w_used, 1)
            pe.wait_ge(table_ready, 1)
            blocks = pe.value_load(table[0:1, 1, 0:1], min_val=1, max_val=MAXB - 1)
            with pe.Fori(0, blocks) as j:
                pe.wait_ge(lo_out, j * BR + R0)
                for h in range(2):
                    wh, wl = weights(J_X + h, j)
                    for n in range(h * HK // 2, (h + 1) * HK // 2):
                        key = ("he", n)
                        claim(key, j)
                        for a in range(2):
                            w_cols = slice((2 * n + a) % HK * 128, ((2 * n + a) % HK + 1) * 128)
                            for k in range(KF):
                                last = passes(PS(key)[:, 0, a * B:(a + 1) * B], (wh[:, k, w_cols], wl[:, k, w_cols]),
                                              (xe_hi[:, k, :], xe_lo[:, k, :]), k == 0, k == KF - 1)
                        last.then_inc(ready[slot(key)], 1)
                    nc.tensor.drain().then_inc(w_used, 1)
                pe.wait_ge(xg_loaded, j * (16 * BC) + 2 * 16 * BC)
                for s in range(BC):
                    for f in range(2):
                        transposes(("xe+", s, f), lambda a: xg[:, s, (f * HK + a) * 128:(f * HK + a + 1) * 128],
                                   HK, 128, 128, j)
                nc.tensor.drain().then_inc(xg_free, 1)
                pe.wait_ge(lo_out, j * BR + nth[("he", KF // 2 - 1)])
                for h in range(2):
                    weights(J_X + 2 + h, j)
                    for s in range(BC):
                        key = ("y", h, s)
                        claim(key, j)
                        by_tokens(key, PS(key)[:, 0, :], HE, J_X + h, slice(s * 128, (s + 1) * 128)).then_inc(ready[slot(key)], 1)
                    nc.tensor.drain().then_inc(w_used, 1)


_INS = ['x', 'src', 'dst', 'L0_gnn_W_self0', 'L0_gnn_W_neigh0', 'L0_gnn_b0', 'L0_gnn_W_self1', 'L0_gnn_W_neigh1',
        'L0_gnn_b1', 'L0_mix_Wq', 'L0_mix_Wk', 'L0_mix_Wv', 'L0_mix_Wo', 'L0_mix_bo', 'L0_ffn_router_w', 'L0_ffn_w1',
        'L0_ffn_w2', 'L0_ffn_shared_gate_up', 'L0_ffn_shared_down', 'L0_ffn_shared_gate_w']


def kernel(**inputs):
    import numpy as _np
    import concourse.bacc as _bacc
    from concourse import mybir as _mybir
    from concourse.bass_utils import run_bass_kernel_spmd as _run

    nc = _bacc.Bacc("TRN2", target_bir_lowering=False, num_devices=1)
    arrays, args = {}, []
    for name in _INS:
        a = _np.ascontiguousarray(inputs[name])
        arrays[f"in_{name}"] = a
        args.append(nc.dram_tensor(f"in_{name}", a.shape, _mybir.dt.from_np(a.dtype), kind="ExternalInput").ap())
    shape = arrays["in_x"].shape
    args.append(nc.dram_tensor("out_0", shape, _mybir.dt.float32, kind="ExternalOutput").ap())
    gps_layer(nc, *args)
    r = _run(nc, [arrays], core_ids=[0])
    return r.results[0]["out_0"]
```

```python
import concourse.bass as bass
from concourse import mybir
from contextlib import ExitStack


def gps_layer(nc, x, src, dst, w_self0, w_neigh0, b0, w_self1, w_neigh1, b1,
              wq, wk, wv, wo, bo, router_w, w1, w2, gate_up, down, gate_w, out):
    f32, f32r, f16 = mybir.dt.float32, mybir.dt.float32r, mybir.dt.float16
    i32, u32 = mybir.dt.int32, mybir.dt.uint32
    ALU, ACT, AX = mybir.AluOpType, mybir.ActivationFunctionType, mybir.AxisListType

    N, D = x.shape
    E = src.shape[0]
    T = 125
    NT = N // T
    KF = D // 128
    HW = D // 2
    HK = KF // 2
    TP = 628
    TH = TP // 2
    LASTH = N - TH
    DH = 64
    HH = HW // DH
    X = router_w.shape[1]
    XP = X + 2
    B = 256
    BC = B // 128
    MAXB = X + (2 * N - X) // B + 1
    SLOTC = MAXB * BC
    CP = 125
    NC = E // CP
    NG = 5
    CG = NC // NG
    CB = 4
    GB = CG // CB
    OHB = 2
    GP = GB // OHB
    CD = (3, 2, 2, 2)
    DIGIT = 4096.0
    EPS = 1e-5
    assert CG * CP < DIGIT and CG % (CB * OHB) == 0 and NT * T == N and NC * CP == E

    halves = lambda m: [m[:, h * HW:(h + 1) * HW].rearrange("(k p) n -> p k n", p=128) for h in range(2)]
    gate, up = gate_up[:, 0:D], gate_up[:, D:2 * D]
    V, K, Q, O = halves(wv), halves(wk), halves(wq), halves(wo)
    N0, S0, N1, S1 = halves(w_neigh0), halves(w_self0), halves(w_neigh1), halves(w_self1)
    G, U, Dn = halves(gate), halves(up), halves(down)
    STREAM = [V[0], V[1], K[0], K[1], Q[0], Q[1], O[0], O[1], N0[0], S0[0], N0[1], S0[1],
              N1[0], S1[0], N1[1], S1[1], G[0], U[0], G[1], U[1], Dn[0]]
    (J_V, J_K, J_Q, J_O, J_L0, J_L1, J_GU, J_D, J_X) = (0, 2, 4, 6, 8, 12, 16, 20, 21)
    w1v = w1.rearrange("e (k p) n -> p e k n", p=128)
    w2v = w2.rearrange("e (k p) n -> p e k n", p=128)

    RING = 4
    units = [("deg",)]
    KLAG = QLAG = 2
    Q_SPLITS = {0: (5, 0), 1: (5, 1), NT + 1: (6, 0), NT + 3: (6, 1)}
    for m in range(KF + KLAG):
        units += ([("k", m)] if m < KF else []) + ([("ctx", 0)] if m == KF + KLAG - 1 else [])
        units += [("kt", m - KLAG)] if m >= KLAG else []
    units += [("ctx", 1)]
    for m in range(2 * NT + QLAG):
        if m - QLAG == NT:
            units += [("at", n) for n in range(HK)]
        if m < 2 * NT:
            units += [("q", m)]
        if m >= QLAG:
            units += [("qt", m - QLAG)]
    units += [("at", n) for n in range(HK, KF)]
    units += [("o", h, i) for h in range(2) for i in range(NT)]
    for h in range(2):
        units += [("g0", h, i) for i in range(NT)] + [("h", h * HK + n) for n in range(HK)]
    for h in range(2):
        units += [("g1", h, i) for i in range(NT)] + [("x1", h, i) for i in range(NT)]
    units += [("x2t", i, f) for i in range(NT) for f in range(2)] + [("lg",), ("lt",)]
    for h in range(2):
        units += [("gt", h * HK + n) for n in range(HK)] + ([("pos",)] if h == 0 else [])
        units += [("up", h * HK + n) for n in range(HK)]
    units += [("xe", s, f) for s in range(BC) for f in range(2)]
    units += [("sd", 0, i) for i in range(NT)]
    U0 = len(units)
    place = {key: n for n, key in enumerate(units)}
    XEP = [(s, f) for s in range(BC) for f in range(2)]
    block_units = ([("he", n) for n in range(KF // 2)] + [("xe+", s, f) for s, f in XEP[:-1]]
                   + [("y", 0, 0), ("xe+",) + XEP[-1]] + [("y", h, s) for h in range(2) for s in range(BC)][1:])
    BU = len(block_units) // RING
    assert BU * RING == len(block_units)
    place.update({key: U0 + n for n, key in enumerate(block_units)})
    place.update({("sd", 1, i): U0 + i for i in range(NT)})
    SIDE = 3
    side = []
    for g in range(NG):
        side += ([("v", 0, g - 1)] if g else []) + [("xt", g, 0), ("xt", g, 1)] + ([("v", 1, g - 1)] if g else [])
    side += [("v", 0, NT - 1), ("v", 1, NT - 1)]
    side_place = {key: n for n, key in enumerate(side)}
    assert NG == NT
    slot = lambda key: RING + side_place[key] % SIDE if key in side_place else place[key] % RING
    use = lambda key: side_place[key] // SIDE if key in side_place else place[key] // RING

    last_unit = {J_V: ("v", 0, NT - 1), J_V + 1: ("v", 1, NT - 1), J_GU: ("gt", HK - 1), J_GU + 1: ("up", HK - 1),
                 J_GU + 2: ("gt", KF - 1), J_GU + 3: ("up", KF - 1), J_D: ("sd", 0, NT - 1)}
    for h in range(2):
        last_unit.update({J_K + h: ("k", (h + 1) * HK - 1), J_Q + h: ("q", (h + 1) * NT - 1), J_O + h: ("o", h, NT - 1),
                          J_L0 + 2 * h: ("g0", h, NT - 1), J_L0 + 2 * h + 1: ("h", (h + 1) * HK - 1),
                          J_L1 + 2 * h: ("g1", h, NT - 1), J_L1 + 2 * h + 1: ("x1", h, NT - 1),
                          J_X + h: ("he", (h + 1) * HK // 2 - 1), J_X + 2 + h: ("y", h, BC - 1)})
    assert J_D == J_X - 1 and place[last_unit[J_D]] == U0 - 1

    v_d = nc.dram_tensor("values", (N, D), f32, kind="Internal").ap()
    attn_d = nc.dram_tensor("attn_out", (N, D), f32, kind="Internal").ap()
    xn2_d = nc.dram_tensor("xn2_rows", (N, D), f32, kind="Internal").ap()
    slot_d = nc.dram_tensor("token_of_slot", (SLOTC * 128, 1), u32, kind="Internal").ap()
    y_d = nc.dram_tensor("expert_rows", (SLOTC * 128, D), f32, kind="Internal").ap()
    y_c = y_d.rearrange("(c p) f -> p c f", p=128)
    y_block = lambda c, f0, f1: y_c[:, bass.ds(c, 1), f0:f1].rearrange("p c f -> p (c f)")
    tok = lambda a: a.rearrange("(i p) f -> p i f", p=T)

    ctx = ExitStack()
    with ctx:
        sem = lambda name: ctx.enter_context(nc.semaphore(name))
        BASE = (nc.sbuf_base + 31) // 32 * 32

        def at(name, offset, shape, dt):
            return nc.alloc_sbuf_tensor_at(name, shape, dt, offset=BASE + offset)

        HALF = KF * HW * 4
        o_w = 0
        o_raw = o_w + 4 * HALF
        R1 = o_raw + HALF
        R1S = 2 * NT * D * 4
        R2 = R1 + R1S
        PAIR = 2 * KF * TP * 4
        RC = R2 + PAIR
        CS = (NT * TP * 4 + 31) // 32 * 32
        VS = (NT * TH * 4 + 31) // 32 * 32
        RCS = 2 * CS
        RG = RC + RCS
        RGS = NT * D * 4
        o_misc = RG + RGS

        w_hi = [at(f"w_hi{b}", o_w + 2 * b * HALF, [128, KF, HW], f32r) for b in range(2)]
        w_lo = [at(f"w_lo{b}", o_w + (2 * b + 1) * HALF, [128, KF, HW], f32r) for b in range(2)]
        w_raw = [at(f"w_raw{b}", o_raw + b * HALF // 2, [128, HK, HW], f32) for b in range(2)]
        xt_hi = at("xt_hi", R1, [128, KF, TP], f32r)
        xt_lo = at("xt_lo", R1 + PAIR // 2, [128, KF, TP], f32r)
        x1 = at("x1", R1, [T, NT, D], f32)
        part = at("part", R1 + R1S // 2, [T, NT, D], f32)
        gate_s = at("gate_s", R1 + R1S // 2, [128, HK, TP], f32)
        zrow = at("zrow", R1 + R1S // 2, [128, D], f32)
        xg = at("xg", R1 + R1S // 2 + HK * TP * 4, [128, BC, D], f32)
        TAIL = R2 + RGS
        k_tok = at("k_tok", R2, [T, NT, D], f32)
        at_lo = at("at_lo", R2, [128, KF, TP], f32r)
        k_exp = at("k_exp", TAIL, [128, 2, TP], f32)
        q_s = at("q_s", TAIL, [T, 2, HW], f32)
        o_s = at("o_s", TAIL, [T, 2, HW], f32)
        ctx_s = at("ctx_s", TAIL + 2 * TP * 4, [128, KF, 128], f32)
        q_t = at("q_t", TAIL + 2 * TP * 4 + KF * 512, [128, HK, TP], f32)
        bias_o = at("bias_o", TAIL + 2 * TP * 4 + KF * 512, [1, 2, D], f32)
        t2_hi = at("t2_hi", R2, [128, KF, TP], f32r)
        t2_lo = at("t2_lo", R2 + PAIR // 2, [128, KF, TP], f32r)
        XE = KF * B * 4
        xe_hi = at("xe_hi", R2, [128, KF, B], f32r)
        xe_lo = at("xe_lo", R2 + XE, [128, KF, B], f32r)
        he_hi = at("he_hi", R2 + 2 * XE, [128, KF, B], f32r)
        he_lo = at("he_lo", R2 + 3 * XE, [128, KF, B], f32r)
        y_s = at("y_s", R2 + 4 * XE, [128, 2, HW], f32)
        c_hi = at("c_hi", RC, [T, NT, TP], f32r)
        c_lo = at("c_lo", RC + RCS // 2, [T, NT, TP], f32r)
        v_tok = at("v_tok", RG, [T, NT, D], f32)
        at_hi = at("at_hi", RG, [128, KF, TP], f32r)
        g_hi = at("g_hi", RG, [T, NT, HW], f32r)
        g_lo = at("g_lo", RG + RGS // 2, [T, NT, HW], f32r)
        y_g = [at("y_first", R1 + R1S // 2, [T, NT, D], f32), at("y_second", R2, [T, NT, D], f32)]
        assert R1S // 2 <= 4 * XE
        s_hi = at("s_hi", RC, [128, KF, TP], f32r)
        s_lo = at("s_lo", RC + PAIR // 2, [128, KF, TP], f32r)
        o_route = RC + PAIR
        x_s = at("x_s", RC, [T, NT, D], f32)
        c_f = at("c_f", R2, [T, NT, 2, TH], f32)
        cv = at("cv", R2 + CS, [T, NT, TH], f32)
        ch = at("ch", R2 + CS + VS, [T, NT, TH], i32)
        deg_s = at("deg_s", R2 + CS + 2 * VS, [T, 2, TH], f32)
        off = [RG]

        def early(name, shape, dt, size):
            t = at(name, off[0], shape, dt)
            off[0] += (shape[1] * (shape[2] if len(shape) > 2 else 1) * size + 31) // 32 * 32
            return t

        src_oh = early("src_oh", [CP, OHB * CB, N + 1], f16, 2)
        dst_oh = early("dst_oh", [CP, OHB * CB, TH], f16, 2)
        iota_n = early("iota_n", [CP, N + 1], f16, 2)
        zero16 = early("zero16", [CP, TH], f16, 2)
        assert off[0] <= RG + RGS
        off = [R2 + CS + 2 * VS + (2 * TH * 4 + 31) // 32 * 32]
        src_i = early("src_i", [CP, NC], i32, 4)
        dst_i = early("dst_i", [CP, NC], i32, 4)
        edge = early("edge", [CP, NC, 4], f32, 4)
        away = early("away", [CP, CB - min(CD), TH], f16, 2)
        v_s = early("v_s", [T, 2, HW], f32, 4)
        assert off[0] <= R2 + PAIR
        off = [o_misc]
        ident = early("ident", [128, 128], f32, 4)
        ones = early("ones", [128, 128], f32, 4)
        b0_s = early("b0_s", [128, KF], f32, 4)
        st = early("st", [T, 2, 6], f32, 4)
        mv = early("mv", [T, 2], f32, 4)
        ve = early("ve", [T, 1], f32, 4)
        sq = early("sq", [T, 1], f32, 4)
        rs = early("rs", [T, 1], f32, 4)
        rt = early("rt", [T, 1], f32, 4)
        nm = early("nm", [T, 1], f32, 4)
        k_m2 = early("k_m2", [128, 2, 2], f32, 4)
        k_nm = early("k_nm", [128, 2], f32, 4)
        k_sum = early("k_sum", [128, KF, 2], f32, 4)
        k_rs = early("k_rs", [128, KF], f32, 4)
        q_m = early("q_m", [T, HH], f32, 4)
        q_sum = early("q_sum", [T, HH], f32, 4)
        rw_raw = early("rw_raw", [128, KF, XP], f32, 4)
        rw_hi = early("rw_hi", [128, KF, XP], f32r, 4)
        rw_lo = early("rw_lo", [128, KF, XP], f32r, 4)
        tri = early("tri", [T, 128], f32, 4)
        tok_id = early("tok_id", [T, NT], u32, 4)
        slots = early("slots", [T, 2, NT], u32, 4)
        wts = early("wts", [T, 3, NT], f32, 4)
        cols = early("cols", [128, SLOTC], u32, 4)
        idx2 = early("idx2", [128, BC], u32, 4)
        table = early("table", [1, 2, MAXB], i32, 4)
        assert BASE + off[0] <= nc.sbuf_usable_end, (BASE + off[0], nc.sbuf_usable_end)
        off = [o_route]
        lgT = early("lgT", [XP, TP], f32, 4)
        lg = early("lg", [T, NT, XP], f32, 4)
        pr = early("pr", [T, NT, X], f32, 4)
        eq = early("eq", [T, NT, X], f32, 4)
        m1 = early("m1", [T, NT, X], f32, 4)
        m2 = early("m2", [T, NT, X], f32, 4)
        mm = early("mm", [T, NT, X], f32, 4)
        r1 = early("r1", [T, NT], f32, 4)
        iota_m8 = early("iota_m8", [T, X], f32, 4)
        start = early("start", [T, X], f32, 4)
        iota_j = early("iota_j", [T, MAXB], f32, 4)
        nb = early("nb", [T, X], f32, 4)
        cum = early("cum", [T, 2, X], f32, 4)
        ind = early("ind", [T, MAXB, X], f32, 4)
        je = early("je", [T, MAXB], f32, 4)
        zslot = early("zslot", [128, SLOTC], u32, 4)
        assert off[0] <= RG + RGS, (off[0], RG + RGS)

        ps = [ctx.enter_context(nc.psum_tensor(f"ps{n}", [128, 2, 512], f32)) for n in range(RING)]
        PS = lambda key: ps[slot(key)]
        side_banks = [ps[2][:, 1, :], ps[3][:, 0, :], ps[3][:, 1, :]]
        PB = lambda key: side_banks[slot(key) - RING] if slot(key) >= RING else ps[slot(key)][:, 0, :]
        as32 = lambda ap: ap.bitcast(f32)
        moving = lambda key: PS(key)[:, :, 0:TH]

        def halved(t, k, p=128):
            return t[0:p, k, :].rearrange("p (c n) -> p c n", c=2)

        ready = [sem(f"psum_ready{n}") for n in range(RING + SIDE)]
        free = [sem(f"psum_free{n}") for n in range(RING + SIDE)]
        w_loaded = [sem(f"w_loaded{n}") for n in range(2)]
        hi_done = sem("hi_done")
        lo_done = sem("lo_done")
        x_loaded, idx_loaded, b0_loaded = sem("x_loaded"), sem("idx_loaded"), sem("b0_loaded")
        edges_set = sem("edges_set")
        iotas_set, consts_set = sem("iotas_set"), sem("consts_set")
        oh_ready, oha_ready, oh_free = sem("oh_ready"), sem("oha_ready"), sem("oh_free")
        cnt_ready, cnt_free, cv_ready, cv_free = sem("cnt_ready"), sem("cnt_free"), sem("cv_ready"), sem("cv_free")
        ln_var, ln_sqrt, ln_scale, ln_done = sem("ln_var"), sem("ln_sqrt"), sem("ln_scale"), sem("ln_done")
        c_ready = sem("c_ready")
        ch_done = sem("ch_done")
        cl_done = sem("cl_done")
        hi_out = sem("hi_out")
        lo_out = sem("lo_out")
        pads_set = sem("pads_set")
        v_copied, v_loaded = sem("v_copied"), sem("v_loaded")
        v_stored = [sem(f"v_stored{n}") for n in range(2)]
        k_max, k_expd, kt_done, ctx_done = sem("k_max"), sem("k_expd"), sem("kt_done"), sem("ctx_done")
        q_sub, q_expd, q_done, qt_done = sem("q_sub"), sem("q_expd"), sem("q_done"), sem("qt_done")
        bias_loaded = sem("bias_loaded")
        o_copied = sem("o_copied")
        o_stored = [sem(f"o_stored{n}") for n in range(2)]
        h_relu = sem("h_relu")
        x1_loaded, x1_done = sem("x1_loaded"), sem("x1_done")
        rw_loaded, rwh_done, rwl_done = sem("rw_loaded"), sem("rwh_done"), sem("rwl_done")
        lgT_done, lg_sub, lg_expd, m_ready = sem("lgT_done"), sem("lg_sub"), sem("lg_expd"), sem("m_ready")
        route_set, slots_ready, table_ready = sem("route_set"), sem("slots_ready"), sem("table_ready")
        zero_stored, ids_stored, cols_loaded, xn2_stored = sem("zero_stored"), sem("ids_stored"), sem("cols_loaded"), sem("xn2_stored")
        idx_ready, xg_loaded = sem("idx_ready"), sem("xg_loaded")
        gate_done, prod_done = sem("gate_done"), sem("prod_done")
        silu_done = sem("silu_done")
        y_copied = sem("y_copied")
        y_stored = [sem(f"y_stored{n}") for n in range(2)]
        zrow_set, gather_clear = sem("zrow_set"), sem("gather_clear")
        y_rows = sem("y_rows")
        yg_loaded = [[sem(f"yg_loaded{i}_{c}") for c in range(2)] for i in range(NT)]
        out_ready, out_stored = sem("out_ready"), sem("out_stored")

        results = ([("xt", i, f) for i in range(NT) for f in range(2)] + [("at", n) for n in range(KF)])
        for h in range(2):
            results += [("g0", h, i) for i in range(NT)] + [("h", h * HK + n) for n in range(HK)]
        for h in range(2):
            results += [("g1", h, i) for i in range(NT)]
        results += [("x2t", i, f) for i in range(NT) for f in range(2)]
        results += [("up", n) for n in range(KF)] + [("xe", s, f) for s in range(BC) for f in range(2)]
        nth = {key: n + 1 for n, key in enumerate(results)}
        R0 = len(results)
        block_results = [("he", n) for n in range(KF // 2)] + [("xe+", s, f) for s in range(BC) for f in range(2)]
        nth.update({key: R0 + n + 1 for n, key in enumerate(block_results)})
        BR = len(block_results)

        block = ctx.enter_context(nc.Block())

        @block.sync
        def _(sp):
            sp.dma_start(src_i[:, :], src.rearrange("(p c) -> p c", c=NC)).then_inc(idx_loaded, 16)
            sp.dma_start(dst_i[:, :], dst.rearrange("(p c) -> p c", c=NC)).then_inc(idx_loaded, 16)
            sp.dma_start(x_s[:, :, :], tok(x)).then_inc(x_loaded, 16)
            sp.dma_start(b0_s[:, :], b0.rearrange("(k p) -> p k", p=128),
                         allow_slow_non_contiguous=True).then_inc(b0_loaded, 16)

            def load(job, view):
                for s in range(2):
                    if job > 0:
                        sp.wait_ge(lo_done, 2 * (job - 1) + s + 1)
                    sp.dma_start(w_raw[s][:, :, :], view[:, s * HK:(s + 1) * HK, :]).then_inc(w_loaded[s], 16)

            for job in range(J_X):
                if job == J_O + 1:
                    sp.wait_ge(ready[slot(("at", KF - 1))], use(("at", KF - 1)) + 1)
                    sp.dma_start(bias_o[:, 0, :], bo.rearrange("(a n) -> a n", a=1)).then_inc(bias_loaded, 16)
                    sp.dma_start(bias_o[:, 1, :], b1.rearrange("(a n) -> a n", a=1)).then_inc(bias_loaded, 16)
                if job == J_L1 + 2:
                    sp.wait_ge(ready[slot(("h", KF - 1))], use(("h", KF - 1)) + 1)
                    sp.wait_ge(o_stored[0], 16 * NT)
                    sp.wait_ge(o_stored[1], 16 * NT)
                    sp.dma_start(x1[:, :, :], tok(x)).then_inc(x1_loaded, 16)
                    sp.dma_start(part[:, :, :], tok(attn_d)).then_inc(x1_loaded, 16)
                    sp.dma_start(rw_raw[:, :, 0:X], router_w.rearrange("(k p) e -> p k e", p=128)).then_inc(rw_loaded, 16)
                    sp.dma_start(rw_raw[:, :, X:X + 1], gate_w.rearrange("(k p) e -> p k e", p=128),
                                 allow_slow_non_contiguous=True).then_inc(rw_loaded, 16)
                if job == J_GU + 1:
                    sp.wait_ge(ln_done, 2 * NT)
                    sp.dma_start(tok(xn2_d), part[:, :, :]).then_inc(xn2_stored, 16)
                if job == J_Q:
                    sp.wait_ge(cnt_ready, NG)
                    for n in range(2):
                        sp.wait_ge(v_stored[n], 16 * NT)
                    sp.dma_start(v_tok[:, :, :], tok(v_d)).then_inc(v_loaded, 16)
                load(job, STREAM[job])

            sp.wait_ge(table_ready, 1)
            blocks = sp.value_load(table[0:1, 1, 0:1], min_val=1, max_val=MAXB - 1)
            with sp.Fori(0, blocks) as j:
                expert = sp.value_load(table[0:1, 0, bass.ds(j, 1)], min_val=0, max_val=X - 1)
                for i in range(4):
                    for s in range(2):
                        sp.wait_ge(lo_done, j * 8 + (2 * (J_X + i - 1) + s + 1))
                        view = (w1v if i < 2 else w2v)[:, bass.ds(expert, 1), s * HK:(s + 1) * HK,
                                                       (i % 2) * HW:(i % 2 + 1) * HW]
                        sp.dma_start(w_raw[s][:, :, :], view.rearrange("p e k n -> p (e k) n")).then_inc(w_loaded[s], 16)
            for s in range(2):
                sp.wait_ge(lo_done, blocks * 8 + (2 * (J_X - 1) + s + 1))
                sp.dma_start(w_raw[s][:, :, :], Dn[1][:, s * HK:(s + 1) * HK, :]).then_inc(w_loaded[s], 16)
            for i in range(NT):
                for h in range(2):
                    sp.wait_ge(out_ready, 2 * i + h + 1)
                    cols_h = slice(h * HW, (h + 1) * HW)
                    sp.dma_start(out[i * T:(i + 1) * T, cols_h], x1[:, i, cols_h]).then_inc(out_stored, 16)
            sp.wait_ge(out_stored, 16 * 2 * NT)

        @block.gpsimd
        def _(pool):
            nc.gpsimd.iota(iota_n[:, :], [[1, N + 1]], base=0, channel_multiplier=0,
                           allow_small_or_imprecise_dtypes=True)
            nc.gpsimd.memset(zero16[:, :], 0.0)
            nc.gpsimd.drain().then_inc(iotas_set, 1)
            nc.gpsimd.drain().then_inc(oh_free, OHB)
            nc.gpsimd.drain().then_inc(cnt_free, 1)
            nc.gpsimd.memset(c_f[:, :, :, :], 0.0)
            nc.gpsimd.memset(ones[:, :], 1.0)
            nc.gpsimd.memset(ident[:, :], 0.0)
            nc.gpsimd.memset(tri[:, :], 1.0)
            nc.gpsimd.memset(rw_raw[:, :, :], 0.0)
            nc.gpsimd.drain()
            nc.gpsimd.affine_select(out=ident[:, :], in_=ident[:, :], compare_op=ALU.not_equal, fill=1.0, base=0,
                                    pattern=[[-1, 128]], channel_multiplier=1)
            nc.gpsimd.affine_select(out=tri[:, :], in_=tri[:, :], compare_op=ALU.is_gt, fill=0.0, base=0,
                                    pattern=[[1, 128]], channel_multiplier=-1)
            nc.gpsimd.iota(tok_id[:, :], [[T, NT]], base=0, channel_multiplier=1)
            nc.gpsimd.memset(as32(xt_hi[:, :, N:TP]), 0.0)
            nc.gpsimd.memset(as32(xt_lo[:, :, N:TP]), 0.0)
            nc.gpsimd.drain().then_inc(consts_set, 1)
            pool.wait_ge(cl_done, NT)
            for n in range(2):
                pool.wait_ge(v_stored[n], 16 * NT)
            nc.gpsimd.memset(q_t[:, :, N:TP], 0.0)
            nc.gpsimd.memset(ctx_s[:, :, :], 0.0)
            nc.gpsimd.drain().then_inc(pads_set, 1)
            pool.wait_ge(ready[slot(("x1", 1, NT - 1))], use(("x1", 1, NT - 1)) + 1)
            nc.gpsimd.memset(as32(t2_hi[:, :, N:TP]), 0.0)
            nc.gpsimd.memset(as32(t2_lo[:, :, N:TP]), 0.0)
            nc.gpsimd.iota(iota_m8[:, :], [[1, X]], base=-X, channel_multiplier=0, allow_small_or_imprecise_dtypes=True)
            nc.gpsimd.iota(iota_j[:, :], [[1, MAXB]], base=0, channel_multiplier=0, allow_small_or_imprecise_dtypes=True)
            nc.gpsimd.memset(zslot[:, :], 0)
            nc.gpsimd.drain().then_inc(route_set, 1)
            pool.wait_ge(route_set, 1)
            pool.dma_start(slot_d.rearrange("(p c) o -> p (c o)", p=128), zslot[:, :]).then_inc(zero_stored, 16)
            pool.wait_ge(zero_stored, 16)
            pool.wait_ge(slots_ready, 1)
            for c in range(2):
                for i in range(NT):
                    nc.gpsimd.indirect_dma_start(
                        out=slot_d, out_offset=bass.IndirectOffsetOnAxis(ap=slots[:, c, i:i + 1], axis=0),
                        in_=tok_id[:, i:i + 1], in_offset=None).then_inc(ids_stored, 16)
            pool.wait_ge(ids_stored, 16 * 2 * NT)
            pool.dma_start(cols[:, :], slot_d.rearrange("(c p) o -> p (c o)", p=128),
                           allow_slow_non_contiguous=True).then_inc(cols_loaded, 16)
            pool.wait_ge(cols_loaded, 16)
            pool.wait_ge(xn2_stored, 16)
            pool.wait_ge(table_ready, 1)
            blocks = pool.value_load(table[0:1, 1, 0:1], min_val=1, max_val=MAXB - 1)
            nc.gpsimd.tensor_copy(idx2[:, :], cols[:, 0:BC]).then_inc(idx_ready, 1)
            pool.wait_ge(idx_ready, 1)
            for s in range(BC):
                nc.gpsimd.indirect_dma_start(
                    out=xg[:, s, :], out_offset=None, in_=xn2_d,
                    in_offset=bass.IndirectOffsetOnAxis(ap=idx2[:, s:s + 1], axis=0)).then_inc(xg_loaded, 16)
            pool.wait_ge(ready[slot(("up", KF - 1))], use(("up", KF - 1)) + 1)
            pool.wait_ge(prod_done, KF)
            nc.gpsimd.memset(zrow[:, :], 0.0)
            nc.gpsimd.drain().then_inc(zrow_set, 1)
            with pool.Fori(0, blocks) as j:
                pool.wait_ge(lo_out, j * BR + R0)
                nc.gpsimd.tensor_copy(idx2[:, :], cols[:, bass.ds(j * BC + BC, BC)])
                nc.gpsimd.drain()
                for s in range(BC):
                    nc.gpsimd.indirect_dma_start(
                        out=xg[:, s, :], out_offset=None, in_=xn2_d,
                        in_offset=bass.IndirectOffsetOnAxis(ap=idx2[:, s:s + 1], axis=0)).then_inc(xg_loaded, 16)
            pool.wait_ge(xg_loaded, blocks * (16 * BC) + 16 * BC)
            pool.wait_ge(lo_out, blocks * BR + R0)
            for s in range(BC):
                pool.wait_ge(y_stored[s], blocks * 32 + 16)
            pool.sem_inc(gather_clear, 1)
            pool.wait_ge(gather_clear, 1)
            pool.wait_ge(y_rows, 16 * BC * MAXB)
            for i in range(NT):
                for c in range(2):
                    nc.gpsimd.indirect_dma_start(
                        out=y_g[c][:, i, :], out_offset=None, in_=y_d,
                        in_offset=bass.IndirectOffsetOnAxis(ap=slots[:, c, i:i + 1], axis=0)).then_inc(yg_loaded[i][c], 16)

        @block.scalar
        def _(act):
            copy = nc.scalar.copy

            def wait_unit(key, base=None):
                act.wait_ge(ready[slot(key)], use(key) + 1 if base is None else base * BU + (use(key) + 1))

            def split_hi(job, base=None, quarters=(0, 1)):
                b = job % 2
                shift = (lambda v, per: v) if base is None else (lambda v, per: base * per + v)
                if job >= 2:
                    wait_unit(last_unit[job - 2], base)
                for s in quarters:
                    act.wait_ge(w_loaded[s], shift(16 * (job + 1), 64))
                    copy(w_hi[b][:, s * HK:(s + 1) * HK, :], w_raw[s][:, :, :]).then_inc(hi_done, 1)

            def destinations(g, p):
                for b in range(OHB):
                    n = g * GB + p * OHB + b
                    act.wait_ge(oh_free, n + 1)
                    for c in range(CD[p], CB):
                        nc.scalar.activation(away[:, c - CD[p], :], iota_n[:, 0:TH], ACT.Abs,
                                             bias=edge[:, n * CB + c, 1:2], scale=-1.0)
                    nc.scalar.drain()
                    for c in range(CD[p], CB):
                        nc.scalar.activation(dst_oh[:, b * CB + c, :], away[:, c - CD[p], :], ACT.Relu,
                                             bias=edge[:, n * CB + c, 2:3], scale=edge[:, n * CB + c, 3:4])
                    nc.scalar.drain().then_inc(oha_ready, 1)

            act.wait_ge(iotas_set, 1)
            act.wait_ge(edges_set, 1)

            def hi_of(key, out_ap, in_ap, base=None):
                wait_unit(key, base)
                copy(out_ap, in_ap).then_inc(hi_out, 1)

            def normal_hi(i):
                for f in range(2):
                    hi_of(("xt", i, f), xt_hi[:, f * HK:(f + 1) * HK, i * T:(i + 1) * T],
                          PB(("xt", i, f))[:, 0:HK * T].rearrange("p (k t) -> p k t", t=T))

            def values(h, i):
                key = ("v", h, i)
                n = [k for k in side if k[0] == "v"].index(key)
                wait_unit(key)
                if i:
                    act.wait_ge(v_stored[h], 16 * i)
                copy(v_s[:, h, :], PB(key)[0:T, :]).then_inc(v_copied, 1)
                act.wait_ge(v_copied, n + 1)
                nc.scalar.drain().then_inc(free[slot(key)], 1)
                act.dma_start(v_d[i * T:(i + 1) * T, h * HW:(h + 1) * HW], v_s[:, h, :]).then_inc(v_stored[h], 16)

            for g in range(NG):
                destinations(g, 0)
                if g > 1:
                    values(1, g - 2)
                if g:
                    normal_hi(g - 1)
                destinations(g, 1)
                if g < 2:
                    split_hi(g, quarters=(0,))
                destinations(g, 2)
                act.wait_ge(ln_var, g + 1)
                nc.scalar.activation(sq[:, :], ve[:, :], ACT.Sqrt).then_inc(ln_sqrt, 1)
                if g:
                    values(0, g - 1)
                destinations(g, 3)
                act.wait_ge(ln_scale, g + 1)
                nc.scalar.activation(x_s[:, g, :], x_s[:, g, :], ACT.Identity, bias=nm[:, :],
                                     scale=rs[:, :]).then_inc(ln_done, 1)
                if g < 2:
                    split_hi(g, quarters=(1,))
                if g:
                    act.wait_ge(cv_free, g)
                act.wait_ge(cnt_ready, g + 1)
                for n in range(0, NT, 2):
                    w = min(2, NT - n)
                    copy(cv[:, n:n + w, :], ps[n // 2][0:T, 0:w, 0:TH])
                nc.scalar.drain().then_inc(cnt_free, 1)
                nc.scalar.drain().then_inc(cv_ready, 1)
            values(1, NT - 2)
            normal_hi(NT - 1)
            values(0, NT - 1)
            split_hi(J_K)
            values(1, NT - 1)
            act.wait_ge(c_ready, 2)
            for n in range(NT):
                copy(c_hi[:, n, :], c_f[:, n, :, :].rearrange("p a b -> p (a b)")).then_inc(ch_done, 1)

            def keys_back(m):
                key = ("kt", m)
                wait_unit(key)
                copy(k_tok[:, 0:4, m * 128:(m + 1) * 128],
                     PS(key)[0:T, 0, :].rearrange("p (i n) -> p i n", i=4)).then_inc(kt_done, 1)
                copy(k_tok[:, 4, m * 128:(m + 1) * 128], PS(key)[0:T, 1, 0:128]).then_inc(kt_done, 1)
                act.wait_ge(kt_done, 2 * (m + 1))
                nc.scalar.drain().then_inc(free[slot(key)], 1)

            act.wait_ge(cl_done, NT)
            for m in range(KF + KLAG):
                if m < KF:
                    wait_unit(("k", m))
                    act.wait_ge(k_max, m + 1)
                    if m >= 2:
                        act.wait_ge(ready[slot(("kt", m - 2))], use(("kt", m - 2)) + 1)
                    nc.scalar.activation(k_exp[:, m % 2, 0:TH], PS(("k", m))[:, 0, 0:TH], ACT.Exp,
                                         bias=k_nm[:, m % 2:m % 2 + 1], accum_out=k_sum[:, m, 0:1])
                    nc.scalar.activation(k_exp[:, m % 2, TH:N], PS(("k", m))[:, 1, 0:LASTH], ACT.Exp,
                                         bias=k_nm[:, m % 2:m % 2 + 1], accum_out=k_sum[:, m, 1:2])
                    nc.scalar.drain().then_inc(k_expd, 1)
                    nc.scalar.drain().then_inc(free[slot(("k", m))], 1)
                if m >= KLAG:
                    keys_back(m - KLAG)
                if m % HK == 0 and m < KF:
                    split_hi(J_K + m // HK + 1)
            act.wait_ge(pads_set, 1)

            def attention_hi(n):
                hi_of(("at", n), halved(at_hi, n), moving(("at", n)))

            for m in range(2 * NT + QLAG):
                if m - QLAG == NT:
                    for n in range(HK):
                        attention_hi(n)
                if m < 2 * NT:
                    act.wait_ge(q_sub, m + 1)
                    nc.scalar.activation(q_s[:, m % 2, :], q_s[:, m % 2, :], ACT.Exp).then_inc(q_expd, 1)
                    if m in Q_SPLITS:
                        split_hi(Q_SPLITS[m][0], quarters=Q_SPLITS[m][1:])
                if m >= QLAG:
                    n = m - QLAG
                    wait_unit(("qt", n))
                    if n == NT:
                        act.wait_ge(ready[slot(("at", HK - 1))], use(("at", HK - 1)) + 1)
                    copy(q_t[:, :, n % NT * T:(n % NT + 1) * T],
                         PS(("qt", n))[:, 0, 0:HK * T].rearrange("p (k t) -> p k t", t=T)).then_inc(qt_done, 1)
                    act.wait_ge(qt_done, n + 1)
                    nc.scalar.drain().then_inc(free[slot(("qt", n))], 1)
            for n in range(HK, KF):
                attention_hi(n)
            for h in range(2):
                split_hi(J_O + h + 1)
                for i in range(NT):
                    n = h * NT + i
                    wait_unit(("o", h, i))
                    if n >= 2:
                        act.wait_ge(o_stored[n % 2], 16 * (n // 2))
                    copy(o_s[:, n % 2, :], PS(("o", h, i))[0:T, 0, :]).then_inc(free[slot(("o", h, i))], 1)
                    act.wait_ge(free[slot(("o", h, i))], use(("o", h, i)) + 1)
                    act.dma_start(attn_d[i * T:(i + 1) * T, h * HW:(h + 1) * HW],
                                  o_s[:, n % 2, :]).then_inc(o_stored[n % 2], 16)
            for h in range(2):
                split_hi(J_L0 + 2 * h + 1)
                for i in range(NT):
                    hi_of(("g0", h, i), g_hi[:, i, :], PS(("g0", h, i))[0:T, 0, :])
                split_hi(J_L0 + 2 * h + 2)
                for n in range(HK):
                    if h == 0 and n == 0:
                        act.wait_ge(o_stored[0], 16 * NT)
                        act.wait_ge(o_stored[1], 16 * NT)
                    act.wait_ge(h_relu, h * HK + n + 1)
                    hi_of(("h", h * HK + n), halved(t2_hi, h * HK + n), moving(("h", h * HK + n)))
            for h in range(2):
                split_hi(J_L1 + 2 * h + 1)
                for i in range(NT):
                    hi_of(("g1", h, i), g_hi[:, i, :], PS(("g1", h, i))[0:T, 0, :])
                split_hi(J_L1 + 2 * h + 2)
            act.wait_ge(rw_loaded, 32)
            copy(rw_hi[:, :, :], rw_raw[:, :, :]).then_inc(rwh_done, 1)
            for i in range(NT):
                act.wait_ge(ln_var, NT + i + 1)
                nc.scalar.activation(sq[:, :], ve[:, :], ACT.Sqrt).then_inc(ln_sqrt, 1)
                act.wait_ge(ln_scale, NT + i + 1)
                nc.scalar.activation(part[:, i, :], x1[:, i, :], ACT.Identity, bias=nm[:, :],
                                     scale=rs[:, :]).then_inc(ln_done, 1)
            act.wait_ge(route_set, 1)
            for i in range(NT):
                for f in range(2):
                    hi_of(("x2t", i, f), t2_hi[:, f * HK:(f + 1) * HK, i * T:(i + 1) * T],
                          PS(("x2t", i, f))[:, 0, 0:HK * T].rearrange("p (k t) -> p k t", t=T))
            wait_unit(("lg",))
            copy(lgT[:, :].rearrange("p (c n) -> p c n", c=2), PS(("lg",))[0:XP, :, 0:TH]).then_inc(lgT_done, 1)
            act.wait_ge(lgT_done, 1)
            nc.scalar.drain().then_inc(free[slot(("lg",))], 1)
            act.wait_ge(lg_sub, 1)
            nc.scalar.activation(pr[:, :, :], pr[:, :, :], ACT.Exp).then_inc(lg_expd, 1)
            nc.scalar.activation(wts[:, 2, :], lg[:, :, X], ACT.Exp, scale=-1.0).then_inc(lg_expd, 1)
            for h in range(2):
                split_hi(J_GU + 2 * h + 1)
                for n in range(HK):
                    key = ("gt", h * HK + n)
                    wait_unit(key)
                    if h == 0 and n == 0:
                        act.wait_ge(xn2_stored, 16)
                    if h == 1:
                        act.wait_ge(prod_done, n + 1)
                    nc.scalar.activation(gate_s[:, n, :].rearrange("p (c n) -> p c n", c=2), moving(key),
                                         ACT.Silu).then_inc(gate_done, 1)
                    act.wait_ge(gate_done, h * HK + n + 1)
                    nc.scalar.drain().then_inc(free[slot(key)], 1)
                split_hi(J_GU + 2 * h + 2)
                for n in range(HK):
                    act.wait_ge(prod_done, h * HK + n + 1)
                    hi_of(("up", h * HK + n), halved(s_hi, h * HK + n), moving(("up", h * HK + n)))
            for s in range(BC):
                for f in range(2):
                    hi_of(("xe", s, f), xe_hi[:, f * HK:(f + 1) * HK, s * 128:(s + 1) * 128],
                          PS(("xe", s, f))[:, 0, :].rearrange("p (k t) -> p k t", t=128))
            split_hi(J_X)
            act.wait_ge(table_ready, 1)
            blocks = act.value_load(table[0:1, 1, 0:1], min_val=1, max_val=MAXB - 1)
            act.wait_ge(zrow_set, 1)
            for s in range(BC):
                act.dma_start(y_c[:, (MAXB - 1) * BC + s, 0:HW], zrow[:, 0:HW]).then_inc(y_stored[s], 16)
                act.dma_start(y_c[:, (MAXB - 1) * BC + s, HW:D], zrow[:, HW:D]).then_inc(y_rows, 16)
            with act.Fori(blocks, MAXB - 1) as j:
                for s in range(BC):
                    act.dma_start(y_block(j * BC + s, 0, D), zrow[:, :]).then_inc(y_rows, 16)
            with act.Fori(0, blocks) as j:
                for h in range(2):
                    split_hi(J_X + h + 1, j)
                    for n in range(h * HK // 2, (h + 1) * HK // 2):
                        key = ("he", n)
                        wait_unit(key, j)
                        nc.scalar.activation(PS(key)[:, 0, :], PS(key)[:, 0, :], ACT.Silu).then_inc(silu_done, 1)
                        act.wait_ge(silu_done, j * (KF // 2) + (n + 1))
                        copy(he_hi[:, 2 * n:2 * n + 2, :].rearrange("p k n -> p (k n)"), PS(key)[:, 0, :]).then_inc(hi_out, 1)

                def rows_hi(s, f):
                    hi_of(("xe+", s, f), xe_hi[:, f * HK:(f + 1) * HK, s * 128:(s + 1) * 128],
                          PS(("xe+", s, f))[:, 0, :].rearrange("p (k t) -> p k t", t=128), j)

                for s, f in XEP[:-1]:
                    rows_hi(s, f)
                for h in range(2):
                    split_hi(J_X + 2 + h + 1, j)
                    for s in range(BC):
                        key = ("y", h, s)
                        wait_unit(key, j)
                        act.wait_ge(y_stored[s], j * 32 + (16 * h + 16))
                        copy(y_s[:, s, :], PS(key)[:, 0, :]).then_inc(y_copied, 1)
                        act.wait_ge(y_copied, j * (2 * BC) + (h * BC + s + 1))
                        act.sem_inc(free[slot(key)], 1)
                        act.dma_start(y_block(j * BC + s, h * HW, (h + 1) * HW), y_s[:, s, :]).then_inc(y_stored[s], 16)
                        if h == s == 0:
                            rows_hi(*XEP[-1])
                act.sem_inc(y_rows, 16 * BC)

        @block.vector
        def _(dve):
            V_ = nc.vector

            def split_lo(job, base=None, quarters=(0, 1)):
                b = job % 2
                for s in quarters:
                    done = 2 * job + s + 1
                    dve.wait_ge(hi_done, done if base is None else base * 8 + done)
                    k = slice(s * HK, (s + 1) * HK)
                    V_.tensor_tensor(w_lo[b][:, k, :], w_raw[s][:, :, :], as32(w_hi[b][:, k, :]),
                                     ALU.subtract).then_inc(lo_done, 1)

            def lo_of(key, out_ap, in_ap, hi_ap, base=None):
                dve.wait_ge(hi_out, nth[key] if base is None else base * BR + nth[key])
                V_.tensor_tensor(out_ap, in_ap, as32(hi_ap), ALU.subtract).then_inc(lo_out, 1)
                dve.wait_ge(lo_out, nth[key] if base is None else base * BR + nth[key])
                dve.sem_inc(free[slot(key)], 1)

            def wait_unit(key, base=None):
                dve.wait_ge(ready[slot(key)], use(key) + 1 if base is None else base * BU + (use(key) + 1))

            def moments(in_ap):
                for c in range(2):
                    V_.bn_stats(st[:, c, :], in_ap[:, c * HW:(c + 1) * HW])
                V_.drain()
                V_.bn_aggr(mv[:, :], st[:, :, :])
                V_.drain()
                V_.tensor_scalar(ve[:, :], mv[:, 1:2], EPS, None, ALU.add).then_inc(ln_var, 1)

            def norm_scale(n):
                dve.wait_ge(ln_sqrt, n)
                V_.reciprocal(rs[:, :], sq[:, :])
                V_.drain()
                V_.tensor_tensor(rt[:, :], rs[:, :], rs[:, :], ALU.mult)
                V_.drain()
                V_.tensor_tensor(rt[:, :], rt[:, :], ve[:, :], ALU.mult)
                V_.drain()
                V_.tensor_scalar(rt[:, :], rt[:, :], -0.5, 1.5, ALU.mult, ALU.add)
                V_.drain()
                V_.tensor_tensor(rs[:, :], rs[:, :], rt[:, :], ALU.mult)
                V_.drain()
                V_.scalar_tensor_tensor(nm[:, :], mv[:, 0:1], -1.0, rs[:, :], ALU.mult, ALU.mult)
                V_.drain().then_inc(ln_scale, 1)

            dve.wait_ge(idx_loaded, 32)
            V_.tensor_copy(edge[:, :, 0], src_i[:, :])
            V_.tensor_copy(edge[:, :, 1], dst_i[:, :])
            V_.drain()
            V_.tensor_scalar(edge[:, :, 3], edge[:, :, 1], float(TH), None, ALU.is_ge)
            V_.drain()
            V_.tensor_scalar(edge[:, :, 2], edge[:, :, 3], DIGIT - 1.0, 1.0, ALU.mult, ALU.add)
            V_.scalar_tensor_tensor(edge[:, :, 1], edge[:, :, 3], -float(TH), edge[:, :, 1], ALU.mult, ALU.add)
            V_.drain()
            V_.tensor_scalar(edge[:, :, 3], edge[:, :, 2], -1.0, None, ALU.mult)
            V_.drain().then_inc(edges_set, 1)

            def one_hots(g, p):
                for b in range(OHB):
                    n = g * GB + p * OHB + b
                    dve.wait_ge(oh_free, n + 1)
                    for c in range(CB):
                        e = n * CB + c
                        V_.tensor_scalar(src_oh[:, b * CB + c, :], iota_n[:, :], edge[:, e, 0:1], None, ALU.is_equal)
                        if c < CD[p]:
                            V_.tensor_scalar(dst_oh[:, b * CB + c, :], iota_n[:, 0:TH], edge[:, e, 1:2], edge[:, e, 2:3],
                                             ALU.is_equal, ALU.mult)
                    V_.drain().then_inc(oh_ready, 1)

            def unpack():
                V_.tensor_scalar(ch[:, :, :], cv[:, :, :], 1.0 / DIGIT, -(DIGIT / 2 - 1) / DIGIT, ALU.mult, ALU.add)
                V_.drain()
                V_.scalar_tensor_tensor(cv[:, :, :], ch[:, :, :], -DIGIT, cv[:, :, :], ALU.mult, ALU.add)
                V_.tensor_tensor(c_f[:, :, 1, :], c_f[:, :, 1, :], ch[:, :, :], ALU.add)
                V_.drain()
                V_.tensor_tensor(c_f[:, :, 0, :], c_f[:, :, 0, :], cv[:, :, :], ALU.add)
                V_.drain().then_inc(cv_free, 1)

            dve.wait_ge(iotas_set, 1)

            def transposed_lo(key, lo, hi, i, f, w=T, base=None):
                at_ = (slice(None), slice(f * HK, (f + 1) * HK), slice(i * w, (i + 1) * w))
                lo_of(key, lo[at_], PB(key)[:, 0:HK * w].rearrange("p (k t) -> p k t", t=w), hi[at_], base)

            for g in range(NG):
                one_hots(g, 0)
                if g:
                    for f in range(2):
                        transposed_lo(("xt", g - 1, f), xt_lo, xt_hi, g - 1, f)
                one_hots(g, 1)
                if g:
                    dve.wait_ge(cv_ready, g)
                    unpack()
                else:
                    dve.wait_ge(consts_set, 1)
                    dve.wait_ge(x_loaded, 16)
                    moments(x_s[:, g, :])
                one_hots(g, 2)
                if g < 2:
                    split_lo(g, quarters=(0,))
                norm_scale(g + 1)
                one_hots(g, 3)
                if g < 2:
                    split_lo(g, quarters=(1,))
                if g < NG - 1:
                    moments(x_s[:, g + 1, :])
            for f in range(2):
                transposed_lo(("xt", NT - 1, f), xt_lo, xt_hi, NT - 1, f)
            dve.wait_ge(cv_ready, NG)
            unpack()
            V_.drain().then_inc(c_ready, 1)
            split_lo(J_K)
            wait_unit(("deg",))
            V_.tensor_scalar(deg_s[:, :, :], PS(("deg",))[0:T, :, 0:TH], 1.0, None, ALU.max)
            V_.drain().then_inc(free[slot(("deg",))], 1)
            V_.reciprocal(deg_s[:, :, :], deg_s[:, :, :])
            V_.drain()
            for n in range(NT):
                V_.tensor_tensor(c_f[:, n, :, :], c_f[:, n, :, :], deg_s[:, :, :], ALU.mult)
            V_.drain().then_inc(c_ready, 1)
            for n in range(NT):
                dve.wait_ge(ch_done, n + 1)
                V_.tensor_tensor(c_lo[:, n, :], c_f[:, n, :, :].rearrange("p a b -> p (a b)"), as32(c_hi[:, n, :]),
                                 ALU.subtract).then_inc(cl_done, 1)

            for m in range(KF):
                key, b = ("k", m), m % 2
                wait_unit(key)
                V_.reduce_max(k_m2[:, b, 0:1], PS(key)[:, 0, 0:TH], axis=AX.X)
                V_.reduce_max(k_m2[:, b, 1:2], PS(key)[:, 1, 0:LASTH], axis=AX.X)
                V_.drain()
                if m >= 2:
                    dve.wait_ge(k_expd, m - 1)
                V_.tensor_scalar(k_nm[:, b:b + 1], k_m2[:, b, 0:1], k_m2[:, b, 1:2], -1.0,
                                 ALU.max, ALU.mult).then_inc(k_max, 1)
                if m % HK == 0:
                    split_lo(J_K + m // HK + 1)
            dve.wait_ge(k_expd, KF)
            dve.wait_ge(pads_set, 1)
            V_.tensor_tensor(k_rs[:, :], k_sum[:, :, 0], k_sum[:, :, 1], ALU.add)
            V_.drain()
            V_.reciprocal(k_rs[:, :], k_rs[:, :])
            V_.drain()
            for c in range(2):
                wait_unit(("ctx", c))
                for p in range(HK):
                    m = c * HK + p
                    for a in range(0, 128, DH):
                        V_.tensor_scalar(ctx_s[a:a + DH, m, a:a + DH],
                                         PS(("ctx", c))[a:a + DH, 0, p * 128 + a:p * 128 + a + DH],
                                         k_rs[a:a + DH, m:m + 1], None, ALU.mult)
                V_.drain().then_inc(free[slot(("ctx", c))], 1)
                V_.drain().then_inc(ctx_done, 1)

            def attention_lo(n):
                lo_of(("at", n), halved(at_lo, n), moving(("at", n)), halved(at_hi, n))

            heads = lambda ap: ap.rearrange("p (h d) -> p h d", d=DH)
            wide = lambda ap: ap.unsqueeze(2).to_broadcast([T, HH, DH])
            for m in range(2 * NT + QLAG):
                if m - QLAG == NT:
                    for n in range(HK):
                        attention_lo(n)
                if m < 2 * NT:
                    key, b = ("q", m), m % 2
                    wait_unit(key)
                    V_.reduce_max(q_m[:, :], heads(PS(key)[0:T, 0, :]), axis=AX.X)
                    V_.drain()
                    if m >= 2:
                        dve.wait_ge(ready[slot(("qt", m - 2))], use(("qt", m - 2)) + 1)
                    V_.tensor_tensor(heads(q_s[:, b, :]), heads(PS(key)[0:T, 0, :]), wide(q_m[:, :]),
                                     ALU.subtract).then_inc(q_sub, 1)
                    V_.drain().then_inc(free[slot(key)], 1)
                    dve.wait_ge(q_expd, m + 1)
                    V_.reduce_sum(q_sum[:, :], heads(q_s[:, b, :]), axis=AX.X)
                    V_.drain()
                    V_.reciprocal(q_sum[:, :], q_sum[:, :])
                    V_.drain()
                    V_.scalar_tensor_tensor(heads(q_s[:, b, :]), heads(q_s[:, b, :]), float(DH) ** -0.5,
                                            wide(q_sum[:, :]), ALU.mult, ALU.mult).then_inc(q_done, 1)
                    if m in Q_SPLITS:
                        split_lo(Q_SPLITS[m][0], quarters=Q_SPLITS[m][1:])
            for n in range(HK, KF):
                attention_lo(n)
            for h in range(2):
                split_lo(J_O + h + 1)
            dve.wait_ge(b0_loaded, 16)
            for h in range(2):
                split_lo(J_L0 + 2 * h + 1)
                for i in range(NT):
                    key = ("g0", h, i)
                    lo_of(key, g_lo[:, i, :], PS(key)[0:T, 0, :], g_hi[:, i, :])
                split_lo(J_L0 + 2 * h + 2)
                for n in range(h * HK, (h + 1) * HK):
                    key = ("h", n)
                    wait_unit(key)
                    V_.tensor_scalar(moving(key), moving(key), b0_s[:, n:n + 1], 0.0, ALU.add,
                                     ALU.max).then_inc(h_relu, 1)
                    lo_of(key, halved(t2_lo, n), moving(key), halved(t2_hi, n))
            for h in range(2):
                split_lo(J_L1 + 2 * h + 1)
                for i in range(NT):
                    key = ("g1", h, i)
                    lo_of(key, g_lo[:, i, :], PS(key)[0:T, 0, :], g_hi[:, i, :])
                split_lo(J_L1 + 2 * h + 2)
                dve.wait_ge(x1_loaded, 32)
                cols_h = slice(h * HW, (h + 1) * HW)
                for i in range(NT):
                    key = ("x1", h, i)
                    wait_unit(key)
                    V_.tensor_tensor(x1[:, i, cols_h], x1[:, i, cols_h], PS(key)[0:T, 0, :], ALU.add)
                    V_.drain().then_inc(free[slot(key)], 1)
                    V_.tensor_tensor(x1[:, i, cols_h], x1[:, i, cols_h], part[:, i, cols_h], ALU.add)
                    if h == 1:
                        if i == 0:
                            dve.wait_ge(rwh_done, 1)
                            V_.tensor_tensor(rw_lo[:, :, :], rw_raw[:, :, :], as32(rw_hi[:, :, :]),
                                             ALU.subtract).then_inc(rwl_done, 1)
                        V_.drain()
                        moments(x1[:, i, :])
                        norm_scale(NT + i + 1)
            for i in range(NT):
                for f in range(2):
                    transposed_lo(("x2t", i, f), t2_lo, t2_hi, i, f)

            ex = lambda ap: ap.unsqueeze(2).to_broadcast([T, NT, X])
            ti = lambda ap: ap.unsqueeze(1).to_broadcast([T, NT, X])
            dve.wait_ge(route_set, 1)
            wait_unit(("lt",))
            V_.tensor_copy(lg[:, :, :], PS(("lt",))[0:T, 0, 0:NT * XP].rearrange("p (i e) -> p i e", e=XP))
            V_.drain().then_inc(free[slot(("lt",))], 1)
            V_.reduce_max(r1[:, :], lg[:, :, 0:X], axis=AX.X)
            V_.drain()
            V_.tensor_tensor(pr[:, :, :], lg[:, :, 0:X], ex(r1[:, :]), ALU.subtract).then_inc(lg_sub, 1)
            dve.wait_ge(lg_expd, 2)
            V_.reduce_sum(r1[:, :], pr[:, :, :], axis=AX.X)
            V_.tensor_scalar(wts[:, 2, :], wts[:, 2, :], 1.0, None, ALU.add)
            V_.drain()
            V_.reciprocal(r1[:, :], r1[:, :])
            V_.reciprocal(wts[:, 2, :], wts[:, 2, :])
            V_.drain()
            V_.tensor_tensor(pr[:, :, :], pr[:, :, :], ex(r1[:, :]), ALU.mult)
            V_.drain()
            for c, mask in enumerate((m1, m2)):
                V_.reduce_max(wts[:, c, :], pr[:, :, :], axis=AX.X)
                V_.drain()
                V_.tensor_tensor(eq[:, :, :], pr[:, :, :], ex(wts[:, c, :]), ALU.is_equal)
                V_.drain()
                V_.tensor_tensor(eq[:, :, :], eq[:, :, :], ti(iota_m8[:, :]), ALU.mult)
                V_.drain()
                V_.tensor_reduce(r1[:, :], eq[:, :, :], axis=AX.X, op=ALU.min)
                V_.drain()
                V_.tensor_tensor(mask[:, :, :], ti(iota_m8[:, :]), ex(r1[:, :]), ALU.is_equal)
                V_.drain()
                if c == 0:
                    V_.scalar_tensor_tensor(pr[:, :, :], m1[:, :, :], -2.0, pr[:, :, :], ALU.mult, ALU.add)
                    V_.drain()
            V_.tensor_tensor(mm[:, :, :], m1[:, :, :], m2[:, :, :], ALU.add).then_inc(m_ready, 1)

            def shared_lo(h):
                for n in range(h * HK, (h + 1) * HK):
                    key = ("up", n)
                    wait_unit(key)
                    dve.wait_ge(gate_done, n + 1)
                    V_.tensor_tensor(moving(key), moving(key), gate_s[:, n % HK, :].rearrange("p (c n) -> p c n", c=2),
                                     ALU.mult).then_inc(prod_done, 1)
                    lo_of(key, halved(s_lo, n), moving(key), halved(s_hi, n))

            split_lo(J_GU + 1)
            wait_unit(("pos",))
            pos = PS(("pos",))[0:T, 0, 0:NT * X].rearrange("p (i e) -> p i e", e=X)
            cnt = PS(("pos",))[0:T, 1, 0:X]
            V_.tensor_scalar(nb[:, :], cnt, 0.0, None, ALU.is_gt)
            V_.drain()
            for c in range(B, N, B):
                V_.scalar_tensor_tensor(nb[:, :], cnt, float(c), nb[:, :], ALU.is_gt, ALU.add)
                V_.drain()
            V_.tensor_copy(cum[:, 0, :], nb[:, :])
            V_.drain()
            for c, step in enumerate((1, 2, 4)):
                V_.tensor_copy(cum[:, (c + 1) % 2, 0:step], cum[:, c % 2, 0:step])
                V_.tensor_tensor(cum[:, (c + 1) % 2, step:X], cum[:, c % 2, step:X], cum[:, c % 2, 0:X - step], ALU.add)
                V_.drain()
            V_.tensor_tensor(start[:, :], cum[:, 1, :], nb[:, :], ALU.subtract)
            V_.drain()
            V_.tensor_scalar(start[:, :], start[:, :], float(B), None, ALU.mult)
            V_.drain()
            V_.tensor_tensor(pr[:, :, :], pos, ti(start[:, :]), ALU.add)
            V_.drain().then_inc(free[slot(("pos",))], 1)
            for c, mask in enumerate((m1, m2)):
                V_.tensor_tensor(eq[:, :, :], pr[:, :, :], mask[:, :, :], ALU.mult)
                V_.drain()
                V_.reduce_sum(r1[:, :], eq[:, :, :], axis=AX.X)
                V_.drain()
                V_.tensor_copy(slots[:, c, :], r1[:, :])
                V_.drain()
            V_.drain().then_inc(slots_ready, 1)
            be = [T, MAXB, X]
            V_.tensor_tensor(ind[:, :, :], cum[:, 1, :].unsqueeze(1).to_broadcast(be),
                             iota_j[:, :].unsqueeze(2).to_broadcast(be), ALU.is_le)
            V_.drain()
            V_.reduce_sum(je[:, :], ind[:, :, :], axis=AX.X)
            V_.drain()
            V_.tensor_scalar(table[0:1, 0, :], je[0:1, :], float(X - 1), None, ALU.min)
            V_.tensor_copy(table[0:1, 1, 0:1], cum[0:1, 1, X - 1:X])
            V_.drain().then_inc(table_ready, 1)
            for h in range(2):
                if h:
                    split_lo(J_GU + 2 * h + 1)
                split_lo(J_GU + 2 * h + 2)
                shared_lo(h)
            for s in range(BC):
                for f in range(2):
                    transposed_lo(("xe", s, f), xe_lo, xe_hi, s, f, 128)
            def shared_out(h, i, base=None):
                key = ("sd", h, i)
                wait_unit(key, base)
                part_h = x1[:, i, h * HW:(h + 1) * HW]
                V_.scalar_tensor_tensor(part_h, PS(key)[0:T, 0, :], wts[:, 2, i:i + 1], part_h, ALU.mult, ALU.add)
                V_.drain().then_inc(free[slot(key)], 1)

            split_lo(J_X)
            for i in range(NT):
                shared_out(0, i)
            blocks = dve.value_load(table[0:1, 1, 0:1], min_val=1, max_val=MAXB - 1)
            with dve.Fori(0, blocks) as j:
                for h in range(2):
                    split_lo(J_X + h + 1, j)
                    for n in range(h * HK // 2, (h + 1) * HK // 2):
                        key = ("he", n)
                        two = lambda t: t[:, 2 * n:2 * n + 2, :].rearrange("p k n -> p (k n)")
                        lo_of(key, two(he_lo), PS(key)[:, 0, :], two(he_hi), j)
                for s, f in XEP[:-1]:
                    transposed_lo(("xe+", s, f), xe_lo, xe_hi, s, f, 128, j)
                split_lo(J_X + 3, j)
                transposed_lo(("xe+",) + XEP[-1], xe_lo, xe_hi, *XEP[-1], 128, j)
                split_lo(J_X + 4, j)
            for i in range(NT):
                for c in range(2):
                    dve.wait_ge(yg_loaded[i][c], 16)
                    V_.scalar_tensor_tensor(x1[:, i, :], y_g[c][:, i, :], wts[:, c, i:i + 1], x1[:, i, :],
                                            ALU.mult, ALU.add)
                    V_.drain()
                V_.drain().then_inc(out_ready, 1)
                shared_out(1, i, blocks)
                V_.drain().then_inc(out_ready, 1)

        @block.tensor
        def _(pe):
            mat = nc.tensor.matmul

            def claim(key, base=None):
                if base is not None:
                    pe.wait_ge(free[slot(key)], base * BU + use(key))
                elif use(key) > 0:
                    pe.wait_ge(free[slot(key)], use(key))

            def passes(out_ap, left, right, start, stop):
                (lh, ll), (rh, rl) = left, right
                mat(out_ap, lh, rh, start=start, stop=False)
                mat(out_ap, lh, rl, start=False, stop=False)
                return mat(out_ap, ll, rh, start=False, stop=stop)

            def weights(job, base=None):
                pe.wait_ge(lo_done, 2 * (job + 1) if base is None else base * 8 + 2 * (job + 1))
                return w_hi[job % 2], w_lo[job % 2]

            def by_tokens(key, out_ap, operand, job, tokens, start=True, stop=True, arrives=None):
                wh, wl = w_hi[job % 2], w_lo[job % 2]
                for k in range(KF):
                    if arrives and arrives(k) is not None:
                        pe.wait_ge(lo_out, arrives(k))
                    last = passes(out_ap, [t[:, k, tokens] for t in operand], (wh[:, k, :], wl[:, k, :]),
                                  start and k == 0, stop and k == KF - 1)
                return last

            def by_features(key, n, operand, job, stop=True):
                wh, wl = w_hi[job % 2], w_lo[job % 2]
                for c in range(2):
                    for k in range(KF):
                        w_cols = slice(n % HK * 128, (n % HK + 1) * 128)
                        last = passes(PS(key)[:, c, 0:TH], (wh[:, k, w_cols], wl[:, k, w_cols]),
                                      [t[:, k, c * TH:(c + 1) * TH] for t in operand], k == 0, stop and k == KF - 1)
                return last

            tile = lambda i: slice(i * T, (i + 1) * T)
            XT, T2, AT, SH, HE = (xt_hi, xt_lo), (t2_hi, t2_lo), (at_hi, at_lo), (s_hi, s_lo), (he_hi, he_lo)

            pe.wait_ge(iotas_set, 1)
            acc = [ps[n // 2][0:T, n % 2, 0:TH] for n in range(NT)]

            def transposes(key, source, count, width, ins, base=None):
                claim(key, base)
                for a in range(count):
                    last = nc.tensor.transpose(PB(key)[:, a * width:(a + 1) * width], source(a), ident[0:ins, 0:ins])
                last.then_inc(ready[slot(key)], 1)

            def values(h, i):
                key = ("v", h, i)
                weights(J_V + h)
                pe.wait_ge(lo_out, nth[("xt", i, 1)])
                claim(key)
                by_tokens(key, PB(key)[0:T, :], XT, J_V + h, tile(i)).then_inc(ready[slot(key)], 1)

            def count(g, lo, hi):
                with pe.Fori(lo, hi) as c:
                    for b in range(OHB):
                        pe.wait_ge(oh_ready, c * OHB + (g * GB + b + 1))
                        pe.wait_ge(oha_ready, c * OHB + (g * GB + b + 1))
                        for e in range(b * CB, (b + 1) * CB):
                            for n in range(NT):
                                last = mat(acc[n], src_oh[:, e, n * T:(n + 1) * T], dst_oh[:, e, :], start=False, stop=False)
                        last.then_inc(oh_free, 1)

            for g in range(NG):
                pe.wait_ge(cnt_free, g + 1)
                for n in range(NT):
                    mat(acc[n], zero16[:, 0:T], zero16[:, :], start=True, stop=False)
                count(g, 0, GB // 2 // OHB)
                if g:
                    values(0, g - 1)
                count(g, GB // 2 // OHB, GB // OHB)
                for n in range(NT):
                    last = mat(acc[n], zero16[:, 0:T], zero16[:, :], start=False, stop=True)
                last.then_inc(cnt_ready, 1)
                if g == 0:
                    pe.wait_ge(consts_set, 1)
                pe.wait_ge(ln_done, g + 1)
                for f in range(2):
                    transposes(("xt", g, f), lambda a: x_s[:, g, (f * HK + a) * 128:(f * HK + a + 1) * 128], HK, T, T)
                if g:
                    values(1, g - 1)
            values(0, NT - 1)
            pe.wait_ge(cnt_free, NG + 1)
            pe.wait_ge(c_ready, 1)
            key = ("deg",)
            for c in range(2):
                for n in range(NT):
                    last = mat(PS(key)[0:T, c, 0:TH], ones[0:T, 0:T], c_f[:, n, c, :], start=n == 0, stop=n == NT - 1)
            last.then_inc(ready[slot(key)], 1)
            values(1, NT - 1)
            for n in range(SIDE):
                pe.wait_ge(free[RING + n], len(side[n::SIDE]))
            def context(c):
                pe.wait_ge(kt_done, 2 * (c + 1) * HK)
                if c == 0:
                    pe.wait_ge(v_loaded, 16)
                key = ("ctx", c)
                claim(key)
                for p in range(HK):
                    m = c * HK + p
                    for i in range(NT):
                        last = mat(PS(key)[:, 0, p * 128:(p + 1) * 128], k_tok[:, i, m * 128:(m + 1) * 128],
                                   v_tok[:, i, m * 128:(m + 1) * 128], start=i == 0, stop=i == NT - 1)
                last.then_inc(ready[slot(key)], 1)

            def keys_back(m):
                key = ("kt", m)
                pe.wait_ge(k_expd, m + 1)
                claim(key)
                for i in range(NT):
                    last = nc.tensor.transpose(PS(key)[0:T, i // 4, i % 4 * 128:(i % 4 + 1) * 128],
                                               k_exp[:, m % 2, tile(i)], ident[:, :])
                last.then_inc(ready[slot(key)], 1)

            for m in range(KF + KLAG):
                if m < KF:
                    if m % HK == 0:
                        weights(J_K + m // HK)
                    key = ("k", m)
                    claim(key)
                    by_features(key, m, XT, J_K + m // HK).then_inc(ready[slot(key)], 1)
                if m == KF + KLAG - 1:
                    context(0)
                if m >= KLAG:
                    keys_back(m - KLAG)
            context(1)

            def attend(n):
                key = ("at", n)
                pe.wait_ge(ctx_done, 2)
                pe.wait_ge(qt_done, NT if n < HK else 2 * NT)
                claim(key)
                for c in range(2):
                    last = mat(PS(key)[:, c, 0:TH], ctx_s[:, n, :], q_t[:, n % HK, c * TH:(c + 1) * TH], start=True, stop=True)
                last.then_inc(ready[slot(key)], 1)

            for m in range(2 * NT + QLAG):
                if m - QLAG == NT:
                    for n in range(HK):
                        attend(n)
                if m < 2 * NT:
                    if m % NT == 0:
                        weights(J_Q + m // NT)
                    key = ("q", m)
                    claim(key)
                    by_tokens(key, PS(key)[0:T, 0, :], XT, J_Q + m // NT, tile(m % NT)).then_inc(ready[slot(key)], 1)
                if m >= QLAG:
                    n = m - QLAG
                    pe.wait_ge(q_done, n + 1)
                    transposes(("qt", n), lambda a: q_s[:, n % 2, a * 128:(a + 1) * 128], HK, T, T)
            for n in range(HK, KF):
                attend(n)
            for h in range(2):
                weights(J_O + h)
                for i in range(NT):
                    key = ("o", h, i)
                    claim(key)
                    by_tokens(key, PS(key)[0:T, 0, :], AT, J_O + h, tile(i), stop=False,
                              arrives=(lambda k: nth[("at", k)]) if h == i == 0 else None)
                    if h == i == 0:
                        pe.wait_ge(bias_loaded, 32)
                    for a in range(2):
                        last = mat(PS(key)[0:T, 0, :], ones[0:1, 0:T], bias_o[:, a, h * HW:(h + 1) * HW],
                                   start=False, stop=a == 1)
                    last.then_inc(ready[slot(key)], 1)
            pe.wait_ge(cl_done, NT)
            for h in range(2):
                job = J_L0 + 2 * h
                weights(job)
                for i in range(NT):
                    key = ("g0", h, i)
                    claim(key)
                    by_tokens(key, PS(key)[0:T, 0, :], XT, job, tile(i)).then_inc(ready[slot(key)], 1)
                weights(job + 1)
                for n in range(h * HK, (h + 1) * HK):
                    key = ("h", n)
                    claim(key)
                    by_features(key, n, XT, job + 1, stop=False)
                    pe.wait_ge(lo_out, nth[("g0", h, NT - 1)])
                    g_cols = slice(n % HK * 128, (n % HK + 1) * 128)
                    for c in range(2):
                        for i in range(NT):
                            last = passes(PS(key)[:, c, 0:TH], (g_hi[:, i, g_cols], g_lo[:, i, g_cols]),
                                          [t[:, i, c * TH:(c + 1) * TH] for t in (c_hi, c_lo)], False, i == NT - 1)
                    last.then_inc(ready[slot(key)], 1)
            for h in range(2):
                job = J_L1 + 2 * h
                weights(job)
                for i in range(NT):
                    key = ("g1", h, i)
                    claim(key)
                    by_tokens(key, PS(key)[0:T, 0, :], T2, job, tile(i),
                              arrives=(lambda k: nth[("h", k)]) if h == i == 0 else None).then_inc(ready[slot(key)], 1)
                weights(job + 1)
                for i in range(NT):
                    key = ("x1", h, i)
                    claim(key)
                    by_tokens(key, PS(key)[0:T, 0, :], T2, job + 1, tile(i), stop=False)
                    pe.wait_ge(lo_out, nth[("g1", h, NT - 1)])
                    for s in range(NT):
                        last = passes(PS(key)[0:T, 0, :], [t[:, s, tile(i)] for t in (c_hi, c_lo)],
                                      (g_hi[:, s, :], g_lo[:, s, :]), False, s == NT - 1)
                    last.then_inc(ready[slot(key)], 1)
            for i in range(NT):
                pe.wait_ge(ln_done, NT + i + 1)
                for f in range(2):
                    transposes(("x2t", i, f), lambda a: part[:, i, (f * HK + a) * 128:(f * HK + a + 1) * 128], HK, T, T)
            pe.wait_ge(lo_out, nth[("x2t", NT - 1, 1)])
            pe.wait_ge(rwl_done, 1)
            pe.wait_ge(route_set, 1)
            key = ("lg",)
            claim(key)
            for c in range(2):
                for k in range(KF):
                    last = passes(PS(key)[0:XP, c, 0:TH], (rw_hi[:, k, :], rw_lo[:, k, :]),
                                  [t[:, k, c * TH:(c + 1) * TH] for t in T2], k == 0, k == KF - 1)
            last.then_inc(ready[slot(key)], 1)
            key = ("lt",)
            pe.wait_ge(lgT_done, 1)
            claim(key)
            for i in range(NT):
                last = nc.tensor.transpose(PS(key)[0:T, 0, i * XP:(i + 1) * XP], lgT[:, tile(i)], ident[0:XP, 0:XP])
            last.then_inc(ready[slot(key)], 1)
            for h in range(2):
                for a, name in enumerate(("gt", "up")):
                    job = J_GU + 2 * h + a
                    weights(job)
                    for n in range(h * HK, (h + 1) * HK):
                        key = (name, n)
                        claim(key)
                        by_features(key, n, T2, job).then_inc(ready[slot(key)], 1)
                    if h == 0 and a == 0:
                        key = ("pos",)
                        pe.wait_ge(m_ready, 1)
                        claim(key)
                        for i in range(NT):
                            out_ap = PS(key)[0:T, 0, i * X:(i + 1) * X]
                            for b in range(i):
                                mat(out_ap, ones[0:T, 0:T], mm[:, b, :], start=b == 0, stop=False)
                            mat(out_ap, tri[:, 0:T], mm[:, i, :], start=i == 0, stop=True)
                        for i in range(NT):
                            last = mat(PS(key)[0:T, 1, 0:X], ones[0:T, 0:T], mm[:, i, :], start=i == 0, stop=i == NT - 1)
                        last.then_inc(ready[slot(key)], 1)
            pe.wait_ge(xg_loaded, 16 * BC)
            for s in range(BC):
                for f in range(2):
                    transposes(("xe", s, f), lambda a: xg[:, s, (f * HK + a) * 128:(f * HK + a + 1) * 128], HK, 128, 128)
            pe.wait_ge(lo_out, nth[("up", KF - 1)])

            def shared_out(h, job, base=None):
                weights(job, base)
                for i in range(NT):
                    key = ("sd", h, i)
                    claim(key, base)
                    by_tokens(key, PS(key)[0:T, 0, :], SH, job, tile(i)).then_inc(ready[slot(key)], 1)

            shared_out(0, J_D)
            pe.wait_ge(table_ready, 1)
            blocks = pe.value_load(table[0:1, 1, 0:1], min_val=1, max_val=MAXB - 1)
            with pe.Fori(0, blocks) as j:
                pe.wait_ge(lo_out, j * BR + R0)
                for h in range(2):
                    wh, wl = weights(J_X + h, j)
                    for n in range(h * HK // 2, (h + 1) * HK // 2):
                        key = ("he", n)
                        claim(key, j)
                        for a in range(2):
                            w_cols = slice((2 * n + a) % HK * 128, ((2 * n + a) % HK + 1) * 128)
                            for k in range(KF):
                                last = passes(PS(key)[:, 0, a * B:(a + 1) * B], (wh[:, k, w_cols], wl[:, k, w_cols]),
                                              (xe_hi[:, k, :], xe_lo[:, k, :]), k == 0, k == KF - 1)
                        last.then_inc(ready[slot(key)], 1)
                pe.wait_ge(xg_loaded, j * (16 * BC) + 2 * 16 * BC)

                def rows_across(s, f):
                    transposes(("xe+", s, f), lambda a: xg[:, s, (f * HK + a) * 128:(f * HK + a + 1) * 128],
                               HK, 128, 128, j)

                for s, f in XEP[:-1]:
                    rows_across(s, f)
                for h in range(2):
                    weights(J_X + 2 + h, j)
                    for s in range(BC):
                        key = ("y", h, s)
                        claim(key, j)
                        by_tokens(key, PS(key)[:, 0, :], HE, J_X + h, slice(s * 128, (s + 1) * 128),
                                  arrives=(lambda k: j * BR + nth[("he", k // 2)] if k % 2 == 0 and k >= KF // 2 else None)
                                  if h == s == 0 else None).then_inc(ready[slot(key)], 1)
                        if h == s == 0:
                            rows_across(*XEP[-1])
            shared_out(1, J_X, blocks)


_INS = ['x', 'src', 'dst', 'L0_gnn_W_self0', 'L0_gnn_W_neigh0', 'L0_gnn_b0', 'L0_gnn_W_self1', 'L0_gnn_W_neigh1',
        'L0_gnn_b1', 'L0_mix_Wq', 'L0_mix_Wk', 'L0_mix_Wv', 'L0_mix_Wo', 'L0_mix_bo', 'L0_ffn_router_w', 'L0_ffn_w1',
        'L0_ffn_w2', 'L0_ffn_shared_gate_up', 'L0_ffn_shared_down', 'L0_ffn_shared_gate_w']


def kernel(**inputs):
    import numpy as _np
    import concourse.bacc as _bacc
    from concourse import mybir as _mybir
    from concourse.bass_utils import run_bass_kernel_spmd as _run

    nc = _bacc.Bacc("TRN2", target_bir_lowering=False, num_devices=1)
    arrays, args = {}, []
    for name in _INS:
        a = _np.ascontiguousarray(inputs[name])
        arrays[f"in_{name}"] = a
        args.append(nc.dram_tensor(f"in_{name}", a.shape, _mybir.dt.from_np(a.dtype), kind="ExternalInput").ap())
    shape = arrays["in_x"].shape
    args.append(nc.dram_tensor("out_0", shape, _mybir.dt.float32, kind="ExternalOutput").ap())
    gps_layer(nc, *args)
    r = _run(nc, [arrays], core_ids=[0])
    return r.results[0]["out_0"]
```

```python
import concourse.bass as bass
from concourse import mybir
from contextlib import ExitStack


def gps_layer(nc, x, src, dst, w_self0, w_neigh0, b0, w_self1, w_neigh1, b1,
              wq, wk, wv, wo, bo, router_w, w1, w2, gate_up, down, gate_w, out):
    f32, f32r, f16 = mybir.dt.float32, mybir.dt.float32r, mybir.dt.float16
    i32, u32 = mybir.dt.int32, mybir.dt.uint32
    ALU, ACT, AX = mybir.AluOpType, mybir.ActivationFunctionType, mybir.AxisListType

    N, D = x.shape
    E = src.shape[0]
    T = 125
    NT = N // T
    KF = D // 128
    HW = D // 2
    HK = KF // 2
    TP = 628
    TH = TP // 2
    LASTH = N - TH
    DH = 64
    HH = HW // DH
    X = router_w.shape[1]
    XP = X + 2
    B = 256
    BC = B // 128
    MAXB = X + (2 * N - X) // B + 1
    SLOTC = MAXB * BC
    CP = 125
    NC = E // CP
    NG = 5
    CG = NC // NG
    CB = 4
    GB = CG // CB
    OHB = 2
    GP = GB // OHB
    CD = (3, 2, 2, 2)
    DIGIT = 4096.0
    EPS = 1e-5
    assert CG * CP < DIGIT and CG % (CB * OHB) == 0 and NT * T == N and NC * CP == E

    halves = lambda m: [m[:, h * HW:(h + 1) * HW].rearrange("(k p) n -> p k n", p=128) for h in range(2)]
    gate, up = gate_up[:, 0:D], gate_up[:, D:2 * D]
    V, K, Q, O = halves(wv), halves(wk), halves(wq), halves(wo)
    N0, S0, N1, S1 = halves(w_neigh0), halves(w_self0), halves(w_neigh1), halves(w_self1)
    G, U, Dn = halves(gate), halves(up), halves(down)
    STREAM = [V[0], V[1], K[0], K[1], Q[0], Q[1], O[0], O[1], N0[0], S0[0], N0[1], S0[1],
              N1[0], S1[0], N1[1], S1[1], G[0], U[0], G[1], U[1], Dn[0]]
    (J_V, J_K, J_Q, J_O, J_L0, J_L1, J_GU, J_D, J_X) = (0, 2, 4, 6, 8, 12, 16, 20, 21)
    w1v = w1.rearrange("e (k p) n -> p e k n", p=128)
    w2v = w2.rearrange("e (k p) n -> p e k n", p=128)

    RING = 4
    units = [("deg",)]
    KLAG = QLAG = 2
    Q_SPLITS = {0: (5, 0), 1: (5, 1), NT + 1: (6, 0), NT + 3: (6, 1)}
    for m in range(KF + KLAG):
        units += ([("k", m)] if m < KF else []) + ([("ctx", 0)] if m == KF + KLAG - 1 else [])
        units += [("kt", m - KLAG)] if m >= KLAG else []
    units += [("ctx", 1)]
    for m in range(2 * NT + QLAG):
        if m < 2 * NT:
            units += [("q", m)]
        if m >= QLAG:
            units += [("qt", m - QLAG)]
        if m == 2 * NT - 1:
            units += [("at", n) for n in range(HK)]
    units += [("at", n) for n in range(HK, KF)]
    units += [("o", h, i) for h in range(2) for i in range(NT)]
    for h in range(2):
        units += [("g0", h, i) for i in range(NT)] + [("h", h * HK + n) for n in range(HK)]
    for h in range(2):
        units += [("g1", h, i) for i in range(NT)]
        for i in range(NT):
            units += [("x1", h, i)] + ([("x2t", i - 1)] if h and i else [])
    GEARLY = 2
    units += [("gt", 0), ("lg",), ("gt", 1), ("x2t", NT - 1), ("lt",)]
    for h in range(2):
        units += [("gt", h * HK + n) for n in range(HK) if h or n >= GEARLY] + ([("pos",)] if h == 0 else [])
        units += [("up", h * HK + n) for n in range(HK)]
    units += [("xe", s, f) for s in range(BC) for f in range(2)]
    units += [("sd", 0, i) for i in range(NT)]
    U0 = len(units)
    place = {key: n for n, key in enumerate(units)}
    ROWS = [(s, f) for s in range(BC) for f in range(2)]
    FIRST, LATER = ROWS[:2], ROWS[2:]
    block_units = ([("he", n) for n in range(KF // 2)] + [("xe+", s, f) for s, f in FIRST]
                   + [("y", 0, 0)] + [("xe+", s, f) for s, f in LATER]
                   + [("y", h, s) for h in range(2) for s in range(BC)][1:])
    BU = len(block_units) // RING
    assert BU * RING == len(block_units)
    place.update({key: U0 + n for n, key in enumerate(block_units)})
    place.update({("sd", 1, i): U0 + i for i in range(NT)})
    SIDE = 3
    side = []
    for g in range(NG):
        side += ([("v", 0, g - 1)] if g else []) + [("xt", g, 0), ("xt", g, 1)] + ([("v", 1, g - 1)] if g else [])
    side += [("v", 0, NT - 1), ("v", 1, NT - 1)]
    side_place = {key: n for n, key in enumerate(side)}
    assert NG == NT
    slot = lambda key: RING + side_place[key] % SIDE if key in side_place else place[key] % RING
    use = lambda key: side_place[key] // SIDE if key in side_place else place[key] // RING

    last_unit = {J_V: ("v", 0, NT - 1), J_V + 1: ("v", 1, NT - 1), J_GU: ("gt", HK - 1), J_GU + 1: ("up", HK - 1),
                 J_GU + 2: ("gt", KF - 1), J_GU + 3: ("up", KF - 1), J_D: ("sd", 0, NT - 1)}
    for h in range(2):
        last_unit.update({J_K + h: ("k", (h + 1) * HK - 1), J_Q + h: ("q", (h + 1) * NT - 1), J_O + h: ("o", h, NT - 1),
                          J_L0 + 2 * h: ("g0", h, NT - 1), J_L0 + 2 * h + 1: ("h", (h + 1) * HK - 1),
                          J_L1 + 2 * h: ("g1", h, NT - 1), J_L1 + 2 * h + 1: ("x1", h, NT - 1),
                          J_X + h: ("he", (h + 1) * HK // 2 - 1), J_X + 2 + h: ("y", h, BC - 1)})
    assert J_D == J_X - 1 and place[last_unit[J_D]] == U0 - 1

    v_d = nc.dram_tensor("values", (N, D), f32, kind="Internal").ap()
    attn_d = nc.dram_tensor("attn_out", (N, D), f32, kind="Internal").ap()
    xn2_d = nc.dram_tensor("xn2_rows", (N, D), f32, kind="Internal").ap()
    slot_d = nc.dram_tensor("token_of_slot", (SLOTC * 128, 1), u32, kind="Internal").ap()
    y_d = nc.dram_tensor("expert_rows", (SLOTC * 128, D), f32, kind="Internal").ap()
    y_c = y_d.rearrange("(c p) f -> p c f", p=128)
    y_block = lambda c, f0, f1: y_c[:, bass.ds(c, 1), f0:f1].rearrange("p c f -> p (c f)")
    tok = lambda a: a.rearrange("(i p) f -> p i f", p=T)
    tile = lambda i: slice(i * T, (i + 1) * T)

    ctx = ExitStack()
    with ctx:
        sem = lambda name: ctx.enter_context(nc.semaphore(name))
        BASE = (nc.sbuf_base + 31) // 32 * 32

        def at(name, offset, shape, dt):
            return nc.alloc_sbuf_tensor_at(name, shape, dt, offset=BASE + offset)

        HALF = KF * HW * 4
        o_w = 0
        o_raw = o_w + 4 * HALF
        R1 = o_raw + HALF
        R1S = 2 * NT * D * 4
        R2 = R1 + R1S
        PAIR = 2 * KF * TP * 4
        RC = R2 + PAIR
        CS = (NT * TP * 4 + 31) // 32 * 32
        VS = (NT * TH * 4 + 31) // 32 * 32
        RCS = 2 * CS
        RG = RC + RCS
        RGS = NT * D * 4
        o_misc = RG + RGS

        w_hi = [at(f"w_hi{b}", o_w + 2 * b * HALF, [128, KF, HW], f32r) for b in range(2)]
        w_lo = [at(f"w_lo{b}", o_w + (2 * b + 1) * HALF, [128, KF, HW], f32r) for b in range(2)]
        w_raw = [at(f"w_raw{b}", o_raw + b * HALF // 2, [128, HK, HW], f32) for b in range(2)]
        xt_hi = at("xt_hi", R1, [128, KF, TP], f32r)
        xt_lo = at("xt_lo", R1 + PAIR // 2, [128, KF, TP], f32r)
        x1 = at("x1", R1, [T, NT, D], f32)
        part = at("part", R1 + R1S // 2, [T, NT, D], f32)
        gate_s = at("gate_s", R1 + R1S // 2, [128, HK, TP], f32)
        zrow = at("zrow", R1 + R1S // 2, [128, D], f32)
        xg = at("xg", R1 + R1S // 2 + HK * TP * 4, [128, BC, D], f32)
        TAIL = R2 + RGS
        k_tok = at("k_tok", R2, [T, NT, D], f32)
        at_lo = at("at_lo", R2, [128, KF, TP], f32r)
        k_exp = at("k_exp", TAIL, [128, 2, TP], f32)
        q_s = at("q_s", TAIL, [T, 2, HW], f32)
        o_s = at("o_s", TAIL, [T, 2, HW], f32)
        ctx_s = at("ctx_s", TAIL + 2 * TP * 4, [128, KF, 128], f32)
        q_t = [at("q_first", R2 + HK * TP * 4, [128, HK, TP], f32),
               at("q_second", TAIL + 2 * TP * 4 + KF * 512, [128, HK, TP], f32)]
        bias_o = at("bias_o", TAIL + 2 * TP * 4 + KF * 512, [T, 2, D], f32)
        t2_hi = at("t2_hi", R2, [128, KF, TP], f32r)
        t2_lo = at("t2_lo", R2 + PAIR // 2, [128, KF, TP], f32r)
        XE = KF * B * 4
        xe_hi = at("xe_hi", R2, [128, KF, B], f32r)
        xe_lo = at("xe_lo", R2 + XE, [128, KF, B], f32r)
        he_hi = at("he_hi", R2 + 2 * XE, [128, KF, B], f32r)
        he_lo = at("he_lo", R2 + 3 * XE, [128, KF, B], f32r)
        y_s = at("y_s", R2 + 4 * XE, [128, 2, HW], f32)
        c_hi = at("c_hi", RC, [T, NT, TP], f32r)
        c_lo = at("c_lo", RC + RCS // 2, [T, NT, TP], f32r)
        v_tok = at("v_tok", RG, [T, NT, D], f32)
        at_hi = at("at_hi", RG, [128, KF, TP], f32r)
        g_hi = at("g_hi", RG, [T, NT, HW], f32r)
        g_lo = at("g_lo", RG + RGS // 2, [T, NT, HW], f32r)
        y_g = [at("y_first", R1 + R1S // 2, [T, NT, D], f32), at("y_second", R2, [T, NT, D], f32)]
        assert R1S // 2 <= 4 * XE
        s_hi = at("s_hi", RC, [128, KF, TP], f32r)
        s_lo = at("s_lo", RC + PAIR // 2, [128, KF, TP], f32r)
        o_route = RC + PAIR
        x_s = at("x_s", RC, [T, NT, D], f32)
        c_f = at("c_f", R2, [T, NT, 2, TH], f32)
        cv = at("cv", R2 + CS, [T, NT, TH], f32)
        ch = at("ch", R2 + CS + VS, [T, NT, TH], i32)
        deg_s = at("deg_s", R2 + CS + 2 * VS, [T, 2, TH], f32)
        off = [RG]

        def following(name, shape, dt, size):
            t = at(name, off[0], shape, dt)
            off[0] += (shape[1] * (shape[2] if len(shape) > 2 else 1) * size + 31) // 32 * 32
            return t

        src_oh = following("src_oh", [CP, OHB * CB, N + 1], f16, 2)
        dst_oh = following("dst_oh", [CP, OHB * CB, TH], f16, 2)
        iota_n = following("iota_n", [CP, N + 1], f16, 2)
        zero16 = following("zero16", [CP, TH], f16, 2)
        assert off[0] <= RG + RGS
        off = [R2 + CS + 2 * VS + (2 * TH * 4 + 31) // 32 * 32]
        src_i = following("src_i", [CP, NC], i32, 4)
        dst_i = following("dst_i", [CP, NC], i32, 4)
        edge = following("edge", [CP, NC, 4], f32, 4)
        away = following("away", [CP, CB - min(CD), TH], f16, 2)
        v_s = following("v_s", [T, 2, HW], f32, 4)
        assert off[0] <= R2 + PAIR
        off = [o_misc]
        ident = following("ident", [128, 128], f32, 4)
        ones = following("ones", [128, 128], f32, 4)
        b0_s = following("b0_s", [128, KF], f32, 4)
        st = following("st", [T, 2, 6], f32, 4)
        mv = following("mv", [T, 2], f32, 4)
        ve = following("ve", [T, 1], f32, 4)
        sq = following("sq", [T, 1], f32, 4)
        rs = following("rs", [T, 1], f32, 4)
        rt = following("rt", [T, 1], f32, 4)
        nm = following("nm", [T, 1], f32, 4)
        k_m2 = following("k_m2", [128, 2, 2], f32, 4)
        k_nm = following("k_nm", [128, 2], f32, 4)
        k_sum = following("k_sum", [128, KF, 2], f32, 4)
        k_rs = following("k_rs", [128, KF], f32, 4)
        q_m = following("q_m", [T, HH], f32, 4)
        q_sum = following("q_sum", [T, HH], f32, 4)
        rw_raw = following("rw_raw", [128, KF, XP], f32, 4)
        rw_hi = following("rw_hi", [128, KF, XP], f32r, 4)
        rw_lo = following("rw_lo", [128, KF, XP], f32r, 4)
        tri = following("tri", [T, 128], f16, 2)
        ones16 = following("ones16", [T, T + 3], f16, 2)
        tok_id = following("tok_id", [T, NT], u32, 4)
        slots = following("slots", [T, 2, NT], u32, 4)
        wts = following("wts", [T, 3, NT], f32, 4)
        cols = following("cols", [128, SLOTC], u32, 4)
        idx2 = following("idx2", [128, BC], u32, 4)
        table = following("table", [1, 2, MAXB], i32, 4)
        assert BASE + off[0] <= nc.sbuf_usable_end, (BASE + off[0], nc.sbuf_usable_end)
        off = [o_route]
        lgT = following("lgT", [XP, TP], f32, 4)
        lg = following("lg", [T, NT, XP], f32, 4)
        pr = following("pr", [T, NT, X], f32, 4)
        eq = following("eq", [T, NT, X], f32, 4)
        m1 = following("m1", [T, NT, X], f32, 4)
        m2 = following("m2", [T, NT, X], f32, 4)
        mm = following("mm", [T, NT, X], f16, 2)
        r1 = following("r1", [T, NT], f32, 4)
        iota_m8 = following("iota_m8", [T, X], f32, 4)
        start = following("start", [T, X], f32, 4)
        iota_j = following("iota_j", [T, MAXB], f32, 4)
        nb = following("nb", [T, X], f32, 4)
        cum = following("cum", [T, 2, X], f32, 4)
        ind = following("ind", [T, MAXB, X], f32, 4)
        je = following("je", [T, MAXB], f32, 4)
        zslot = following("zslot", [128, SLOTC], u32, 4)
        assert off[0] <= RG + RGS, (off[0], RG + RGS)

        ps = [ctx.enter_context(nc.psum_tensor(f"ps{n}", [128, 2, 512], f32)) for n in range(RING)]
        PS = lambda key: ps[slot(key)]
        side_banks = [ps[2][:, 1, :], ps[3][:, 0, :], ps[3][:, 1, :]]
        PB = lambda key: side_banks[slot(key) - RING] if slot(key) >= RING else ps[slot(key)][:, 0, :]
        as32 = lambda ap: ap.bitcast(f32)
        moving = lambda key: PS(key)[:, :, 0:TH]

        def halved(t, k, p=128):
            return t[0:p, k, :].rearrange("p (c n) -> p c n", c=2)

        ready = [sem(f"psum_ready{n}") for n in range(RING + SIDE)]
        free = [sem(f"psum_free{n}") for n in range(RING + SIDE)]
        w_loaded = [sem(f"w_loaded{n}") for n in range(2)]
        hi_done = sem("hi_done")
        lo_done = sem("lo_done")
        x_loaded, idx_loaded, b0_loaded = sem("x_loaded"), sem("idx_loaded"), sem("b0_loaded")
        edges_set = sem("edges_set")
        iotas_set, consts_set = sem("iotas_set"), sem("consts_set")
        oh_ready, oha_ready, oh_free = sem("oh_ready"), sem("oha_ready"), sem("oh_free")
        cnt_ready, cnt_free, cv_ready, cv_free = sem("cnt_ready"), sem("cnt_free"), sem("cv_ready"), sem("cv_free")
        ln_var, ln_sqrt, ln_scale, ln_done = sem("ln_var"), sem("ln_sqrt"), sem("ln_scale"), sem("ln_done")
        c_ready = sem("c_ready")
        ch_done = sem("ch_done")
        cl_done = sem("cl_done")
        hi_out = sem("hi_out")
        lo_out = sem("lo_out")
        pads_set = sem("pads_set")
        v_copied, v_loaded = sem("v_copied"), sem("v_loaded")
        v_stored = [sem(f"v_stored{n}") for n in range(2)]
        k_max, k_expd, kt_done, ctx_done = sem("k_max"), sem("k_expd"), sem("kt_done"), sem("ctx_done")
        q_sub, q_expd, q_done, qt_done = sem("q_sub"), sem("q_expd"), sem("q_done"), sem("qt_done")
        bias_loaded = sem("bias_loaded")
        o_copied = sem("o_copied")
        o_stored = [sem(f"o_stored{n}") for n in range(2)]
        h_relu = sem("h_relu")
        x1_loaded = sem("x1_loaded")
        rw_loaded, rwh_done, rwl_done = sem("rw_loaded"), sem("rwh_done"), sem("rwl_done")
        lgT_done, lg_sub, lg_expd, m_ready = sem("lgT_done"), sem("lg_sub"), sem("lg_expd"), sem("m_ready")
        t2_padded, route_set, slots_ready, table_ready = sem("t2_padded"), sem("route_set"), sem("slots_ready"), sem("table_ready")
        zero_stored, ids_stored, cols_loaded, xn2_stored = sem("zero_stored"), sem("ids_stored"), sem("cols_loaded"), sem("xn2_stored")
        idx_ready, xg_loaded = sem("idx_ready"), sem("xg_loaded")
        gate_done, prod_done = sem("gate_done"), sem("prod_done")
        silu_done = sem("silu_done")
        y_copied = sem("y_copied")
        y_stored = [sem(f"y_stored{n}") for n in range(2)]
        zrow_set, gather_clear = sem("zrow_set"), sem("gather_clear")
        y_rows = sem("y_rows")
        yg_loaded = [[sem(f"yg_loaded{i}_{c}") for c in range(2)] for i in range(NT)]
        out_ready, out_stored = sem("out_ready"), sem("out_stored")

        results = ([("xt", i, f) for i in range(NT) for f in range(2)] + [("at", n) for n in range(KF)])
        for h in range(2):
            results += [("g0", h, i) for i in range(NT)] + [("h", h * HK + n) for n in range(HK)]
        for h in range(2):
            results += [("g1", h, i) for i in range(NT)]
        results += [("x2t", i, f) for i in range(NT) for f in range(2)]
        results += [("up", n) for n in range(KF)] + [("xe", s, f) for s in range(BC) for f in range(2)]
        nth = {key: n + 1 for n, key in enumerate(results)}
        R0 = len(results)
        block_results = [("he", n) for n in range(KF // 2)] + [("xe+", s, f) for s in range(BC) for f in range(2)]
        nth.update({key: R0 + n + 1 for n, key in enumerate(block_results)})
        BR = len(block_results)

        block = ctx.enter_context(nc.Block())

        @block.sync
        def _(sp):
            sp.dma_start(src_i[:, :], src.rearrange("(p c) -> p c", c=NC)).then_inc(idx_loaded, 16)
            sp.dma_start(dst_i[:, :], dst.rearrange("(p c) -> p c", c=NC)).then_inc(idx_loaded, 16)
            sp.dma_start(x_s[:, :, :], tok(x)).then_inc(x_loaded, 16)
            sp.dma_start(b0_s[:, :], b0.rearrange("(k p) -> p k", p=128),
                         allow_slow_non_contiguous=True).then_inc(b0_loaded, 16)

            def load(job, view):
                for s in range(2):
                    if job > 0:
                        sp.wait_ge(lo_done, 2 * (job - 1) + s + 1)
                    sp.dma_start(w_raw[s][:, :, :], view[:, s * HK:(s + 1) * HK, :]).then_inc(w_loaded[s], 16)

            for job in range(J_X):
                if job == J_O + 1:
                    sp.wait_ge(ready[slot(("at", KF - 1))], use(("at", KF - 1)) + 1)
                    sp.dma_start(bias_o[:, 0, :], bo.partition_broadcast(T)).then_inc(bias_loaded, 16)
                    sp.dma_start(bias_o[:, 1, :], b1.partition_broadcast(T)).then_inc(bias_loaded, 16)
                if job == J_L1 + 2:
                    sp.wait_ge(ready[slot(("h", KF - 1))], use(("h", KF - 1)) + 1)
                    sp.wait_ge(o_stored[0], 16 * NT)
                    sp.wait_ge(o_stored[1], 16 * NT)
                    sp.dma_start(x1[:, :, :], tok(x)).then_inc(x1_loaded, 16)
                    sp.dma_start(part[:, :, :], tok(attn_d)).then_inc(x1_loaded, 16)
                    sp.dma_start(rw_raw[:, :, 0:X], router_w.rearrange("(k p) e -> p k e", p=128)).then_inc(rw_loaded, 16)
                    sp.dma_start(rw_raw[:, :, X:X + 1], gate_w.rearrange("(k p) e -> p k e", p=128),
                                 allow_slow_non_contiguous=True).then_inc(rw_loaded, 16)
                if job == J_GU + 1:
                    sp.wait_ge(ln_done, 2 * NT)
                    sp.dma_start(tok(xn2_d), part[:, :, :]).then_inc(xn2_stored, 16)
                if job == J_Q:
                    sp.wait_ge(cnt_ready, NG)
                    for n in range(2):
                        sp.wait_ge(v_stored[n], 16 * NT)
                    sp.dma_start(v_tok[:, :, :], tok(v_d)).then_inc(v_loaded, 16)
                load(job, STREAM[job])

            sp.wait_ge(table_ready, 1)
            blocks = sp.value_load(table[0:1, 1, 0:1], min_val=1, max_val=MAXB - 1)
            with sp.Fori(0, blocks) as j:
                expert = sp.value_load(table[0:1, 0, bass.ds(j, 1)], min_val=0, max_val=X - 1)
                for i in range(4):
                    for s in range(2):
                        sp.wait_ge(lo_done, j * 8 + (2 * (J_X + i - 1) + s + 1))
                        view = (w1v if i < 2 else w2v)[:, bass.ds(expert, 1), s * HK:(s + 1) * HK,
                                                       (i % 2) * HW:(i % 2 + 1) * HW]
                        sp.dma_start(w_raw[s][:, :, :], view.rearrange("p e k n -> p (e k) n")).then_inc(w_loaded[s], 16)
            for s in range(2):
                sp.wait_ge(lo_done, blocks * 8 + (2 * (J_X - 1) + s + 1))
                sp.dma_start(w_raw[s][:, :, :], Dn[1][:, s * HK:(s + 1) * HK, :]).then_inc(w_loaded[s], 16)
            for i in range(NT):
                for h in range(2):
                    sp.wait_ge(out_ready, 2 * i + h + 1)
                    cols_h = slice(h * HW, (h + 1) * HW)
                    sp.dma_start(out[i * T:(i + 1) * T, cols_h], x1[:, i, cols_h]).then_inc(out_stored, 16)
            sp.wait_ge(out_stored, 16 * 2 * NT)

        @block.gpsimd
        def _(pool):
            nc.gpsimd.iota(iota_n[:, :], [[1, N + 1]], base=0, channel_multiplier=0,
                           allow_small_or_imprecise_dtypes=True)
            nc.gpsimd.memset(zero16[:, :], 0.0)
            nc.gpsimd.drain().then_inc(iotas_set, 1)
            nc.gpsimd.drain().then_inc(oh_free, OHB)
            nc.gpsimd.drain().then_inc(cnt_free, 1)
            nc.gpsimd.memset(c_f[:, :, :, :], 0.0)
            nc.gpsimd.memset(ones[:, :], 1.0)
            nc.gpsimd.memset(ident[:, :], 0.0)
            nc.gpsimd.memset(tri[:, :], 1.0)
            nc.gpsimd.memset(ones16[:, :], 1.0)
            nc.gpsimd.memset(rw_raw[:, :, :], 0.0)
            nc.gpsimd.drain()
            nc.gpsimd.affine_select(out=ident[:, :], in_=ident[:, :], compare_op=ALU.not_equal, fill=1.0, base=0,
                                    pattern=[[-1, 128]], channel_multiplier=1)
            nc.gpsimd.affine_select(out=tri[:, :], in_=tri[:, :], compare_op=ALU.is_gt, fill=0.0, base=0,
                                    pattern=[[1, 128]], channel_multiplier=-1)
            nc.gpsimd.iota(tok_id[:, :], [[T, NT]], base=0, channel_multiplier=1)
            nc.gpsimd.memset(as32(xt_hi[:, :, N:TP]), 0.0)
            nc.gpsimd.memset(as32(xt_lo[:, :, N:TP]), 0.0)
            nc.gpsimd.drain().then_inc(consts_set, 1)
            pool.wait_ge(cl_done, NT)
            for n in range(2):
                pool.wait_ge(v_stored[n], 16 * NT)
            nc.gpsimd.memset(q_t[1][:, :, N:TP], 0.0)
            nc.gpsimd.memset(ctx_s[:, :, :], 0.0)
            nc.gpsimd.drain().then_inc(pads_set, 1)
            pool.wait_ge(ready[slot(("ctx", 1))], use(("ctx", 1)) + 1)
            nc.gpsimd.memset(q_t[0][:, :, N:TP], 0.0)
            nc.gpsimd.drain().then_inc(pads_set, 1)
            pool.wait_ge(ready[slot(("x1", 0, 0))], use(("x1", 0, 0)) + 1)
            nc.gpsimd.memset(as32(t2_hi[:, :, N:TP]), 0.0)
            nc.gpsimd.memset(as32(t2_lo[:, :, N:TP]), 0.0)
            nc.gpsimd.drain().then_inc(t2_padded, 1)
            pool.wait_ge(ready[slot(("x1", 1, NT - 1))], use(("x1", 1, NT - 1)) + 1)
            nc.gpsimd.iota(iota_m8[:, :], [[1, X]], base=-X, channel_multiplier=0, allow_small_or_imprecise_dtypes=True)
            nc.gpsimd.iota(iota_j[:, :], [[1, MAXB]], base=0, channel_multiplier=0, allow_small_or_imprecise_dtypes=True)
            nc.gpsimd.memset(zslot[:, :], 0)
            nc.gpsimd.drain().then_inc(route_set, 1)
            pool.wait_ge(route_set, 1)
            pool.dma_start(slot_d.rearrange("(p c) o -> p (c o)", p=128), zslot[:, :]).then_inc(zero_stored, 16)
            pool.wait_ge(zero_stored, 16)
            pool.wait_ge(slots_ready, 1)
            for c in range(2):
                for i in range(NT):
                    nc.gpsimd.indirect_dma_start(
                        out=slot_d, out_offset=bass.IndirectOffsetOnAxis(ap=slots[:, c, i:i + 1], axis=0),
                        in_=tok_id[:, i:i + 1], in_offset=None).then_inc(ids_stored, 16)
            pool.wait_ge(ids_stored, 16 * 2 * NT)
            pool.dma_start(cols[:, :], slot_d.rearrange("(c p) o -> p (c o)", p=128),
                           allow_slow_non_contiguous=True).then_inc(cols_loaded, 16)
            pool.wait_ge(cols_loaded, 16)
            pool.wait_ge(xn2_stored, 16)
            pool.wait_ge(table_ready, 1)
            blocks = pool.value_load(table[0:1, 1, 0:1], min_val=1, max_val=MAXB - 1)
            nc.gpsimd.tensor_copy(idx2[:, :], cols[:, 0:BC]).then_inc(idx_ready, 1)
            pool.wait_ge(idx_ready, 1)
            for s in range(BC):
                nc.gpsimd.indirect_dma_start(
                    out=xg[:, s, :], out_offset=None, in_=xn2_d,
                    in_offset=bass.IndirectOffsetOnAxis(ap=idx2[:, s:s + 1], axis=0)).then_inc(xg_loaded, 16)
            pool.wait_ge(ready[slot(("up", KF - 1))], use(("up", KF - 1)) + 1)
            pool.wait_ge(prod_done, KF)
            nc.gpsimd.memset(zrow[:, :], 0.0)
            nc.gpsimd.drain().then_inc(zrow_set, 1)
            with pool.Fori(0, blocks) as j:
                pool.wait_ge(lo_out, j * BR + R0)
                nc.gpsimd.tensor_copy(idx2[:, :], cols[:, bass.ds(j * BC + BC, BC)])
                nc.gpsimd.drain()
                for s in range(BC):
                    nc.gpsimd.indirect_dma_start(
                        out=xg[:, s, :], out_offset=None, in_=xn2_d,
                        in_offset=bass.IndirectOffsetOnAxis(ap=idx2[:, s:s + 1], axis=0)).then_inc(xg_loaded, 16)
            pool.wait_ge(xg_loaded, blocks * (16 * BC) + 16 * BC)
            pool.wait_ge(lo_out, blocks * BR + R0)
            for s in range(BC):
                pool.wait_ge(y_stored[s], blocks * 32 + 16)
            pool.sem_inc(gather_clear, 1)
            pool.wait_ge(gather_clear, 1)
            pool.wait_ge(y_rows, 16 * BC * MAXB)
            for i in range(NT):
                for c in range(2):
                    nc.gpsimd.indirect_dma_start(
                        out=y_g[c][:, i, :], out_offset=None, in_=y_d,
                        in_offset=bass.IndirectOffsetOnAxis(ap=slots[:, c, i:i + 1], axis=0)).then_inc(yg_loaded[i][c], 16)

        @block.scalar
        def _(act):
            copy = nc.scalar.copy

            def wait_unit(key, base=None):
                act.wait_ge(ready[slot(key)], use(key) + 1 if base is None else base * BU + (use(key) + 1))

            def split_hi(job, base=None, quarters=(0, 1)):
                b = job % 2
                shift = (lambda v, per: v) if base is None else (lambda v, per: base * per + v)
                if job >= 2:
                    wait_unit(last_unit[job - 2], base)
                for s in quarters:
                    act.wait_ge(w_loaded[s], shift(16 * (job + 1), 64))
                    copy(w_hi[b][:, s * HK:(s + 1) * HK, :], w_raw[s][:, :, :]).then_inc(hi_done, 1)

            def destinations(g, p):
                for b in range(OHB):
                    n = g * GB + p * OHB + b
                    act.wait_ge(oh_free, n + 1)
                    for c in range(CD[p], CB):
                        nc.scalar.activation(away[:, c - CD[p], :], iota_n[:, 0:TH], ACT.Abs,
                                             bias=edge[:, n * CB + c, 1:2], scale=-1.0)
                    nc.scalar.drain()
                    for c in range(CD[p], CB):
                        nc.scalar.activation(dst_oh[:, b * CB + c, :], away[:, c - CD[p], :], ACT.Relu,
                                             bias=edge[:, n * CB + c, 2:3], scale=edge[:, n * CB + c, 3:4])
                    nc.scalar.drain().then_inc(oha_ready, 1)

            act.wait_ge(iotas_set, 1)
            act.wait_ge(edges_set, 1)

            def hi_of(key, out_ap, in_ap, base=None):
                wait_unit(key, base)
                copy(out_ap, in_ap).then_inc(hi_out, 1)

            def normal_hi(i):
                for f in range(2):
                    hi_of(("xt", i, f), xt_hi[:, f * HK:(f + 1) * HK, i * T:(i + 1) * T],
                          PB(("xt", i, f))[:, 0:HK * T].rearrange("p (k t) -> p k t", t=T))

            def values(h, i):
                key = ("v", h, i)
                n = [k for k in side if k[0] == "v"].index(key)
                wait_unit(key)
                if i:
                    act.wait_ge(v_stored[h], 16 * i)
                copy(v_s[:, h, :], PB(key)[0:T, :]).then_inc(v_copied, 1)
                act.wait_ge(v_copied, n + 1)
                nc.scalar.drain().then_inc(free[slot(key)], 1)
                act.dma_start(v_d[i * T:(i + 1) * T, h * HW:(h + 1) * HW], v_s[:, h, :]).then_inc(v_stored[h], 16)

            for g in range(NG):
                destinations(g, 0)
                if g:
                    normal_hi(g - 1)
                if g > 1:
                    values(1, g - 2)
                destinations(g, 1)
                if g < 2:
                    split_hi(g, quarters=(0,))
                destinations(g, 2)
                act.wait_ge(ln_var, g + 1)
                nc.scalar.activation(sq[:, :], ve[:, :], ACT.Sqrt).then_inc(ln_sqrt, 1)
                if g:
                    values(0, g - 1)
                destinations(g, 3)
                act.wait_ge(ln_scale, g + 1)
                nc.scalar.activation(x_s[:, g, :], x_s[:, g, :], ACT.Identity, bias=nm[:, :],
                                     scale=rs[:, :]).then_inc(ln_done, 1)
                if g < 2:
                    split_hi(g, quarters=(1,))
                if g:
                    act.wait_ge(cv_free, g)
                act.wait_ge(cnt_ready, g + 1)
                for n in range(0, NT, 2):
                    w = min(2, NT - n)
                    copy(cv[:, n:n + w, :], ps[n // 2][0:T, 0:w, 0:TH])
                nc.scalar.drain().then_inc(cnt_free, 1)
                nc.scalar.drain().then_inc(cv_ready, 1)
            normal_hi(NT - 1)
            values(1, NT - 2)
            values(0, NT - 1)
            split_hi(J_K)
            values(1, NT - 1)
            act.wait_ge(c_ready, 2)
            for n in range(NT):
                copy(c_hi[:, n, :], c_f[:, n, :, :].rearrange("p a b -> p (a b)")).then_inc(ch_done, 1)

            def keys_back(m):
                key = ("kt", m)
                wait_unit(key)
                copy(k_tok[:, 0:4, m * 128:(m + 1) * 128],
                     PS(key)[0:T, 0, :].rearrange("p (i n) -> p i n", i=4)).then_inc(kt_done, 1)
                copy(k_tok[:, 4, m * 128:(m + 1) * 128], PS(key)[0:T, 1, 0:128]).then_inc(kt_done, 1)
                act.wait_ge(kt_done, 2 * (m + 1))
                nc.scalar.drain().then_inc(free[slot(key)], 1)

            act.wait_ge(cl_done, NT)
            for m in range(KF + KLAG):
                if m < KF:
                    wait_unit(("k", m))
                    act.wait_ge(k_max, m + 1)
                    if m >= 2:
                        act.wait_ge(ready[slot(("kt", m - 2))], use(("kt", m - 2)) + 1)
                    nc.scalar.activation(k_exp[:, m % 2, 0:TH], PS(("k", m))[:, 0, 0:TH], ACT.Exp,
                                         bias=k_nm[:, m % 2:m % 2 + 1], accum_out=k_sum[:, m, 0:1])
                    nc.scalar.activation(k_exp[:, m % 2, TH:N], PS(("k", m))[:, 1, 0:LASTH], ACT.Exp,
                                         bias=k_nm[:, m % 2:m % 2 + 1], accum_out=k_sum[:, m, 1:2])
                    nc.scalar.drain().then_inc(k_expd, 1)
                    nc.scalar.drain().then_inc(free[slot(("k", m))], 1)
                if m >= KLAG:
                    keys_back(m - KLAG)
                if m % HK == 0 and m < KF:
                    split_hi(J_K + m // HK + 1)

            def attention_hi(n):
                hi_of(("at", n), halved(at_hi, n), moving(("at", n)))

            for m in range(2 * NT + QLAG):
                if m < 2 * NT:
                    act.wait_ge(q_sub, m + 1)
                    nc.scalar.activation(q_s[:, m % 2, :], q_s[:, m % 2, :], ACT.Exp).then_inc(q_expd, 1)
                if m >= QLAG:
                    n = m - QLAG
                    if n == 0:
                        act.wait_ge(pads_set, 2)
                    wait_unit(("qt", n))
                    copy(q_t[n // NT][:, :, n % NT * T:(n % NT + 1) * T],
                         PS(("qt", n))[:, 0, 0:HK * T].rearrange("p (k t) -> p k t", t=T)).then_inc(qt_done, 1)
                    act.wait_ge(qt_done, n + 1)
                    nc.scalar.drain().then_inc(free[slot(("qt", n))], 1)
                if m in Q_SPLITS:
                    split_hi(Q_SPLITS[m][0], quarters=Q_SPLITS[m][1:])
                if m == 2 * NT - 1:
                    for n in range(HK):
                        attention_hi(n)
            for n in range(HK, KF):
                attention_hi(n)
            for h in range(2):
                split_hi(J_O + h + 1)
                for i in range(NT):
                    n = h * NT + i
                    act.wait_ge(o_copied, n + 1)
                    act.dma_start(attn_d[i * T:(i + 1) * T, h * HW:(h + 1) * HW],
                                  o_s[:, n % 2, :]).then_inc(o_stored[n % 2], 16)
            for h in range(2):
                split_hi(J_L0 + 2 * h + 1)
                for i in range(NT):
                    hi_of(("g0", h, i), g_hi[:, i, :], PS(("g0", h, i))[0:T, 0, :])
                split_hi(J_L0 + 2 * h + 2)
                for n in range(HK):
                    if h == 0 and n == 0:
                        act.wait_ge(o_stored[0], 16 * NT)
                        act.wait_ge(o_stored[1], 16 * NT)
                    act.wait_ge(h_relu, h * HK + n + 1)
                    hi_of(("h", h * HK + n), halved(t2_hi, h * HK + n), moving(("h", h * HK + n)))
            for h in range(2):
                split_hi(J_L1 + 2 * h + 1)
                for i in range(NT):
                    hi_of(("g1", h, i), g_hi[:, i, :], PS(("g1", h, i))[0:T, 0, :])
                split_hi(J_L1 + 2 * h + 2)
            act.wait_ge(rw_loaded, 32)
            copy(rw_hi[:, :, :], rw_raw[:, :, :]).then_inc(rwh_done, 1)

            def normal_hi_2(i):
                wait_unit(("x2t", i))
                for f in range(2):
                    copy(t2_hi[:, f * HK:(f + 1) * HK, i * T:(i + 1) * T],
                         PS(("x2t", i))[:, f, 0:HK * T].rearrange("p (k t) -> p k t", t=T)).then_inc(hi_out, 1)

            for i in range(NT):
                if i:
                    normal_hi_2(i - 1)
                act.wait_ge(ln_var, NT + i + 1)
                nc.scalar.activation(sq[:, :], ve[:, :], ACT.Sqrt).then_inc(ln_sqrt, 1)
                act.wait_ge(ln_scale, NT + i + 1)
                nc.scalar.activation(part[:, i, :], x1[:, i, :], ACT.Identity, bias=nm[:, :],
                                     scale=rs[:, :]).then_inc(ln_done, 1)
            normal_hi_2(NT - 1)
            wait_unit(("lg",))
            copy(lgT[:, :].rearrange("p (c n) -> p c n", c=2), PS(("lg",))[0:XP, :, 0:TH]).then_inc(lgT_done, 1)
            act.wait_ge(lgT_done, 1)
            nc.scalar.drain().then_inc(free[slot(("lg",))], 1)

            def gate(n):
                key = ("gt", n)
                wait_unit(key)
                if n == 0:
                    act.wait_ge(xn2_stored, 16)
                if n >= HK:
                    act.wait_ge(prod_done, n - HK + 1)
                nc.scalar.activation(gate_s[:, n % HK, :].rearrange("p (c n) -> p c n", c=2), moving(key),
                                     ACT.Silu).then_inc(gate_done, 1)
                act.wait_ge(gate_done, n + 1)
                nc.scalar.drain().then_inc(free[slot(key)], 1)

            gate(0)
            act.wait_ge(lg_sub, 1)
            nc.scalar.activation(pr[:, :, :], pr[:, :, :], ACT.Exp).then_inc(lg_expd, 1)
            nc.scalar.activation(wts[:, 2, :], lg[:, :, X], ACT.Exp, scale=-1.0).then_inc(lg_expd, 1)
            for h in range(2):
                split_hi(J_GU + 2 * h + 1)
                for n in range(h * HK or 1, (h + 1) * HK):
                    gate(n)
                split_hi(J_GU + 2 * h + 2)
                for n in range(HK):
                    act.wait_ge(prod_done, h * HK + n + 1)
                    hi_of(("up", h * HK + n), halved(s_hi, h * HK + n), moving(("up", h * HK + n)))
            for s in range(BC):
                for f in range(2):
                    hi_of(("xe", s, f), xe_hi[:, f * HK:(f + 1) * HK, s * 128:(s + 1) * 128],
                          PS(("xe", s, f))[:, 0, :].rearrange("p (k t) -> p k t", t=128))
            split_hi(J_X)
            act.wait_ge(table_ready, 1)
            blocks = act.value_load(table[0:1, 1, 0:1], min_val=1, max_val=MAXB - 1)
            act.wait_ge(zrow_set, 1)
            for s in range(BC):
                act.dma_start(y_c[:, (MAXB - 1) * BC + s, 0:HW], zrow[:, 0:HW]).then_inc(y_stored[s], 16)
                act.dma_start(y_c[:, (MAXB - 1) * BC + s, HW:D], zrow[:, HW:D]).then_inc(y_rows, 16)
            with act.Fori(blocks, MAXB - 1) as j:
                for s in range(BC):
                    act.dma_start(y_block(j * BC + s, 0, D), zrow[:, :]).then_inc(y_rows, 16)
            with act.Fori(0, blocks) as j:
                for h in range(2):
                    split_hi(J_X + h + 1, j)
                    for n in range(h * HK // 2, (h + 1) * HK // 2):
                        key = ("he", n)
                        wait_unit(key, j)
                        nc.scalar.activation(PS(key)[:, 0, :], PS(key)[:, 0, :], ACT.Silu).then_inc(silu_done, 1)
                        act.wait_ge(silu_done, j * (KF // 2) + (n + 1))
                        copy(he_hi[:, 2 * n:2 * n + 2, :].rearrange("p k n -> p (k n)"), PS(key)[:, 0, :]).then_inc(hi_out, 1)

                def rows_hi(s, f):
                    hi_of(("xe+", s, f), xe_hi[:, f * HK:(f + 1) * HK, s * 128:(s + 1) * 128],
                          PS(("xe+", s, f))[:, 0, :].rearrange("p (k t) -> p k t", t=128), j)

                for s, f in FIRST:
                    rows_hi(s, f)
                for h in range(2):
                    split_hi(J_X + 2 + h + 1, j)
                    for s in range(BC):
                        key = ("y", h, s)
                        wait_unit(key, j)
                        act.wait_ge(y_stored[s], j * 32 + (16 * h + 16))
                        copy(y_s[:, s, :], PS(key)[:, 0, :]).then_inc(y_copied, 1)
                        act.wait_ge(y_copied, j * (2 * BC) + (h * BC + s + 1))
                        act.sem_inc(free[slot(key)], 1)
                        act.dma_start(y_block(j * BC + s, h * HW, (h + 1) * HW), y_s[:, s, :]).then_inc(y_stored[s], 16)
                        if h == s == 0:
                            for rows in LATER:
                                rows_hi(*rows)
                act.sem_inc(y_rows, 16 * BC)

        @block.vector
        def _(dve):
            V_ = nc.vector

            def split_lo(job, base=None, quarters=(0, 1)):
                b = job % 2
                for s in quarters:
                    done = 2 * job + s + 1
                    dve.wait_ge(hi_done, done if base is None else base * 8 + done)
                    k = slice(s * HK, (s + 1) * HK)
                    V_.tensor_tensor(w_lo[b][:, k, :], w_raw[s][:, :, :], as32(w_hi[b][:, k, :]),
                                     ALU.subtract).then_inc(lo_done, 1)

            def lo_of(key, out_ap, in_ap, hi_ap, base=None):
                dve.wait_ge(hi_out, nth[key] if base is None else base * BR + nth[key])
                V_.tensor_tensor(out_ap, in_ap, as32(hi_ap), ALU.subtract).then_inc(lo_out, 1)
                dve.wait_ge(lo_out, nth[key] if base is None else base * BR + nth[key])
                dve.sem_inc(free[slot(key)], 1)

            def wait_unit(key, base=None):
                dve.wait_ge(ready[slot(key)], use(key) + 1 if base is None else base * BU + (use(key) + 1))

            def moments(in_ap):
                for c in range(2):
                    V_.bn_stats(st[:, c, :], in_ap[:, c * HW:(c + 1) * HW])
                V_.drain()
                V_.bn_aggr(mv[:, :], st[:, :, :])
                V_.drain()
                V_.tensor_scalar(ve[:, :], mv[:, 1:2], EPS, None, ALU.add).then_inc(ln_var, 1)

            def norm_scale(n):
                dve.wait_ge(ln_sqrt, n)
                V_.reciprocal(rs[:, :], sq[:, :])
                V_.drain()
                V_.tensor_tensor(rt[:, :], rs[:, :], rs[:, :], ALU.mult)
                V_.drain()
                V_.tensor_tensor(rt[:, :], rt[:, :], ve[:, :], ALU.mult)
                V_.drain()
                V_.tensor_scalar(rt[:, :], rt[:, :], -0.5, 1.5, ALU.mult, ALU.add)
                V_.drain()
                V_.tensor_tensor(rs[:, :], rs[:, :], rt[:, :], ALU.mult)
                V_.drain()
                V_.scalar_tensor_tensor(nm[:, :], mv[:, 0:1], -1.0, rs[:, :], ALU.mult, ALU.mult)
                V_.drain().then_inc(ln_scale, 1)

            dve.wait_ge(idx_loaded, 32)
            V_.tensor_copy(edge[:, :, 0], src_i[:, :])
            V_.tensor_copy(edge[:, :, 1], dst_i[:, :])
            V_.drain()
            V_.tensor_scalar(edge[:, :, 3], edge[:, :, 1], float(TH), None, ALU.is_ge)
            V_.drain()
            V_.tensor_scalar(edge[:, :, 2], edge[:, :, 3], DIGIT - 1.0, 1.0, ALU.mult, ALU.add)
            V_.scalar_tensor_tensor(edge[:, :, 1], edge[:, :, 3], -float(TH), edge[:, :, 1], ALU.mult, ALU.add)
            V_.drain()
            V_.tensor_scalar(edge[:, :, 3], edge[:, :, 2], -1.0, None, ALU.mult)
            V_.drain().then_inc(edges_set, 1)

            def one_hots(g, p):
                for b in range(OHB):
                    n = g * GB + p * OHB + b
                    dve.wait_ge(oh_free, n + 1)
                    for c in range(CB):
                        e = n * CB + c
                        V_.tensor_scalar(src_oh[:, b * CB + c, :], iota_n[:, :], edge[:, e, 0:1], None, ALU.is_equal)
                        if c < CD[p]:
                            V_.tensor_scalar(dst_oh[:, b * CB + c, :], iota_n[:, 0:TH], edge[:, e, 1:2], edge[:, e, 2:3],
                                             ALU.is_equal, ALU.mult)
                    V_.drain().then_inc(oh_ready, 1)

            def unpack():
                V_.tensor_scalar(ch[:, :, :], cv[:, :, :], 1.0 / DIGIT, -(DIGIT / 2 - 1) / DIGIT, ALU.mult, ALU.add)
                V_.drain()
                V_.scalar_tensor_tensor(cv[:, :, :], ch[:, :, :], -DIGIT, cv[:, :, :], ALU.mult, ALU.add)
                V_.tensor_tensor(c_f[:, :, 1, :], c_f[:, :, 1, :], ch[:, :, :], ALU.add)
                V_.drain()
                V_.tensor_tensor(c_f[:, :, 0, :], c_f[:, :, 0, :], cv[:, :, :], ALU.add)
                V_.drain().then_inc(cv_free, 1)

            dve.wait_ge(iotas_set, 1)

            def transposed_lo(key, lo, hi, i, f, w=T, base=None):
                at_ = (slice(None), slice(f * HK, (f + 1) * HK), slice(i * w, (i + 1) * w))
                lo_of(key, lo[at_], PB(key)[:, 0:HK * w].rearrange("p (k t) -> p k t", t=w), hi[at_], base)

            for g in range(NG):
                one_hots(g, 0)
                if g:
                    for f in range(2):
                        transposed_lo(("xt", g - 1, f), xt_lo, xt_hi, g - 1, f)
                one_hots(g, 1)
                if g:
                    dve.wait_ge(cv_ready, g)
                    unpack()
                else:
                    dve.wait_ge(consts_set, 1)
                    dve.wait_ge(x_loaded, 16)
                    moments(x_s[:, g, :])
                one_hots(g, 2)
                if g < 2:
                    split_lo(g, quarters=(0,))
                norm_scale(g + 1)
                one_hots(g, 3)
                if g < 2:
                    split_lo(g, quarters=(1,))
                if g < NG - 1:
                    moments(x_s[:, g + 1, :])
            for f in range(2):
                transposed_lo(("xt", NT - 1, f), xt_lo, xt_hi, NT - 1, f)
            dve.wait_ge(cv_ready, NG)
            unpack()
            V_.drain().then_inc(c_ready, 1)
            split_lo(J_K)
            wait_unit(("deg",))
            V_.tensor_scalar(deg_s[:, :, :], PS(("deg",))[0:T, :, 0:TH], 1.0, None, ALU.max)
            V_.drain().then_inc(free[slot(("deg",))], 1)
            V_.reciprocal(deg_s[:, :, :], deg_s[:, :, :])
            V_.drain()
            for n in range(NT):
                V_.tensor_tensor(c_f[:, n, :, :], c_f[:, n, :, :], deg_s[:, :, :], ALU.mult)
            V_.drain().then_inc(c_ready, 1)
            for n in range(NT):
                dve.wait_ge(ch_done, n + 1)
                V_.tensor_tensor(c_lo[:, n, :], c_f[:, n, :, :].rearrange("p a b -> p (a b)"), as32(c_hi[:, n, :]),
                                 ALU.subtract).then_inc(cl_done, 1)

            for m in range(KF):
                key, b = ("k", m), m % 2
                wait_unit(key)
                V_.reduce_max(k_m2[:, b, 0:1], PS(key)[:, 0, 0:TH], axis=AX.X)
                V_.reduce_max(k_m2[:, b, 1:2], PS(key)[:, 1, 0:LASTH], axis=AX.X)
                V_.drain()
                if m >= 2:
                    dve.wait_ge(k_expd, m - 1)
                V_.tensor_scalar(k_nm[:, b:b + 1], k_m2[:, b, 0:1], k_m2[:, b, 1:2], -1.0,
                                 ALU.max, ALU.mult).then_inc(k_max, 1)
                if m % HK == 0:
                    split_lo(J_K + m // HK + 1)
            dve.wait_ge(k_expd, KF)
            dve.wait_ge(pads_set, 1)
            V_.tensor_tensor(k_rs[:, :], k_sum[:, :, 0], k_sum[:, :, 1], ALU.add)
            V_.drain()
            V_.reciprocal(k_rs[:, :], k_rs[:, :])
            V_.drain()
            for c in range(2):
                wait_unit(("ctx", c))
                for p in range(HK):
                    m = c * HK + p
                    for a in range(0, 128, DH):
                        V_.tensor_scalar(ctx_s[a:a + DH, m, a:a + DH],
                                         PS(("ctx", c))[a:a + DH, 0, p * 128 + a:p * 128 + a + DH],
                                         k_rs[a:a + DH, m:m + 1], None, ALU.mult)
                V_.drain().then_inc(free[slot(("ctx", c))], 1)
                V_.drain().then_inc(ctx_done, 1)

            def attention_lo(n):
                lo_of(("at", n), halved(at_lo, n), moving(("at", n)), halved(at_hi, n))

            heads = lambda ap: ap.rearrange("p (h d) -> p h d", d=DH)
            wide = lambda ap: ap.unsqueeze(2).to_broadcast([T, HH, DH])
            for m in range(2 * NT + QLAG):
                if m < 2 * NT:
                    key, b = ("q", m), m % 2
                    wait_unit(key)
                    V_.reduce_max(q_m[:, :], heads(PS(key)[0:T, 0, :]), axis=AX.X)
                    V_.drain()
                    if m >= 2:
                        dve.wait_ge(ready[slot(("qt", m - 2))], use(("qt", m - 2)) + 1)
                    V_.tensor_tensor(heads(q_s[:, b, :]), heads(PS(key)[0:T, 0, :]), wide(q_m[:, :]),
                                     ALU.subtract).then_inc(q_sub, 1)
                    V_.drain().then_inc(free[slot(key)], 1)
                    dve.wait_ge(q_expd, m + 1)
                    V_.reduce_sum(q_sum[:, :], heads(q_s[:, b, :]), axis=AX.X)
                    V_.drain()
                    V_.reciprocal(q_sum[:, :], q_sum[:, :])
                    V_.drain()
                    V_.scalar_tensor_tensor(heads(q_s[:, b, :]), heads(q_s[:, b, :]), float(DH) ** -0.5,
                                            wide(q_sum[:, :]), ALU.mult, ALU.mult).then_inc(q_done, 1)
                    if m in Q_SPLITS:
                        split_lo(Q_SPLITS[m][0], quarters=Q_SPLITS[m][1:])
                if m == 2 * NT - 1:
                    for n in range(HK):
                        attention_lo(n)
            for n in range(HK, KF):
                attention_lo(n)
            dve.wait_ge(bias_loaded, 32)
            V_.tensor_tensor(bias_o[:, 0, :], bias_o[:, 0, :], bias_o[:, 1, :], ALU.add)
            V_.drain()
            for h in range(2):
                split_lo(J_O + h + 1)
                for i in range(NT):
                    key, n = ("o", h, i), h * NT + i
                    wait_unit(key)
                    if n >= 2:
                        dve.wait_ge(o_stored[n % 2], 16 * (n // 2))
                    V_.tensor_tensor(o_s[:, n % 2, :], PS(key)[0:T, 0, :], bias_o[:, 0, h * HW:(h + 1) * HW],
                                     ALU.add).then_inc(o_copied, 1)
                    V_.drain().then_inc(free[slot(key)], 1)
            dve.wait_ge(b0_loaded, 16)
            for h in range(2):
                split_lo(J_L0 + 2 * h + 1)
                for i in range(NT):
                    key = ("g0", h, i)
                    lo_of(key, g_lo[:, i, :], PS(key)[0:T, 0, :], g_hi[:, i, :])
                split_lo(J_L0 + 2 * h + 2)
                for n in range(h * HK, (h + 1) * HK):
                    key = ("h", n)
                    wait_unit(key)
                    V_.tensor_scalar(moving(key), moving(key), b0_s[:, n:n + 1], 0.0, ALU.add,
                                     ALU.max).then_inc(h_relu, 1)
                    lo_of(key, halved(t2_lo, n), moving(key), halved(t2_hi, n))
            def normal_lo_2(i):
                for f in range(2):
                    at_ = (slice(None), slice(f * HK, (f + 1) * HK), tile(i))
                    dve.wait_ge(hi_out, nth[("x2t", i, f)])
                    V_.tensor_tensor(t2_lo[at_], PS(("x2t", i))[:, f, 0:HK * T].rearrange("p (k t) -> p k t", t=T),
                                     as32(t2_hi[at_]), ALU.subtract).then_inc(lo_out, 1)
                V_.drain().then_inc(free[slot(("x2t", i))], 1)

            for h in range(2):
                split_lo(J_L1 + 2 * h + 1)
                for i in range(NT):
                    key = ("g1", h, i)
                    lo_of(key, g_lo[:, i, :], PS(key)[0:T, 0, :], g_hi[:, i, :])
                split_lo(J_L1 + 2 * h + 2)
                dve.wait_ge(x1_loaded, 32)
                cols_h = slice(h * HW, (h + 1) * HW)
                for i in range(NT):
                    key = ("x1", h, i)
                    wait_unit(key)
                    V_.tensor_tensor(x1[:, i, cols_h], x1[:, i, cols_h], PS(key)[0:T, 0, :], ALU.add)
                    V_.drain().then_inc(free[slot(key)], 1)
                    V_.tensor_tensor(x1[:, i, cols_h], x1[:, i, cols_h], part[:, i, cols_h], ALU.add)
                    if h == 1:
                        if i == 0:
                            dve.wait_ge(rwh_done, 1)
                            V_.tensor_tensor(rw_lo[:, :, :], rw_raw[:, :, :], as32(rw_hi[:, :, :]),
                                             ALU.subtract).then_inc(rwl_done, 1)
                        V_.drain()
                        moments(x1[:, i, :])
                        norm_scale(NT + i + 1)
                        if i:
                            normal_lo_2(i - 1)
            normal_lo_2(NT - 1)

            ex = lambda ap: ap.unsqueeze(2).to_broadcast([T, NT, X])
            ti = lambda ap: ap.unsqueeze(1).to_broadcast([T, NT, X])
            dve.wait_ge(route_set, 1)
            wait_unit(("lt",))
            V_.tensor_copy(lg[:, :, :], PS(("lt",))[0:T, 0, 0:NT * XP].rearrange("p (i e) -> p i e", e=XP))
            V_.drain().then_inc(free[slot(("lt",))], 1)
            V_.reduce_max(r1[:, :], lg[:, :, 0:X], axis=AX.X)
            V_.drain()
            V_.tensor_tensor(pr[:, :, :], lg[:, :, 0:X], ex(r1[:, :]), ALU.subtract).then_inc(lg_sub, 1)
            dve.wait_ge(lg_expd, 2)
            V_.reduce_sum(r1[:, :], pr[:, :, :], axis=AX.X)
            V_.tensor_scalar(wts[:, 2, :], wts[:, 2, :], 1.0, None, ALU.add)
            V_.drain()
            V_.reciprocal(r1[:, :], r1[:, :])
            V_.reciprocal(wts[:, 2, :], wts[:, 2, :])
            V_.drain()
            V_.tensor_tensor(pr[:, :, :], pr[:, :, :], ex(r1[:, :]), ALU.mult)
            V_.drain()
            for c, mask in enumerate((m1, m2)):
                V_.reduce_max(wts[:, c, :], pr[:, :, :], axis=AX.X)
                V_.drain()
                V_.tensor_tensor(eq[:, :, :], pr[:, :, :], ex(wts[:, c, :]), ALU.is_equal)
                V_.drain()
                V_.tensor_tensor(eq[:, :, :], eq[:, :, :], ti(iota_m8[:, :]), ALU.mult)
                V_.drain()
                V_.tensor_reduce(r1[:, :], eq[:, :, :], axis=AX.X, op=ALU.min)
                V_.drain()
                V_.tensor_tensor(mask[:, :, :], ti(iota_m8[:, :]), ex(r1[:, :]), ALU.is_equal)
                V_.drain()
                if c == 0:
                    V_.scalar_tensor_tensor(pr[:, :, :], m1[:, :, :], -2.0, pr[:, :, :], ALU.mult, ALU.add)
                    V_.drain()
            V_.tensor_tensor(mm[:, :, :], m1[:, :, :], m2[:, :, :], ALU.add).then_inc(m_ready, 1)

            def shared_lo(h):
                for n in range(h * HK, (h + 1) * HK):
                    key = ("up", n)
                    wait_unit(key)
                    dve.wait_ge(gate_done, n + 1)
                    V_.tensor_tensor(moving(key), moving(key), gate_s[:, n % HK, :].rearrange("p (c n) -> p c n", c=2),
                                     ALU.mult).then_inc(prod_done, 1)
                    lo_of(key, halved(s_lo, n), moving(key), halved(s_hi, n))

            split_lo(J_GU + 1)
            wait_unit(("pos",))
            pos = PS(("pos",))[0:T, 0, 0:NT * X].rearrange("p (i e) -> p i e", e=X)
            cnt = PS(("pos",))[0:T, 1, 0:X]
            V_.tensor_scalar(nb[:, :], cnt, 0.0, None, ALU.is_gt)
            V_.drain()
            for c in range(B, N, B):
                V_.scalar_tensor_tensor(nb[:, :], cnt, float(c), nb[:, :], ALU.is_gt, ALU.add)
                V_.drain()
            V_.tensor_copy(cum[:, 0, :], nb[:, :])
            V_.drain()
            for c, step in enumerate((1, 2, 4)):
                V_.tensor_copy(cum[:, (c + 1) % 2, 0:step], cum[:, c % 2, 0:step])
                V_.tensor_tensor(cum[:, (c + 1) % 2, step:X], cum[:, c % 2, step:X], cum[:, c % 2, 0:X - step], ALU.add)
                V_.drain()
            V_.tensor_tensor(start[:, :], cum[:, 1, :], nb[:, :], ALU.subtract)
            V_.drain()
            V_.tensor_scalar(start[:, :], start[:, :], float(B), None, ALU.mult)
            V_.drain()
            V_.tensor_tensor(pr[:, :, :], pos, ti(start[:, :]), ALU.add)
            V_.drain().then_inc(free[slot(("pos",))], 1)
            for c, mask in enumerate((m1, m2)):
                V_.tensor_tensor(eq[:, :, :], pr[:, :, :], mask[:, :, :], ALU.mult)
                V_.drain()
                V_.reduce_sum(r1[:, :], eq[:, :, :], axis=AX.X)
                V_.drain()
                V_.tensor_copy(slots[:, c, :], r1[:, :])
                V_.drain()
            V_.drain().then_inc(slots_ready, 1)
            be = [T, MAXB, X]
            V_.tensor_tensor(ind[:, :, :], cum[:, 1, :].unsqueeze(1).to_broadcast(be),
                             iota_j[:, :].unsqueeze(2).to_broadcast(be), ALU.is_le)
            V_.drain()
            V_.reduce_sum(je[:, :], ind[:, :, :], axis=AX.X)
            V_.drain()
            V_.tensor_scalar(table[0:1, 0, :], je[0:1, :], float(X - 1), None, ALU.min)
            V_.tensor_copy(table[0:1, 1, 0:1], cum[0:1, 1, X - 1:X])
            V_.drain().then_inc(table_ready, 1)
            for h in range(2):
                if h:
                    split_lo(J_GU + 2 * h + 1)
                split_lo(J_GU + 2 * h + 2)
                shared_lo(h)
            for s in range(BC):
                for f in range(2):
                    transposed_lo(("xe", s, f), xe_lo, xe_hi, s, f, 128)
            def shared_out(h, i, base=None):
                key = ("sd", h, i)
                wait_unit(key, base)
                part_h = x1[:, i, h * HW:(h + 1) * HW]
                V_.scalar_tensor_tensor(part_h, PS(key)[0:T, 0, :], wts[:, 2, i:i + 1], part_h, ALU.mult, ALU.add)
                V_.drain().then_inc(free[slot(key)], 1)

            split_lo(J_X)
            for i in range(NT):
                shared_out(0, i)
            blocks = dve.value_load(table[0:1, 1, 0:1], min_val=1, max_val=MAXB - 1)
            with dve.Fori(0, blocks) as j:
                for h in range(2):
                    split_lo(J_X + h + 1, j)
                    for n in range(h * HK // 2, (h + 1) * HK // 2):
                        key = ("he", n)
                        two = lambda t: t[:, 2 * n:2 * n + 2, :].rearrange("p k n -> p (k n)")
                        lo_of(key, two(he_lo), PS(key)[:, 0, :], two(he_hi), j)
                for s, f in FIRST:
                    transposed_lo(("xe+", s, f), xe_lo, xe_hi, s, f, 128, j)
                split_lo(J_X + 3, j)
                for s, f in LATER:
                    transposed_lo(("xe+", s, f), xe_lo, xe_hi, s, f, 128, j)
                split_lo(J_X + 4, j)
            for i in range(NT):
                for c in range(2):
                    dve.wait_ge(yg_loaded[i][c], 16)
                    V_.scalar_tensor_tensor(x1[:, i, :], y_g[c][:, i, :], wts[:, c, i:i + 1], x1[:, i, :],
                                            ALU.mult, ALU.add)
                    V_.drain()
                V_.drain().then_inc(out_ready, 1)
                shared_out(1, i, blocks)
                V_.drain().then_inc(out_ready, 1)

        @block.tensor
        def _(pe):
            mat = nc.tensor.matmul

            def claim(key, base=None):
                if base is not None:
                    pe.wait_ge(free[slot(key)], base * BU + use(key))
                elif use(key) > 0:
                    pe.wait_ge(free[slot(key)], use(key))

            def passes(out_ap, left, right, start, stop):
                (lh, ll), (rh, rl) = left, right
                mat(out_ap, lh, rh, start=start, stop=False)
                mat(out_ap, lh, rl, start=False, stop=False)
                return mat(out_ap, ll, rh, start=False, stop=stop)

            def weights(job, base=None):
                pe.wait_ge(lo_done, 2 * (job + 1) if base is None else base * 8 + 2 * (job + 1))
                return w_hi[job % 2], w_lo[job % 2]

            def by_tokens(key, out_ap, operand, job, tokens, start=True, stop=True, arrives=None):
                wh, wl = w_hi[job % 2], w_lo[job % 2]
                for k in range(KF):
                    if arrives and arrives(k) is not None:
                        pe.wait_ge(lo_out, arrives(k))
                    last = passes(out_ap, [t[:, k, tokens] for t in operand], (wh[:, k, :], wl[:, k, :]),
                                  start and k == 0, stop and k == KF - 1)
                return last

            def by_features(key, n, operand, job, stop=True, banks=(0, 1)):
                wh, wl = w_hi[job % 2], w_lo[job % 2]
                for c in banks:
                    for k in range(KF):
                        w_cols = slice(n % HK * 128, (n % HK + 1) * 128)
                        last = passes(PS(key)[:, c, 0:TH], (wh[:, k, w_cols], wl[:, k, w_cols]),
                                      [t[:, k, c * TH:(c + 1) * TH] for t in operand], k == 0, stop and k == KF - 1)
                return last

            XT, T2, AT, SH, HE = (xt_hi, xt_lo), (t2_hi, t2_lo), (at_hi, at_lo), (s_hi, s_lo), (he_hi, he_lo)

            pe.wait_ge(iotas_set, 1)
            acc = [ps[n // 2][0:T, n % 2, 0:TH] for n in range(NT)]

            def transposes(key, source, count, width, ins, base=None):
                claim(key, base)
                for a in range(count):
                    last = nc.tensor.transpose(PB(key)[:, a * width:(a + 1) * width], source(a), ident[0:ins, 0:ins])
                last.then_inc(ready[slot(key)], 1)

            def values(h, i):
                key = ("v", h, i)
                weights(J_V + h)
                pe.wait_ge(lo_out, nth[("xt", i, 1)])
                claim(key)
                by_tokens(key, PB(key)[0:T, :], XT, J_V + h, tile(i)).then_inc(ready[slot(key)], 1)

            def count(g, lo, hi):
                with pe.Fori(lo, hi) as c:
                    for b in range(OHB):
                        pe.wait_ge(oh_ready, c * OHB + (g * GB + b + 1))
                        pe.wait_ge(oha_ready, c * OHB + (g * GB + b + 1))
                        for e in range(b * CB, (b + 1) * CB):
                            for n in range(NT):
                                last = mat(acc[n], src_oh[:, e, n * T:(n + 1) * T], dst_oh[:, e, :], start=False, stop=False)
                        last.then_inc(oh_free, 1)

            for g in range(NG):
                pe.wait_ge(cnt_free, g + 1)
                for n in range(NT):
                    mat(acc[n], zero16[:, 0:T], zero16[:, :], start=True, stop=False)
                count(g, 0, GB // 2 // OHB)
                if g:
                    values(0, g - 1)
                count(g, GB // 2 // OHB, GB // OHB)
                for n in range(NT):
                    last = mat(acc[n], zero16[:, 0:T], zero16[:, :], start=False, stop=True)
                last.then_inc(cnt_ready, 1)
                if g == 0:
                    pe.wait_ge(consts_set, 1)
                pe.wait_ge(ln_done, g + 1)
                for f in range(2):
                    transposes(("xt", g, f), lambda a: x_s[:, g, (f * HK + a) * 128:(f * HK + a + 1) * 128], HK, T, T)
                if g:
                    values(1, g - 1)
            values(0, NT - 1)
            pe.wait_ge(cnt_free, NG + 1)
            pe.wait_ge(c_ready, 1)
            key = ("deg",)
            for c in range(2):
                for n in range(NT):
                    last = mat(PS(key)[0:T, c, 0:TH], ones[0:T, 0:T], c_f[:, n, c, :], start=n == 0, stop=n == NT - 1)
            last.then_inc(ready[slot(key)], 1)
            values(1, NT - 1)
            for n in range(SIDE):
                pe.wait_ge(free[RING + n], len(side[n::SIDE]))
            def context(c):
                pe.wait_ge(kt_done, 2 * (c + 1) * HK)
                if c == 0:
                    pe.wait_ge(v_loaded, 16)
                key = ("ctx", c)
                claim(key)
                for p in range(HK):
                    m = c * HK + p
                    for i in range(NT):
                        last = mat(PS(key)[:, 0, p * 128:(p + 1) * 128], k_tok[:, i, m * 128:(m + 1) * 128],
                                   v_tok[:, i, m * 128:(m + 1) * 128], start=i == 0, stop=i == NT - 1)
                last.then_inc(ready[slot(key)], 1)

            def keys_back(m):
                key = ("kt", m)
                pe.wait_ge(k_expd, m + 1)
                claim(key)
                for i in range(NT):
                    last = nc.tensor.transpose(PS(key)[0:T, i // 4, i % 4 * 128:(i % 4 + 1) * 128],
                                               k_exp[:, m % 2, tile(i)], ident[:, :])
                last.then_inc(ready[slot(key)], 1)

            for m in range(KF + KLAG):
                if m < KF:
                    if m % HK == 0:
                        weights(J_K + m // HK)
                    key = ("k", m)
                    claim(key)
                    by_features(key, m, XT, J_K + m // HK).then_inc(ready[slot(key)], 1)
                if m == KF + KLAG - 1:
                    context(0)
                if m >= KLAG:
                    keys_back(m - KLAG)
            context(1)

            def attend(n):
                key = ("at", n)
                pe.wait_ge(ctx_done, 2)
                pe.wait_ge(qt_done, NT if n < HK else 2 * NT)
                claim(key)
                for c in range(2):
                    last = mat(PS(key)[:, c, 0:TH], ctx_s[:, n, :], q_t[n // HK][:, n % HK, c * TH:(c + 1) * TH], start=True, stop=True)
                last.then_inc(ready[slot(key)], 1)

            for m in range(2 * NT + QLAG):
                if m < 2 * NT:
                    if m % NT == 0:
                        weights(J_Q + m // NT)
                    key = ("q", m)
                    claim(key)
                    by_tokens(key, PS(key)[0:T, 0, :], XT, J_Q + m // NT, tile(m % NT)).then_inc(ready[slot(key)], 1)
                if m >= QLAG:
                    n = m - QLAG
                    pe.wait_ge(q_done, n + 1)
                    transposes(("qt", n), lambda a: q_s[:, n % 2, a * 128:(a + 1) * 128], HK, T, T)
                if m == 2 * NT - 1:
                    for n in range(HK):
                        attend(n)
            for n in range(HK, KF):
                attend(n)
            for h in range(2):
                weights(J_O + h)
                for i in range(NT):
                    key = ("o", h, i)
                    claim(key)
                    by_tokens(key, PS(key)[0:T, 0, :], AT, J_O + h, tile(i),
                              arrives=(lambda k: nth[("at", k)]) if h == i == 0 else None).then_inc(ready[slot(key)], 1)
            pe.wait_ge(cl_done, NT)
            for h in range(2):
                job = J_L0 + 2 * h
                weights(job)
                for i in range(NT):
                    key = ("g0", h, i)
                    claim(key)
                    by_tokens(key, PS(key)[0:T, 0, :], XT, job, tile(i)).then_inc(ready[slot(key)], 1)
                weights(job + 1)
                for n in range(h * HK, (h + 1) * HK):
                    key = ("h", n)
                    claim(key)
                    by_features(key, n, XT, job + 1, stop=False)
                    pe.wait_ge(lo_out, nth[("g0", h, NT - 1)])
                    g_cols = slice(n % HK * 128, (n % HK + 1) * 128)
                    for c in range(2):
                        for i in range(NT):
                            last = passes(PS(key)[:, c, 0:TH], (g_hi[:, i, g_cols], g_lo[:, i, g_cols]),
                                          [t[:, i, c * TH:(c + 1) * TH] for t in (c_hi, c_lo)], False, i == NT - 1)
                    last.then_inc(ready[slot(key)], 1)
            def normal_across(i):
                key = ("x2t", i)
                pe.wait_ge(ln_done, NT + i + 1)
                claim(key)
                for k in range(KF):
                    last = nc.tensor.transpose(PS(key)[:, k // HK, k % HK * T:(k % HK + 1) * T],
                                               part[:, i, k * 128:(k + 1) * 128], ident[0:T, 0:T])
                last.then_inc(ready[slot(key)], 1)

            for h in range(2):
                job = J_L1 + 2 * h
                weights(job)
                for i in range(NT):
                    key = ("g1", h, i)
                    claim(key)
                    by_tokens(key, PS(key)[0:T, 0, :], T2, job, tile(i),
                              arrives=(lambda k: nth[("h", k)]) if h == i == 0 else None).then_inc(ready[slot(key)], 1)
                weights(job + 1)
                for i in range(NT):
                    key = ("x1", h, i)
                    claim(key)
                    by_tokens(key, PS(key)[0:T, 0, :], T2, job + 1, tile(i), stop=False)
                    pe.wait_ge(lo_out, nth[("g1", h, NT - 1)])
                    for s in range(NT):
                        last = passes(PS(key)[0:T, 0, :], [t[:, s, tile(i)] for t in (c_hi, c_lo)],
                                      (g_hi[:, s, :], g_lo[:, s, :]), False, s == NT - 1)
                    last.then_inc(ready[slot(key)], 1)
                    if h and i:
                        normal_across(i - 1)
            assert TH <= (NT - 2) * T
            weights(J_GU)

            def gates(n, c):
                if c == 0:
                    claim(("gt", n))
                last = by_features(("gt", n), n, T2, J_GU, banks=(c,))
                if c == 1:
                    last.then_inc(ready[slot(("gt", n))], 1)

            def logits(c):
                for k in range(KF):
                    last = passes(PS(("lg",))[0:XP, c, 0:TH], (rw_hi[:, k, :], rw_lo[:, k, :]),
                                  [t[:, k, c * TH:(c + 1) * TH] for t in T2], k == 0, k == KF - 1)
                return last

            pe.wait_ge(lo_out, nth[("x2t", NT - 3, 1)])
            gates(0, 0)
            pe.wait_ge(rwl_done, 1)
            claim(("lg",))
            logits(0)
            normal_across(NT - 1)
            gates(1, 0)
            pe.wait_ge(t2_padded, 1)
            pe.wait_ge(lo_out, nth[("x2t", NT - 1, 1)])
            logits(1).then_inc(ready[slot(("lg",))], 1)
            gates(0, 1)
            gates(1, 1)
            key = ("lt",)
            pe.wait_ge(lgT_done, 1)
            claim(key)
            for i in range(NT):
                last = nc.tensor.transpose(PS(key)[0:T, 0, i * XP:(i + 1) * XP], lgT[:, tile(i)], ident[0:XP, 0:XP])
            last.then_inc(ready[slot(key)], 1)
            for h in range(2):
                for a, name in enumerate(("gt", "up")):
                    job = J_GU + 2 * h + a
                    weights(job)
                    for n in range(GEARLY if job == J_GU else h * HK, (h + 1) * HK):
                        key = (name, n)
                        claim(key)
                        by_features(key, n, T2, job).then_inc(ready[slot(key)], 1)
                    if h == 0 and a == 0:
                        key = ("pos",)
                        pe.wait_ge(m_ready, 1)
                        claim(key)
                        for i in range(NT):
                            out_ap = PS(key)[0:T, 0, i * X:(i + 1) * X]
                            for b in range(i):
                                mat(out_ap, ones16[:, 0:T], mm[:, b, :], start=b == 0, stop=False)
                            mat(out_ap, tri[:, 0:T], mm[:, i, :], start=i == 0, stop=True)
                        for i in range(NT):
                            last = mat(PS(key)[0:T, 1, 0:X], ones16[:, 0:T], mm[:, i, :], start=i == 0, stop=i == NT - 1)
                        last.then_inc(ready[slot(key)], 1)
            pe.wait_ge(xg_loaded, 16 * BC)
            for s in range(BC):
                for f in range(2):
                    transposes(("xe", s, f), lambda a: xg[:, s, (f * HK + a) * 128:(f * HK + a + 1) * 128], HK, 128, 128)
            pe.wait_ge(lo_out, nth[("up", KF - 1)])

            def shared_out(h, job, base=None):
                weights(job, base)
                for i in range(NT):
                    key = ("sd", h, i)
                    claim(key, base)
                    by_tokens(key, PS(key)[0:T, 0, :], SH, job, tile(i)).then_inc(ready[slot(key)], 1)

            shared_out(0, J_D)
            pe.wait_ge(table_ready, 1)
            blocks = pe.value_load(table[0:1, 1, 0:1], min_val=1, max_val=MAXB - 1)
            with pe.Fori(0, blocks) as j:
                pe.wait_ge(lo_out, j * BR + R0)
                for h in range(2):
                    wh, wl = weights(J_X + h, j)
                    for n in range(h * HK // 2, (h + 1) * HK // 2):
                        key = ("he", n)
                        claim(key, j)
                        for a in range(2):
                            w_cols = slice((2 * n + a) % HK * 128, ((2 * n + a) % HK + 1) * 128)
                            for k in range(KF):
                                last = passes(PS(key)[:, 0, a * B:(a + 1) * B], (wh[:, k, w_cols], wl[:, k, w_cols]),
                                              (xe_hi[:, k, :], xe_lo[:, k, :]), k == 0, k == KF - 1)
                        last.then_inc(ready[slot(key)], 1)
                pe.wait_ge(xg_loaded, j * (16 * BC) + 2 * 16 * BC)

                def rows_across(s, f):
                    transposes(("xe+", s, f), lambda a: xg[:, s, (f * HK + a) * 128:(f * HK + a + 1) * 128],
                               HK, 128, 128, j)

                for s, f in FIRST:
                    rows_across(s, f)
                for h in range(2):
                    weights(J_X + 2 + h, j)
                    for s in range(BC):
                        key = ("y", h, s)
                        claim(key, j)
                        by_tokens(key, PS(key)[:, 0, :], HE, J_X + h, slice(s * 128, (s + 1) * 128),
                                  arrives=(lambda k: j * BR + nth[("he", k // 2)] if k % 2 == 0 and k >= KF // 2 else None)
                                  if h == s == 0 else None).then_inc(ready[slot(key)], 1)
                        if h == s == 0:
                            for rows in LATER:
                                rows_across(*rows)
            shared_out(1, J_X, blocks)


_INS = ['x', 'src', 'dst', 'L0_gnn_W_self0', 'L0_gnn_W_neigh0', 'L0_gnn_b0', 'L0_gnn_W_self1', 'L0_gnn_W_neigh1',
        'L0_gnn_b1', 'L0_mix_Wq', 'L0_mix_Wk', 'L0_mix_Wv', 'L0_mix_Wo', 'L0_mix_bo', 'L0_ffn_router_w', 'L0_ffn_w1',
        'L0_ffn_w2', 'L0_ffn_shared_gate_up', 'L0_ffn_shared_down', 'L0_ffn_shared_gate_w']


def kernel(**inputs):
    import numpy as _np
    import concourse.bacc as _bacc
    from concourse import mybir as _mybir
    from concourse.bass_utils import run_bass_kernel_spmd as _run

    nc = _bacc.Bacc("TRN2", target_bir_lowering=False, num_devices=1)
    arrays, args = {}, []
    for name in _INS:
        a = _np.ascontiguousarray(inputs[name])
        arrays[f"in_{name}"] = a
        args.append(nc.dram_tensor(f"in_{name}", a.shape, _mybir.dt.from_np(a.dtype), kind="ExternalInput").ap())
    shape = arrays["in_x"].shape
    args.append(nc.dram_tensor("out_0", shape, _mybir.dt.float32, kind="ExternalOutput").ap())
    gps_layer(nc, *args)
    r = _run(nc, [arrays], core_ids=[0])
    return r.results[0]["out_0"]
```
